# Optimizing a Trainium2 kernel written in Bass

```python
import numpy as np
import jax
import jax.numpy as jnp

def _softmax(x, axis=-1):
    return jax.nn.softmax(x, axis=axis)

def _gelu(x):
    return jax.nn.gelu(x, approximate=True)

def _silu(x):
    return jax.nn.silu(x)

def _sigmoid(x):
    return jax.nn.sigmoid(x)

def _layernorm(x, axis=-1, eps=1e-05):
    m = jnp.mean(x, axis=axis, keepdims=True)
    v = jnp.var(x, axis=axis, keepdims=True)
    return (x - m) / jnp.sqrt(v + eps)

def _scatter_add(tgt, idx, src, axis=0):
    return tgt.at[idx].add(src)

def _segment_sum(src, seg, n):
    return jax.ops.segment_sum(src, seg, n)
kernel_name = 'mk_decoder_postln_d1_seqx_r4_308716'

def setup_inputs(seed: int=0):
    np.random.seed(seed)
    _w = jnp.asarray

    def _rec_inputs():
        import jax
        import jax.numpy as jnp
        _rk = jax.random.key(seed)
        x = -0.0003929 + 0.9999 * jax.random.normal(jax.random.fold_in(_rk, 1), (32, 100, 256), jnp.float32)
        _lenS = 100 - jax.random.randint(jax.random.fold_in(_rk, 7), (32,), 0, max(1, 100 // 4) + 1, jnp.int32)
        _lenS2 = 361 - jax.random.randint(jax.random.fold_in(_rk, 8), (32,), 0, max(1, 361 // 4) + 1, jnp.int32)
        _ctx_1024P = jax.random.normal(jax.random.fold_in(_rk, 11), (32, 16, 256), jnp.float32)
        _ctx_1024c = jax.random.dirichlet(jax.random.fold_in(_rk, 511), 0.3 * jnp.ones((16,), jnp.float32), (32, 361))
        _ctx_1024t = jnp.einsum('bsk,bkd->bsd', _ctx_1024c, _ctx_1024P)
        _ctx_1024t = _ctx_1024t * jax.lax.rsqrt(jnp.mean(jnp.square(_ctx_1024t)) + 1e-12) * 0.953939
        ctx_1024 = -0.000514642 + 1.00011 * (_ctx_1024t + 0.3 * jax.random.normal(jax.random.fold_in(_rk, 611), (32, 361, 256), jnp.float32))
        _validS = jnp.arange(100)[None, :] < _lenS[:, None]
        _validS2 = jnp.arange(361)[None, :] < _lenS2[:, None]
        _causal = jnp.tril(jnp.ones((100, 100), dtype=bool))
        mask_BxS2_bk0 = jnp.logical_not(jnp.broadcast_to(_validS2[:, :], (32, 361)))
        return (x, ctx_1024, mask_BxS2_bk0)
    x, ctx_1024, mask_BxS2_bk0 = _rec_inputs()

    def _L0_attn_setup():
        import jax, jax.numpy as jnp
        import numpy as np
        B, S, E = (4, 256, 256)
        N, D = (16, 64)
        key = jax.random.key(seed)
        k0, k1, k2, k3, k4 = jax.random.split(key, 5)
        return {'inputs': jax.random.normal(k0, (B, S, E), dtype=jnp.float32), 'WQ': jax.random.normal(k1, (N, E, D), dtype=jnp.float32) * 0.02, 'WK': jax.random.normal(k2, (N, E, D), dtype=jnp.float32) * 0.02, 'WV_down': jax.random.normal(k3, (N, E, D), dtype=jnp.float32) * 0.02, 'WV_up': jax.random.normal(k4, (N, D, E), dtype=jnp.float32) * 0.02}
    _L0_attn_all = _L0_attn_setup()
    _L0_attn_in = {k: v for k, v in _L0_attn_all.items() if k in ('WQ', 'WK', 'WV_down', 'WV_up')}
    del _L0_attn_all

    def _L0_xattn_setup():
        import jax, jax.numpy as jnp
        import numpy as np
        DIM = 256
        HEADS = 16
        HEAD_DIM = DIM // HEADS
        B, N, S = (4, 1024, 128)
        key = jax.random.key(seed)
        ks = jax.random.split(key, 9)
        scale = DIM ** (-0.5)
        return {'x': jax.random.normal(ks[0], (B, N, DIM), dtype=jnp.float32), 'context': jax.random.normal(ks[1], (B, S, DIM), dtype=jnp.float32), 'context_mask': jax.random.uniform(ks[2], (B, S)) < 0.2, 'q_w': jax.random.normal(ks[3], (DIM, DIM), dtype=jnp.float32) * scale, 'q_b': jnp.zeros((DIM,), dtype=jnp.float32), 'kv_w': jax.random.normal(ks[4], (DIM, 2 * DIM), dtype=jnp.float32) * scale, 'kv_b': jnp.zeros((2 * DIM,), dtype=jnp.float32), 'proj_w': jax.random.normal(ks[5], (DIM, DIM), dtype=jnp.float32) * scale, 'proj_b': jnp.zeros((DIM,), dtype=jnp.float32)}
    _L0_xattn_all = _L0_xattn_setup()
    _L0_xattn_in = {k: v for k, v in _L0_xattn_all.items() if k in ('q_w', 'q_b', 'kv_w', 'kv_b', 'proj_w', 'proj_b')}
    del _L0_xattn_all

    def _L0_ffn_setup():
        import jax, jax.numpy as jnp
        import numpy as np
        S, B, H, I, E = (128, 2, 256, 704, 8)
        key = jax.random.key(seed)
        ks = jax.random.split(key, 5)
        return {'hidden_states': jax.random.normal(ks[0], (S, B, H), dtype=jnp.float32), 'router_w': jax.random.normal(ks[1], (E, H), dtype=jnp.float32) * 0.02, 'gate_w': jax.random.normal(ks[2], (E, I, H), dtype=jnp.float32) * 0.02, 'up_w': jax.random.normal(ks[3], (E, I, H), dtype=jnp.float32) * 0.02, 'down_w': jax.random.normal(ks[4], (E, H, I), dtype=jnp.float32) * 0.02}
    _L0_ffn_all = _L0_ffn_setup()
    _L0_ffn_in = {k: v for k, v in _L0_ffn_all.items() if k in ('router_w', 'gate_w', 'up_w', 'down_w')}
    del _L0_ffn_all
    return {'x': x, 'ctx_1024': ctx_1024, 'mask_BxS2_bk0': mask_BxS2_bk0, 'L0_attn_WQ': _L0_attn_in['WQ'], 'L0_attn_WK': _L0_attn_in['WK'], 'L0_attn_WV_down': _L0_attn_in['WV_down'], 'L0_attn_WV_up': _L0_attn_in['WV_up'], 'L0_xattn_q_w': _L0_xattn_in['q_w'], 'L0_xattn_q_b': _L0_xattn_in['q_b'], 'L0_xattn_kv_w': _L0_xattn_in['kv_w'], 'L0_xattn_kv_b': _L0_xattn_in['kv_b'], 'L0_xattn_proj_w': _L0_xattn_in['proj_w'], 'L0_xattn_proj_b': _L0_xattn_in['proj_b'], 'L0_ffn_router_w': _L0_ffn_in['router_w'], 'L0_ffn_gate_w': _L0_ffn_in['gate_w'], 'L0_ffn_up_w': _L0_ffn_in['up_w'], 'L0_ffn_down_w': _L0_ffn_in['down_w']}

def reference(x, ctx_1024, mask_BxS2_bk0, L0_attn_WQ, L0_attn_WK, L0_attn_WV_down, L0_attn_WV_up, L0_xattn_q_w, L0_xattn_q_b, L0_xattn_kv_w, L0_xattn_kv_b, L0_xattn_proj_w, L0_xattn_proj_b, L0_ffn_router_w, L0_ffn_gate_w, L0_ffn_up_w, L0_ffn_down_w):
    import jax
    import jax.numpy as jnp

    def _L0_attn_ref(inputs, WQ, WK, WV_down, WV_up):
        import jax, jax.numpy as jnp
        import numpy as np
        B, S, E = (4, 256, 256)
        N, D = (16, 64)
        d = WQ.shape[-1]
        Q = jnp.einsum('bse,ned->nbsd', inputs, WQ)
        K = jnp.einsum('bse,ned->nbsd', inputs, WK)
        scores = jnp.einsum('nbsd,nbSd->nbsS', K, Q) / jnp.sqrt(jnp.float32(d))
        scores = jnp.triu(scores)
        scores = jnp.where(scores == 0, jnp.finfo(jnp.float32).min, scores)
        attn = jax.nn.softmax(scores, axis=-1)
        inp_down = jnp.einsum('bse,ned->nbsd', inputs, WV_down)
        v_down = jnp.einsum('nbss,nbsd->nbsd', attn, inp_down)
        V = jnp.einsum('nbsd,nde->nbse', v_down, WV_up)
        delta_e = jnp.mean(V, axis=0)
        return inputs + delta_e

    def _L0_xattn_ref(x, context, context_mask, q_w, q_b, kv_w, kv_b, proj_w, proj_b):
        import jax, jax.numpy as jnp
        import numpy as np
        DIM = 256
        HEADS = 16
        HEAD_DIM = DIM // HEADS
        B, N, S = (4, 1024, 128)
        b, n, c = x.shape
        s = context.shape[1]
        h, d = (HEADS, HEAD_DIM)
        scale = d ** (-0.5)
        q = (x @ q_w + q_b).reshape(b, n, h, d)
        kv = (context @ kv_w + kv_b).reshape(b, s, 2, h, d)
        k = kv[:, :, 0]
        v = kv[:, :, 1]
        attn = jnp.einsum('bnhd,bshd->bhns', q, k) * scale
        attn = jnp.where(context_mask[:, None, None, :], -jnp.inf, attn)
        attn = jax.nn.softmax(attn, axis=-1)
        out = jnp.einsum('bhns,bshd->bnhd', attn, v).reshape(b, n, c)
        return out @ proj_w + proj_b

    def _L0_ffn_ref(hidden_states, router_w, gate_w, up_w, down_w):
        import jax, jax.numpy as jnp
        import numpy as np
        S, B, H, I, E = (128, 2, 256, 704, 8)
        router_logits = jnp.einsum('sbh,eh->sbe', hidden_states, router_w)
        routing_indices = jnp.argmax(router_logits, axis=-1)
        out = jnp.zeros_like(hidden_states)
        for e in range(E):
            mask = (routing_indices == e)[..., None]
            xe = jnp.where(mask, hidden_states, 0.0)
            g = jnp.einsum('sbh,ih->sbi', xe, gate_w[e])
            u = jnp.einsum('sbh,ih->sbi', xe, up_w[e])
            ye = jnp.einsum('sbi,hi->sbh', jax.nn.silu(g) * u, down_w[e])
            out = out + jnp.where(mask, ye, 0.0)
        return out
    x = _layernorm(x + _L0_attn_ref(x, L0_attn_WQ, L0_attn_WK, L0_attn_WV_down, L0_attn_WV_up), axis=-1)
    x = _layernorm(x + _L0_xattn_ref(x, ctx_1024, mask_BxS2_bk0, L0_xattn_q_w, L0_xattn_q_b, L0_xattn_kv_w, L0_xattn_kv_b, L0_xattn_proj_w, L0_xattn_proj_b), axis=-1)
    x = _layernorm(x + _L0_ffn_ref(x, L0_ffn_router_w, L0_ffn_gate_w, L0_ffn_up_w, L0_ffn_down_w), axis=-1)
    return x

_drawn_inputs = setup_inputs


def setup_inputs(seed=0):
    import zlib

    import numpy as np

    out = dict(_drawn_inputs(seed))
    spreads = {'L0_xattn_q_b': (0.0, 0.401), 'L0_xattn_kv_b': (0.0, 0.1), 'L0_xattn_proj_b': (0.0, 0.1)}
    factors = {'L0_attn_WQ': 8.0, 'L0_attn_WK': 8.0, 'L0_attn_WV_down': 8.0, 'L0_attn_WV_up': 8.0}
    for name, (base, spread) in spreads.items():
        noise = np.random.default_rng([zlib.crc32(name.encode()), seed]).standard_normal(out[name].shape)
        drawn = base * np.exp(spread * noise) if base else spread * noise
        out[name] = jnp.asarray(drawn.astype(out[name].dtype))
    for name, factor in factors.items():
        out[name] = (out[name] * factor).astype(out[name].dtype)
    return out
```

```python
from contextlib import ExitStack

import concourse.bass as bass
from concourse import mybir

F32 = mybir.dt.float32
U8 = mybir.dt.uint8
U32 = mybir.dt.uint32
I32 = mybir.dt.int32
ALU = mybir.AluOpType
ACT = mybir.ActivationFunctionType
AX_X = mybir.AxisListType.X

B, S, E = 32, 100, 256
KE = E // 128
EPS = 1e-5

N1, D1 = 16, 64
C1 = N1 * D1 // 128
GB = 4
G1 = B // GB
GS = GB * S
BELOW = -3.0e38


N2, D2 = 16, 16
S2 = 361
PARTS = [(0, 5), (5, 5), (10, 6)]
PR = 96
MASK_ROW, MAX_ROW = 96, 97
CTX = [(0, 121), (121, 120), (241, 120)]
TILES = [(p, S * h0 + w * i, w) for p, (h0, n) in enumerate(PARTS)
         for w in [S * n // (4 if n == 5 else 5)] for i in range(S * n // w)]
RUNS = [(0, 0, 500), (1, 500, 500), (2, 1000, 300), (2, 1300, 300)]
MASKED = -1.0e30

X, FF = 8, 704
FC = -(-FF // 128)
QF = FF // 2
SLOTS = 128
NT = (B * S + X * (SLOTS - 1)) // SLOTS
CT = B * S // SLOTS


def wait(eng, sem, value):
    if isinstance(value, int) and value <= 0:
        return
    eng.wait_ge(sem, value)


def self_attention(nc, io, mem):
    wq, wk, wv, wu, xT = mem["wq"], mem["wk"], mem["wv"], mem["wu"], mem["xT"]
    with ExitStack() as ctx:
        sb = lambda name, shape, dt=F32: ctx.enter_context(nc.sbuf_tensor(name, shape, dt))
        sem = lambda name: ctx.enter_context(nc.semaphore(name))
        bank = [ctx.enter_context(nc.psum_tensor(f"a_bank{i}", [128, 512], F32)) for i in range(8)]
        q_ps, k_ps = bank[0], bank[1]
        score_ps = [bank[2], bank[3]]
        share_ps, v_ps = bank[4], bank[5]
        delta_ps = [bank[6], bank[7]]

        ident = sb("a_ident", [128, 128])
        below = sb("a_below", [S, S])
        q_blk = sb("a_q_blk", [128, 2, GB, 2, S])
        kT = sb("a_kT", [128, 2, GS])
        dead = sb("a_dead", [S, 2, GB, S])
        scores = sb("a_scores", [S, 2, 2, GB, S])
        neg_max = sb("a_neg_max", [S, 2, 2, GB])
        probs = sb("a_probs", [S, 2, 2, GB, S])
        total = sb("a_total", [S, 2, 2, GB])
        diag = sb("a_diag", [S, 2, 2, GB, S])
        top = sb("a_top", [S, 2, GB])
        inv = sb("a_inv", [S, 2, GB])
        share = sb("a_share", [S, 2, GB, 2 * D1])
        shareT = sb("a_shareT", [128, 2, GS])
        vT = sb("a_vT", [128, 2, GS])
        x_nat = sb("a_x", [S, GB, E])
        y = sb("a_y", [S, GB, E])
        stats = sb("a_stats", [S, GB, 6])
        pause = sb("a_pause", [1, 1])
        mv = sb("a_mv", [S, GB, 2])
        veps = sb("a_veps", [S, GB])
        rstd = sb("a_rstd", [S, GB])
        half = sb("a_half", [S, GB])

        consts_in, qk_in, vu_in, x_in, x1_out = (sem(n) for n in ("a_consts_in", "a_qk_in", "a_vu_in", "a_x_in", "a_x1_out"))
        half_set = sem("a_half_set")
        q_ready, k_ready, q_evac, k_evac = (sem(n) for n in ("a_q_ready", "a_k_ready", "a_q_evac", "a_k_evac"))
        scores_ready, dead_found, masked, max_ready = (sem(n) for n in ("a_scores_ready", "a_dead_found", "a_masked", "a_max_ready"))
        exp_done, diag_ready, sums_ready, share_ready = (sem(n) for n in ("a_exp_done", "a_diag_ready", "a_sums_ready", "a_share_ready"))
        shareT_ready, shareT_evac, v_ready, v_scaled = (sem(n) for n in ("a_shareT_ready", "a_shareT_evac", "a_v_ready", "a_v_scaled"))
        delta_steps, added, stats_done, var_ready, rstd_ready, x1_ready = (
            sem(n) for n in ("a_delta_steps", "a_added", "a_stats_done", "a_var_ready", "a_rstd_ready", "a_x1_ready"))

        def schedule(stages):
            def positions(g, cs, first=False, last=False):
                for c in cs:
                    for lag, do in stages:
                        if lag <= c:
                            if not last:
                                do(g, c - lag, C1 * g + c - lag)
                        elif lag <= c + C1 and not first:
                            do(g - 1, c - lag + C1, C1 * g + c - lag)
            return positions

        def run(eng, stages):
            positions = schedule(stages)
            positions(0, range(C1), first=True)
            with eng.Fori(1, G1) as g:
                positions(g, range(C1))
            positions(G1, range(C1), last=True)

        block = ctx.enter_context(nc.Block())

        @block.sync
        def _(sp):
            sp.dma_start(xT[:, 0, :], io["xT"][0]).then_inc(qk_in, 16)
            sp.dma_start(wq, io["wq"]).then_inc(qk_in, 16)
            sp.dma_start(xT[:, 1, :], io["xT"][1]).then_inc(qk_in, 16)
            sp.dma_start(wk, io["wk"]).then_inc(qk_in, 16)
            sp.dma_start(below[:, :], io["below"]).then_inc(consts_in, 16)
            sp.dma_start(ident[:, :], io["ident"]).then_inc(consts_in, 16)
            sp.dma_start(wv, io["wv"]).then_inc(vu_in, 16)
            sp.dma_start(wu, io["wu"]).then_inc(vu_in, 16)
            x_of = io["x"].rearrange("(g b) s e -> g s b e", b=GB)
            x1_of = io["x1"].rearrange("(g b s) e -> g s b e", b=GB, s=S)

            def load(g):
                wait(sp, added, GB * g)
                sp.dma_start(x_nat[:, :, :], x_of[g]).then_inc(x_in, 16)

            def store(g):
                sp.wait_ge(x1_ready, g + 1)
                sp.dma_start(x1_of[g], y[:, :, :]).then_inc(x1_out, 16)

            load(0)
            with sp.Fori(1, G1) as g:
                load(g)
                store(g - 1)
            store(G1 - 1)
            sp.wait_ge(x1_out, 16 * G1)

        @block.tensor
        def _(pe):
            def project_qk(g, c, n):
                for w, ps, ready, evac in ((wq, q_ps, q_ready, q_evac), (wk, k_ps, k_ready, k_evac)):
                    wait(pe, evac, n)
                    for k in range(KE):
                        last = pe.matmul(ps[:, 0:GS], w[:, k, 128 * c:128 * c + 128], xT[:, k, bass.ds(g * GS, GS)],
                                         start=(k == 0), stop=(k == KE - 1))
                    last.then_inc(ready, 1)

            def score(g, c, n):
                pe.wait_ge(q_evac, n + 1)
                pe.wait_ge(k_evac, n + 1)
                for i in range(2):
                    wait(pe, masked, 2 * n - 1 + i)
                    for b in (2 * i, 2 * i + 1):
                        last = pe.matmul(score_ps[i][0:S, 2 * S * (b % 2):2 * S * (b % 2) + 2 * S],
                                         kT[:, c % 2, S * b:S * b + S], q_blk[:, c % 2, b].rearrange("p h s -> p (h s)"),
                                         start=True, stop=True)
                    last.then_inc(scores_ready, 1)

            def values(g, c, n):
                pe.wait_ge(share_ready, n + 1)
                wait(pe, shareT_evac, n)
                for b in range(GB):
                    last = pe.transpose(share_ps[:, S * b:S * b + S], share[:, c % 2, b, :], ident[0:S, 0:S])
                last.then_inc(shareT_ready, 1)
                wait(pe, v_scaled, n)
                for k in range(KE):
                    last = pe.matmul(v_ps[:, 0:GS], wv[:, k, 128 * c:128 * c + 128], xT[:, k, bass.ds(g * GS, GS)],
                                     start=(k == 0), stop=(k == KE - 1))
                last.then_inc(v_ready, 1)

            def expand(g, c, n):
                pe.wait_ge(v_scaled, n + 1)
                if c == 0:
                    wait(pe, added, GB * g)
                for b in range(GB):
                    last = pe.matmul(delta_ps[b // 2][0:S, E * (b % 2):E * (b % 2) + E], vT[:, c % 2, S * b:S * b + S],
                                     wu[:, c, :], start=(c == 0 and b % 2 == 0), stop=(c == C1 - 1),
                                     skip_group_check=True)
                last.then_inc(delta_steps, 1)

            pe.wait_ge(qk_in, 64)
            pe.wait_ge(consts_in, 32)
            pe.wait_ge(vu_in, 32)
            run(pe, [(0, project_qk), (1, score), (4, values), (6, expand)])

        @block.scalar
        def _(act):
            def evacuate(g, c, n):
                act.wait_ge(q_ready, n + 1)
                wait(act, scores_ready, 2 * n - 2)
                for h in range(2):
                    rows = slice(64 * h, 64 * h + 64)
                    last = act.activation(q_blk[rows, c % 2, :, h, :], q_ps[rows, 0:GS].rearrange("p (b s) -> p b s", b=GB),
                                          ACT.Copy, scale=D1 ** -0.5)
                last.then_inc(q_evac, 1)
                act.wait_ge(k_ready, n + 1)
                act.activation(kT[:, c % 2, :], k_ps[:, 0:GS], ACT.Copy).then_inc(k_evac, 1)

            def exps(g, c, n):
                wait(act, diag_ready, n - 1)
                wait(act, share_ready, n - 1)
                for i in range(2):
                    act.wait_ge(max_ready, 2 * n + 1 + i)
                    for b in range(GB):
                        last = act.activation(probs[:, c % 2, i, b, :], scores[:, c % 2, i, b, :], ACT.Exp,
                                              bias=neg_max[:, c % 2, i, b:b + 1],
                                              accum_out=total[:, c % 2, i, b:b + 1])
                last.then_inc(exp_done, 1)

            def share_copy(g, c, n):
                act.wait_ge(shareT_ready, n + 1)
                wait(act, v_scaled, n - 1)
                act.activation(shareT[:, c % 2, :], share_ps[:, 0:GS], ACT.Copy, scale=1.0 / N1).then_inc(shareT_evac, 1)

            act.wait_ge(half_set, 2)
            run(act, [(0, evacuate), (2, exps), (4, share_copy)])

        @block.gpsimd
        def _(pool):
            def pick(g, c, n):
                pool.wait_ge(exp_done, n + 1)
                wait(pool, sums_ready, n - 1)
                eye = ident[0:S, 0:S].unsqueeze(1).to_broadcast([S, 2 * GB, S])
                pool.tensor_tensor(diag[:, c % 2].rearrange("s i b t -> s (i b) t"),
                                   probs[:, c % 2].rearrange("s i b t -> s (i b) t"), eye, ALU.mult).then_inc(diag_ready, 1)

            def inverse_root(g, c, n):
                if c == C1 - 1:
                    pool.wait_ge(var_ready, g + 1)
                    pool.tensor_tensor(rstd[:, :], veps[:, :], half[:, :], ALU.pow).then_inc(rstd_ready, 1)

            pool.memset(half[:, :], -0.5).then_inc(half_set, 1)
            pool.wait_ge(half_set, 1)
            pool.memset(q_blk[:, :, :, :, :], 0.0).then_inc(half_set, 1)
            pool.wait_ge(consts_in, 32)
            run(pool, [(2, pick), (7, inverse_root)])

        @block.vector
        def _(dve):
            def mask(g, c, n):
                for i in range(2):
                    dve.wait_ge(scores_ready, 2 * n + 1 + i)
                    sc = score_ps[i][0:S, 0:GS].rearrange("s (b t) -> s b t", b=GB)
                    low = below[:, :].unsqueeze(1).to_broadcast([S, GB, S])
                    dve.scalar_tensor_tensor(out=dead[:, i], in0=sc, scalar=0.0, in1=low,
                                             op0=ALU.is_equal, op1=ALU.max).then_inc(dead_found, 1)
                wait(dve, exp_done, n - 1)
                for i in range(2):
                    dve.wait_ge(dead_found, 2 * n + 1 + i)
                    sc = score_ps[i][0:S, 0:GS].rearrange("s (b t) -> s b t", b=GB)
                    dve.scalar_tensor_tensor(out=scores[:, c % 2, i], in0=dead[:, i], scalar=BELOW, in1=sc,
                                             op0=ALU.mult, op1=ALU.add).then_inc(masked, 1)
                for i in range(2):
                    dve.wait_ge(masked, 2 * n + 1 + i)
                    dve.tensor_reduce(neg_max[:, c % 2, i], scores[:, c % 2, i], AX_X, ALU.max,
                                      negate=True).then_inc(max_ready, 1)

            def shares(g, c, n):
                dve.wait_ge(diag_ready, n + 1)
                wait(dve, share_ready, n)
                dve.tensor_reduce(top[:, :, :], diag[:, c % 2], AX_X, ALU.add).then_inc(sums_ready, 1)
                dve.reciprocal(inv[:, :, :], total[:, c % 2]).then_inc(sums_ready, 1)
                wait(dve, shareT_ready, n - 1)
                dve.wait_ge(sums_ready, 2 * n + 2)
                wide = lambda t: t[:, :, :].rearrange("s i b -> s (i b)").unsqueeze(2).to_broadcast([S, 2 * GB, D1])
                dve.tensor_tensor(share[:, c % 2].rearrange("s b (h d) -> s (b h) d", h=2), wide(top), wide(inv),
                                  ALU.mult).then_inc(share_ready, 1)

            def scale_values(g, c, n):
                dve.wait_ge(shareT_evac, n + 1)
                dve.wait_ge(v_ready, n + 1)
                wait(dve, delta_steps, n - 1)
                dve.tensor_tensor(vT[:, c % 2, :], v_ps[:, 0:GS], shareT[:, c % 2, :], ALU.mult).then_inc(v_scaled, 1)

            def add_up(g, c, n):
                if c < C1 - 1:
                    return
                dve.wait_ge(delta_steps, C1 * g + C1)
                dve.wait_ge(x_in, 16 * g + 16)
                wait(dve, x1_out, 16 * g)
                for b in range(GB):
                    dve.scalar_tensor_tensor(out=y[:, b, :], in0=x_nat[:, b, :], scalar=2.0,
                                             in1=delta_ps[b // 2][0:S, E * (b % 2):E * (b % 2) + E],
                                             op0=ALU.mult, op1=ALU.add).then_inc(added, 1)
                for b in range(GB):
                    dve.wait_ge(added, GB * g + b + 1)
                    dve.bn_stats(stats[:, b, :], y[:, b, :]).then_inc(stats_done, 1)
                dve.wait_ge(stats_done, 2 * GB * g + GB)
                dve.memset(pause[:, :], 0.0)
                for b in range(GB):
                    dve.bn_aggr(mv[:, b, :], stats[:, b, :]).then_inc(stats_done, 1)
                dve.wait_ge(stats_done, 2 * GB * g + 2 * GB)
                dve.tensor_scalar(veps[:, :], mv[:, :, 1], EPS, None, ALU.add).then_inc(var_ready, 1)

            def normalize(g, c, n):
                if c < C1 - 1:
                    return
                dve.wait_ge(rstd_ready, g + 1)
                for b in range(GB):
                    last = dve.tensor_scalar(y[:, b, :], y[:, b, :], mv[:, b, 0:1], rstd[:, b:b + 1],
                                             ALU.subtract, ALU.mult)
                last.then_inc(x1_ready, 1)

            dve.wait_ge(consts_in, 32)
            run(dve, [(5, scale_values), (1, mask), (3, shares), (7, add_up), (8, normalize)])



def cross_attention(nc, io, mem):
    wq, wk, wv, wp, oh = mem["q_w"], mem["k_w"], mem["v_w"], mem["p_w"], mem["choice"]
    with ExitStack() as ctx:
        sb = lambda name, shape, dt=F32: ctx.enter_context(nc.sbuf_tensor(name, shape, dt))
        sem = lambda name: ctx.enter_context(nc.semaphore(name))
        bank = [ctx.enter_context(nc.psum_tensor(f"b_bank{i}", [128, 512], F32)) for i in range(8)]
        front_ps, stream_ps, exp_ps, o_ps, misc_ps = bank[0], bank[1:4], bank[4:6], bank[6], bank[7]

        ident = sb("b_ident", [128, 128])
        q_bias, k_bias = sb("b_q_bias", [PR, 3]), sb("b_k_bias", [PR, 3])
        v_bias = sb("b_v_bias", [CTX[0][1], E])
        block_of = sb("b_block_of", [PR, N2])
        sum_of = sb("b_sum_of", [128, 128])
        rank = sb("b_rank", [S, X])
        router = sb("b_router", [128, KE, X])
        mask_u8 = sb("b_mask_u8", [B, S2], U8)
        mask_f = sb("b_mask_f", [B, S2])
        x1_nat = sb("b_x1_nat", [S, 2, E])
        x1_res = sb("b_x1_res", [S, E])
        c_T = sb("b_c_T", [128, 2, KE, S2])
        x1_T = sb("b_x1_T", [128, KE, S])
        q_T = sb("b_q_T", [PR, 3, S])
        q_blk = sb("b_q_blk", [PR + 2, 2, N2 * S])
        k_T = sb("b_k_T", [PR + 2, 2, 3, S2])
        v = sb("b_v", [CTX[0][1], 2, 3, N2, 32])
        neg_max = sb("b_neg_max", [125, len(TILES)])
        max_T = sb("b_max_T", [8, 2, 125])
        probs = mem["probs"]
        o_raw = sb("b_o_raw", [128, 4 * S])
        inv = sb("b_inv", [128, 4 * S])
        o_T = sb("b_o_T", [128, 4 * S])
        y = sb("b_y", [S, 2, E])
        pause = sb("b_pause", [1, 1])
        stats, mv = sb("b_stats", [S, 6]), sb("b_mv", [S, 2, 2])
        veps, rstd, half = sb("b_veps", [S, 1]), sb("b_rstd", [S, 1]), sb("b_half", [S, 1])
        x2_T = sb("b_x2_T", [128, KE, S])
        best, value, first = sb("b_best", [S, 1]), sb("b_value", [S, X]), sb("b_first", [S, 1])

        zeros = sb("b_zeros", [128, E])

        zeros_out = sem("b_zeros_out")
        consts_in, mask_read, mask_made, mask_out, ones_set = (sem(n) for n in (
            "b_consts_in", "b_mask_read", "b_mask_made", "b_mask_out", "b_ones_set"))
        x1_in, ctx_in, mask_in, max_in = ([sem(f"b_{n}{p}") for p in range(2)] for n in ("x1_in", "ctx_in", "mask_in", "max_in"))
        res_in, x2_out = sem("b_res_in"), [sem(f"b_x2_out{p}") for p in range(2)]
        x1T_ready, x1T_evac, q_ready, q_evac, blk_ready = (sem(n) for n in (
            "b_x1T_ready", "b_x1T_evac", "b_q_ready", "b_q_evac", "b_blk_ready"))
        k_ready, k_evac, v_ready, v_evac, score_ready, max_done = (sem(n) for n in (
            "b_k_ready", "b_k_evac", "b_v_ready", "b_v_evac", "b_score_ready", "b_max_done"))
        maxT_ready, maxT_evac, shifted_ready, exp_done = (sem(n) for n in (
            "b_maxT_ready", "b_maxT_evac", "b_shifted_ready", "b_exp_done"))
        o_ready, o_evac, sums_ready, inv_ready, o_normed, y_ready = (sem(n) for n in (
            "b_o_ready", "b_o_evac", "b_sums_ready", "b_inv_ready", "b_o_normed", "b_y_ready"))
        added, stats_done, var_ready, rstd_ready, x2_ready = (sem(n) for n in (
            "b_added", "b_stats_done", "b_var_ready", "b_rstd_ready", "b_x2_ready"))
        x2T_ready, x2T_evac, logits_ready, picked = (sem(n) for n in (
            "b_x2T_ready", "b_x2T_evac", "b_logits_ready", "b_picked"))

        def run(eng, position):
            for b in range(2):
                position(b, b % 2)
            with eng.Fori(1, B // 2 - 1) as pair:
                for p in range(2):
                    position(2 * pair + p, p)
            for b in range(B - 2, B + 2):
                position(b, b % 2)

        def live(b):
            return not isinstance(b, int) or 0 <= b < B

        def slot(b, p):
            return b - p + 2

        block = ctx.enter_context(nc.Block())

        @block.sync
        def _(sp):
            for dst, src in ((ident[:, :], io["ident"]), (q_bias[:, :], io["q_b"]), (k_bias[:, :], io["k_b"]),
                             (v_bias[:, :], io["v_b"].partition_broadcast(CTX[0][1])), (block_of[:, :], io["block_of"]),
                             (sum_of[:, :], io["sum_of"]), (rank[:, :], io["rank"]), (router[:, :, :], io["router"]),
                             (wq, io["q_w"]), (wk, io["k_w"]), (wv, io["v_w"]), (wp, io["p_w"])):
                sp.dma_start(dst, src).then_inc(consts_in, 16)
            sp.dma_start(mask_u8[:, :], io["mask"]).then_inc(mask_read, 16)
            sp.wait_ge(mask_made, 1)
            sp.dma_start(io["mask_f"], mask_f[:, :]).then_inc(mask_out, 16)
            sp.wait_ge(mask_out, 16)
            sp.wait_ge(ones_set, 6)

            def load(b, p):
                if not live(b):
                    return
                wait(sp, x1T_ready, b - 1)
                sp.dma_start(x1_nat[:, p, :], io["x1"][bass.ds(b * S, S), :]).then_inc(x1_in[p], 16)
                wait(sp, v_ready, 3 * (b - 1))
                sp.dma_start(c_T[:, p], io["ctxT"][bass.ds(b, 1)].rearrange("a p k s -> (a p) k s")).then_inc(ctx_in[p], 16)
                wait(sp, shifted_ready, 12 * (b - 1))
                for part in range(3):
                    sp.dma_start(k_T[MASK_ROW:MASK_ROW + 1, p, part, :], io["mask_f"][bass.ds(b, 1), :]).then_inc(mask_in[p], 16)

            def fetch(b):
                sp.dma_start(mem["gate_up"][:, bass.ds(b * FF, 2 * FF)], io["gate_up"][bass.ds(b * 64, 128), :])\
                  .then_inc(mem["gate_up_in"], 16)

            def position(b, p):
                if live(b) and p == 0:
                    fetch(b)
                if live(b - 1):
                    wait(sp, added, b - 1)
                    sp.dma_start(x1_res[:, :], io["x1"][bass.ds((b - 1) * S, S), :]).then_inc(res_in, 16)
                if live(b - 2):
                    sp.wait_ge(x2_ready, b - 1)
                    sp.dma_start(io["x2"][bass.ds((b - 2) * S, S), :], y[:, p, :]).then_inc(x2_out[p], 16)
                load(b + 1, 1 - p)
                if live(b):
                    sp.wait_ge(maxT_evac, 2 * b + 2)
                    sp.dma_start(q_blk[MAX_ROW:MAX_ROW + 1, p, 0:1000].rearrange("o (t w) -> o t w", t=8),
                                 max_T[0:8, 0, 0:125]).then_inc(max_in[p], 16)
                    sp.dma_start(q_blk[MAX_ROW:MAX_ROW + 1, p, 1000:1600].rearrange("o (t w) -> o t w", t=5),
                                 max_T[0:5, 1, 0:120]).then_inc(max_in[p], 16)

            load(0, 0)
            sp.dma_start(io["sorted"].rearrange("(p r) e -> p r e", p=128),
                         zeros[:, :].unsqueeze(1).to_broadcast([128, NT * SLOTS // 128, E])).then_inc(zeros_out, 16)
            run(sp, position)
            sp.wait_ge(zeros_out, 16)
            for p in range(2):
                sp.wait_ge(x2_out[p], 16 * (B // 2))

        @block.gpsimd
        def _(pool):
            for n, (rows, value) in enumerate(((v[:, :, :, :, :], 0.0), (v[:, :, :, :, D2:D2 + 1], 1.0),
                                               (k_T[PR:PR + 2, :, :, :], 1.0), (q_blk[PR:PR + 2, :, :], 1.0),
                                               (half[:, :], -0.5), (zeros[:, :], 0.0))):
                pool.memset(rows, value).then_inc(ones_set, 1)
                pool.wait_ge(ones_set, n + 1)
            pool.wait_ge(consts_in, 16 * 12)

            def position(b, p):
                if live(b):
                    pool.wait_ge(q_evac, b + 1)
                    wait(pool, shifted_ready, 12 * (b - 1))
                    for part, (h0, n) in enumerate(PARTS):
                        cols = q_blk[0:PR, p, S * h0:S * (h0 + n)].rearrange("r (h s) -> r h s", h=n)
                        pool.tensor_tensor(cols, q_T[:, part, :].unsqueeze(1).to_broadcast([PR, n, S]),
                                           block_of[:, h0:h0 + n].unsqueeze(2).to_broadcast([PR, n, S]),
                                           ALU.mult).then_inc(blk_ready, 1)
                if live(b - 1):
                    pool.wait_ge(var_ready, b)
                    pool.tensor_tensor(rstd[:, :], veps[:, :], half[:, :], ALU.pow).then_inc(rstd_ready, 1)

            run(pool, position)

        @block.tensor
        def _(pe):
            pe.wait_ge(consts_in, 16 * 12)
            pe.wait_ge(ones_set, 4)

            def front(b, p):
                pe.wait_ge(x1_in[p], 8 * slot(b, p))
                wait(pe, q_evac, b)
                for k in range(KE):
                    last = pe.transpose(front_ps[:, S * k:S * k + S], x1_nat[:, p, 128 * k:128 * k + 128], ident[0:S, 0:S])
                last.then_inc(x1T_ready, 1)
                pe.wait_ge(ctx_in[p], 8 * slot(b, p))
                wait(pe, max_done, 13 * b)
                for part in range(3):
                    for k in range(KE):
                        last = pe.matmul(stream_ps[part][0:PR, 0:S2], wk[:, k, PR * part:PR * part + PR], c_T[:, p, k, :],
                                         start=(k == 0), stop=(k == KE - 1))
                    last.then_inc(k_ready, 1)
                pe.wait_ge(x1T_evac, b + 1)
                for part in range(3):
                    for k in range(KE):
                        last = pe.matmul(front_ps[0:PR, S * (2 + part):S * (3 + part)], wq[:, k, PR * part:PR * part + PR],
                                         x1_T[:, k, :], start=(k == 0), stop=(k == KE - 1))
                last.then_inc(q_ready, 1)

            def values(b, p):
                for i, (c0, n) in enumerate(CTX):
                    pe.wait_ge(k_evac, 3 * b + i + 1)
                    for k in range(KE):
                        last = pe.matmul(stream_ps[i][0:n, 0:E], c_T[:, p, k, c0:c0 + n], wv[:, k, :],
                                         start=(k == 0), stop=(k == KE - 1))
                    last.then_inc(v_ready, 1)

            def rows(b, p, t0, t1):
                if t0 == 0:
                    pe.wait_ge(k_evac, 3 * b + 3)
                    pe.wait_ge(mask_in[p], 24 * slot(b, p))
                for t in range(t0, t1):
                    part, col, w = TILES[t]
                    pe.wait_ge(blk_ready, 3 * b + part + 1)
                    if t < 3:
                        pe.wait_ge(v_evac, 3 * b + t + 1)
                    else:
                        pe.wait_ge(max_done, 13 * b + t - 2)
                    pe.matmul(stream_ps[t % 3][0:w, 0:S2], q_blk[0:MASK_ROW + 1, p, col:col + w],
                              k_T[0:MASK_ROW + 1, p, part, :], start=True, stop=True).then_inc(score_ready, 1)

            def maxima(b, p):
                pe.wait_ge(max_done, 13 * b + 13)
                wait(pe, o_evac, b)
                pe.transpose(o_ps[0:8, 0:125], neg_max[0:125, 0:8], ident[0:125, 0:125])
                pe.transpose(o_ps[0:5, 128:248], neg_max[0:120, 8:13], ident[0:120, 0:120]).then_inc(maxT_ready, 1)

            def shifted(b, p, r):
                part, col, w = RUNS[r]
                if r == 0:
                    pe.wait_ge(max_in[p], 16 * slot(b, p))
                for j, (c0, n) in enumerate(CTX):
                    e = 3 * r + j
                    wait(pe, exp_done, 12 * b + e - 1)
                    pe.matmul(exp_ps[e % 2][0:n, 0:w], k_T[0:MAX_ROW + 1, p, part, c0:c0 + n],
                              q_blk[0:MAX_ROW + 1, p, col:col + w], start=True, stop=True).then_inc(shifted_ready, 1)

            def attend(b, p, quad):
                pe.wait_ge(exp_done, 12 * b + 3 * quad + 3)
                if quad == 0:
                    pe.wait_ge(v_evac, 3 * b + 3)
                    pe.wait_ge(maxT_evac, 2 * b + 2)
                for j, (c0, n) in enumerate(CTX):
                    for q in range(4):
                        h = 4 * quad + q
                        last = pe.matmul(o_ps[32 * q:32 * q + 32, S * quad:S * quad + S], v[0:n, p, j, h, :],
                                         probs[0:n, j, S * h:S * h + S], start=(j == 0), stop=(j == 2),
                                         tile_position=(0, 32 * q))
                if quad == 3:
                    last.then_inc(o_ready, 1)

            def sums(b):
                pe.wait_ge(o_evac, b + 1)
                wait(pe, picked, 4 * (b - 1) + 2)
                pe.matmul(misc_ps[:, 0:4 * S], sum_of[:, :], o_raw[:, :], start=True, stop=True).then_inc(sums_ready, 1)

            def project(b):
                pe.wait_ge(o_normed, b + 1)
                for quad in range(4):
                    last = pe.matmul(misc_ps[0:S, 0:E], o_T[:, S * quad:S * quad + S], wp[:, quad, :],
                                     start=(quad == 0), stop=(quad == 3))
                last.then_inc(y_ready, 1)

            def turn(b, p):
                pe.wait_ge(x2_ready, b + 1)
                for k in range(KE):
                    last = pe.transpose(misc_ps[:, S * k:S * k + S], y[:, p, 128 * k:128 * k + 128], ident[0:S, 0:S])
                last.then_inc(x2T_ready, 1)

            def route(b):
                pe.wait_ge(x2T_evac, b + 1)
                for k in range(KE):
                    last = pe.matmul(misc_ps[0:S, 0:X], x2_T[:, k, :], router[:, k, :], start=(k == 0), stop=(k == KE - 1))
                last.then_inc(logits_ready, 1)

            def position(b, p):
                now, then, old = live(b), live(b - 1), live(b - 2)
                if now:
                    front(b, p)
                if then:
                    shifted(b - 1, 1 - p, 0)
                    shifted(b - 1, 1 - p, 1)
                    attend(b - 1, 1 - p, 0)
                if old:
                    turn(b - 2, p)
                if then:
                    shifted(b - 1, 1 - p, 2)
                    attend(b - 1, 1 - p, 1)
                if old:
                    route(b - 2)
                if then:
                    shifted(b - 1, 1 - p, 3)
                if now:
                    values(b, p)
                if then:
                    attend(b - 1, 1 - p, 2)
                    attend(b - 1, 1 - p, 3)
                if now:
                    rows(b, p, 0, 6)
                if then:
                    sums(b - 1)
                if now:
                    rows(b, p, 6, 13)
                if then:
                    project(b - 1)
                if now:
                    maxima(b, p)

            run(pe, position)

        @block.scalar
        def _(act):
            def exps(b, r):
                part, col, w = RUNS[r]
                for j, (c0, n) in enumerate(CTX):
                    e = 3 * r + j
                    act.wait_ge(shifted_ready, 12 * b + e + 1)
                    act.activation(probs[0:n, j, col:col + w], exp_ps[e % 2][0:n, 0:w], ACT.Exp).then_inc(exp_done, 1)

            def position(b, p):
                now, then, old = live(b), live(b - 1), live(b - 2)
                if now:
                    act.wait_ge(x1T_ready, b + 1)
                    wait(act, q_ready, b)
                    act.activation(x1_T[:, :, :], front_ps[:, 0:KE * S].rearrange("p (k s) -> p k s", k=KE),
                                   ACT.Copy).then_inc(x1T_evac, 1)
                    wait(act, shifted_ready, 12 * (b - 1))
                    for part in range(3):
                        act.wait_ge(k_ready, 3 * b + part + 1)
                        act.activation(k_T[0:PR, p, part, :], stream_ps[part][0:PR, 0:S2], ACT.Identity,
                                       bias=k_bias[:, part:part + 1]).then_inc(k_evac, 1)
                if then:
                    wait(act, o_ready, b - 1)
                    exps(b - 1, 0)
                    exps(b - 1, 1)
                if old:
                    act.wait_ge(x2T_ready, b - 1)
                    wait(act, logits_ready, b - 2)
                    act.activation(x2_T[:, :, :], misc_ps[:, 0:KE * S].rearrange("p (k s) -> p k s", k=KE),
                                   ACT.Copy).then_inc(x2T_evac, 1)
                if then:
                    exps(b - 1, 2)
                    exps(b - 1, 3)
                    act.wait_ge(o_ready, b)
                    wait(act, o_normed, b - 1)
                    act.activation(o_raw[:, :], o_ps[:, 0:4 * S], ACT.Copy).then_inc(o_evac, 1)
                if now:
                    act.wait_ge(maxT_ready, b + 1)
                    if live(b - 1):
                        act.wait_ge(max_in[1 - p], 16 * slot(b - 1, 1 - p))
                    act.activation(max_T[0:8, 0, 0:125], o_ps[0:8, 0:125], ACT.Copy).then_inc(maxT_evac, 1)
                    act.activation(max_T[0:5, 1, 0:120], o_ps[0:5, 128:248], ACT.Copy).then_inc(maxT_evac, 1)

            act.wait_ge(consts_in, 16 * 12)
            run(act, position)

        @block.vector
        def _(dve):
            dve.wait_ge(mask_read, 16)
            dve.tensor_scalar(mask_f[:, :], mask_u8[:, :], MASKED, None, ALU.mult).then_inc(mask_made, 1)
            dve.wait_ge(consts_in, 16 * 12)
            dve.wait_ge(ones_set, 4)

            def normalize(b, p):
                dve.wait_ge(rstd_ready, b + 1)
                dve.tensor_scalar(y[:, p, :], y[:, p, :], mv[:, p, 0:1], rstd[:, 0:1],
                                  ALU.subtract, ALU.mult).then_inc(x2_ready, 1)

            def pick(b):
                dve.wait_ge(logits_ready, b + 1)
                logits = misc_ps[0:S, 0:X]
                wait(dve, picked, 4 * b)
                dve.tensor_reduce(best[:, :], logits, AX_X, ALU.max).then_inc(picked, 1)
                dve.wait_ge(picked, 4 * b + 1)
                dve.scalar_tensor_tensor(out=value[:, :], in0=logits, scalar=best[:, 0:1], in1=rank[:, :],
                                         op0=ALU.is_equal, op1=ALU.add).then_inc(picked, 1)
                dve.wait_ge(picked, 4 * b + 2)
                dve.tensor_reduce(first[:, :], value[:, :], AX_X, ALU.max).then_inc(picked, 1)
                dve.wait_ge(picked, 4 * b + 3)
                dve.tensor_scalar(oh[:, bass.ds(b, 1), :], value[:, :].unsqueeze(1), first[:, 0:1], None,
                                  ALU.is_equal).then_inc(picked, 1)

            def biased(b, p):
                wait(dve, o_ready, b - 1)
                for i, (c0, n) in enumerate(CTX):
                    dve.wait_ge(v_ready, 3 * b + i + 1)
                    heads = lambda t: t.rearrange("c (h d) -> c h d", h=N2)
                    dve.tensor_tensor(v[0:n, p, i, :, 0:D2], heads(stream_ps[i][0:n, 0:E]), heads(v_bias[0:n, :]),
                                      ALU.add).then_inc(v_evac, 1)

            def maxima(b, t0, t1):
                if t0 == 0:
                    wait(dve, maxT_ready, b)
                for t in range(t0, t1):
                    w = TILES[t][2]
                    dve.wait_ge(score_ready, 13 * b + t + 1)
                    dve.tensor_reduce(neg_max[0:w, t:t + 1], stream_ps[t % 3][0:w, 0:S2], AX_X, ALU.max,
                                      negate=True).then_inc(max_done, 1)

            def divide(b):
                dve.wait_ge(sums_ready, b + 1)
                wait(dve, o_normed, b)
                dve.reciprocal(inv[:, :], misc_ps[:, 0:4 * S]).then_inc(inv_ready, 1)
                dve.wait_ge(inv_ready, b + 1)
                wait(dve, y_ready, b)
                dve.tensor_tensor(o_T[:, :], o_raw[:, :], inv[:, :], ALU.mult).then_inc(o_normed, 1)

            def add_up(b, p):
                dve.wait_ge(y_ready, b + 1)
                dve.wait_ge(res_in, 16 * (b + 1))
                wait(dve, x2T_ready, b - 1)
                if live(b - 2):
                    dve.wait_ge(x2_out[p], 8 * slot(b - 2, p))
                dve.tensor_tensor(y[:, p, :], misc_ps[0:S, 0:E], x1_res[:, :], ALU.add).then_inc(added, 1)
                dve.wait_ge(added, b + 1)
                dve.bn_stats(stats[:, :], y[:, p, :]).then_inc(stats_done, 1)
                dve.wait_ge(stats_done, 2 * b + 1)
                wait(dve, x2_ready, b - 1)
                dve.memset(pause[:, :], 0.0)
                dve.bn_aggr(mv[:, p, :], stats[:, :]).then_inc(stats_done, 1)
                dve.wait_ge(stats_done, 2 * b + 2)
                dve.tensor_scalar(veps[:, :], mv[:, p, 1:2], EPS, None, ALU.add).then_inc(var_ready, 1)

            def position(b, p):
                now, then, old = live(b), live(b - 1), live(b - 2)
                if old:
                    normalize(b - 2, p)
                if now:
                    dve.wait_ge(q_ready, b + 1)
                    wait(dve, blk_ready, 3 * b)
                    dve.tensor_tensor(q_T[:, :, :], front_ps[0:PR, 2 * S:5 * S].rearrange("r (t s) -> r t s", t=3),
                                      q_bias[:, :].unsqueeze(2).to_broadcast([PR, 3, S]), ALU.add).then_inc(q_evac, 1)
                if old:
                    pick(b - 2)
                if now:
                    biased(b, p)
                    maxima(b, 0, 6)
                if then:
                    divide(b - 1)
                if now:
                    maxima(b, 6, 13)
                if then:
                    add_up(b - 1, 1 - p)

            run(dve, position)


def experts(nc, io, mem):
    gu, dn, oh, gu_in = mem["gate_up"], mem["down"], mem["choice"], mem["gate_up_in"]
    with ExitStack() as ctx:
        sb = lambda name, shape, dt=F32: ctx.enter_context(nc.sbuf_tensor(name, shape, dt))
        sem = lambda name: ctx.enter_context(nc.semaphore(name))
        bank = [ctx.enter_context(nc.psum_tensor(f"c_bank{i}", [128, 512], F32)) for i in range(8)]
        gate_ps, up_ps, hT_ps, y_ps, xT_ps = bank[0:2], bank[2:4], bank[4:6], bank[6], bank[7]
        before_ps, count_ps = bank[0], bank[1]

        ident = sb("c_ident", [128, 128])
        earlier, ones = sb("c_earlier", [S, S]), sb("c_ones", [S, S])
        full, tile_no = sb("c_full", [S, CT]), sb("c_tile_no", [1, NT])
        count = sb("c_count", [S, X, B])
        upto = sb("c_upto", [S, 2, X, B])
        over = sb("c_over", [S, X, CT])
        tiles_of = sb("c_tiles_of", [S, X])
        ends = sb("c_ends", [S, 2, X])
        start = sb("c_start", [S, X])
        passed = sb("c_passed", [1, NT, X])
        expert_f, expert_of = sb("c_expert_f", [1, NT]), sb("c_expert_of", [1, NT], I32)
        place = sb("c_place", [S, B, X])
        slot_f, slot_of = sb("c_slot_f", [S, B]), sb("c_slot_of", [S, B], U32)
        x2 = sb("c_x2", [S, B, E])
        x_tile = sb("c_x_tile", [SLOTS, 2, E])
        x_T = sb("c_x_T", [128, 2, KE, SLOTS])
        gate = sb("c_gate", [SLOTS, 2, QF])
        hidden = sb("c_hidden", [SLOTS, 2, FF])
        h_T = sb("c_h_T", [128, FC, SLOTS])
        y_tile = sb("c_y_tile", [SLOTS, 2, E])
        answer = sb("c_answer", [S, 2, GB, E])
        stats, mv = sb("c_stats", [S, GB, 6]), sb("c_mv", [S, 2, GB, 2])
        veps, rstd, half = sb("c_veps", [S, GB]), sb("c_rstd", [S, 2, GB]), sb("c_half", [S, GB])

        consts_in, x2_in, dn_in, half_set = (sem(n) for n in ("c_consts_in", "c_x2_in", "c_dn_in", "c_half_set"))
        counted, math, slots_ready, experts_ready = (sem(n) for n in ("c_counted", "c_math", "c_slots_ready", "c_experts_ready"))
        scattered = sem("c_scattered")
        tile_in, tile_out, gather_in, out_out = ([sem(f"c_{n}{p}") for p in range(2)] for n in ("tile_in", "tile_out", "gather_in", "out_out"))
        xT_ready, xT_evac, gate_ready, up_ready, silu_done, gated = (sem(n) for n in (
            "c_xT_ready", "c_xT_evac", "c_gate_ready", "c_up_ready", "c_silu_done", "c_gated"))
        hT_ready, hT_evac_a, hT_evac_b, y_ready, y_evac = (sem(n) for n in (
            "c_hT_ready", "c_hT_evac_a", "c_hT_evac_b", "c_y_ready", "c_y_evac"))
        added, stats_done, var_ready, rstd_ready, out_ready = (sem(n) for n in (
            "c_added", "c_stats_done", "c_var_ready", "c_rstd_ready", "c_out_ready"))

        def run(eng, position):
            for j in range(2):
                position(j, j % 2)
            with eng.Fori(1, NT // 2 - 1) as pair:
                for p in range(2):
                    position(2 * pair + p, p)
            for j in range(NT - 2, NT + 1):
                position(j, j % 2)

        def live(j):
            return not isinstance(j, int) or 0 <= j < NT

        block = ctx.enter_context(nc.Block())

        @block.sync
        def _(sp):
            for dst, src in ((earlier[:, :], io["earlier"]), (ones[:, :], io["ones"]), (full[:, :], io["full"]),
                             (tile_no[:, :], io["tile_no"]), (ident[:, :], io["ident"])):
                sp.dma_start(dst, src).then_inc(consts_in, 16)
            sp.dma_start(x2[:, :, :], io["x2"].rearrange("(b s) e -> s b e", s=S)).then_inc(x2_in, 16)
            for x in range(X):
                sp.dma_start(dn[:, x], io["down"][x]).then_inc(dn_in, 16)

            def load(j, p):
                if live(j):
                    wait(sp, xT_ready, j - 1)
                    sp.dma_start(x_tile[:, p, :], io["sorted"][bass.ds(j * SLOTS, SLOTS), :]).then_inc(tile_in[p], 16)

            def position(j, p):
                load(j + 2, p)
                if live(j - 1):
                    sp.wait_ge(y_evac, j)
                    sp.dma_start(io["answers"][bass.ds((j - 1) * SLOTS, SLOTS), :], y_tile[:, 1 - p, :])\
                      .then_inc(tile_out[1 - p], 16)

            sp.wait_ge(scattered, 16 * B)
            for j in range(2):
                load(j, j)
            run(sp, position)
            for g in range(G1):
                sp.wait_ge(out_ready, g + 1)
                sp.dma_start(io["out"][GB * g:GB * g + GB].rearrange("b s e -> s b e"), answer[:, g % 2])\
                  .then_inc(out_out[g % 2], 16)
            for p in range(2):
                sp.wait_ge(out_out[p], 16 * (G1 // 2))

        @block.gpsimd
        def _(pool):
            pool.memset(half[:, :], -0.5).then_inc(half_set, 1)
            pool.wait_ge(x2_in, 16)
            pool.wait_ge(slots_ready, 1)
            for b in range(B):
                pool.indirect_dma_start(out=io["sorted"], out_offset=bass.IndirectOffsetOnAxis(ap=slot_of[:, b:b + 1], axis=0),
                                        in_=x2[:, b, :], in_offset=None).then_inc(scattered, 16)
            for p in range(2):
                pool.wait_ge(tile_out[p], 16 * (NT // 2))

            def gather(g):
                if g >= 2:
                    pool.wait_ge(out_out[g % 2], 16 * (g // 2))
                for b in range(GB):
                    n = GB * g + b
                    pool.indirect_dma_start(out=answer[:, g % 2, b, :], out_offset=None, in_=io["answers"],
                                            in_offset=bass.IndirectOffsetOnAxis(ap=slot_of[:, n:n + 1], axis=0))\
                        .then_inc(gather_in[g % 2], 16)

            pool.wait_ge(half_set, 1)
            gather(0)
            for g in range(G1):
                if g + 1 < G1:
                    gather(g + 1)
                pool.wait_ge(var_ready, g + 1)
                pool.tensor_tensor(rstd[:, g % 2], veps[:, :], half[:, :], ALU.pow).then_inc(rstd_ready, 1)

        @block.tensor
        def _(pe):
            pe.wait_ge(consts_in, 16 * 5)
            flat = oh[:, :, :].rearrange("s b x -> s (b x)")
            pe.matmul(before_ps[0:S, 0:B * X], earlier[:, :], flat, start=True, stop=True).then_inc(counted, 1)
            pe.matmul(count_ps[0:S, 0:B * X], ones[:, :], flat, start=True, stop=True).then_inc(counted, 1)

            def expert(j):
                return pe.value_load(expert_of[0:1, bass.ds(j, 1)], min_val=0, max_val=X - 1)

            def turn(j, p):
                pe.wait_ge(tile_in[p], 8 * (j - p + 2))
                wait(pe, xT_evac, j)
                for k in range(KE):
                    last = pe.transpose(xT_ps[:, SLOTS * k:SLOTS * k + SLOTS], x_tile[:, p, 128 * k:128 * k + 128], ident[:, :])
                last.then_inc(xT_ready, 1)

            def gate_up(j, p):
                x = expert(j)
                pe.wait_ge(xT_evac, j + 1)
                for h in range(2):
                    for ps, col, ready, freed in ((gate_ps, 0, gate_ready, silu_done), (up_ps, FF, up_ready, gated)):
                        wait(pe, freed, 2 * (j - 1) + h + 1)
                        for k in range(KE):
                            cols = slice(col + QF * h, col + QF * h + QF)
                            last = pe.matmul(ps[h][:, 0:QF], x_T[:, p, k, :],
                                             gu[:, bass.ds(x, 1), k, cols].rearrange("p a f -> p (a f)"),
                                             start=(k == 0), stop=(k == KE - 1))
                        last.then_inc(ready, 1)

            def turn_hidden(j, p):
                pe.wait_ge(gated, 2 * j + 2)
                wait(pe, hT_evac_a, j)
                wait(pe, hT_evac_b, 2 * j)
                for c in range(FC):
                    n = min(128, FF - 128 * c)
                    last = pe.transpose(hT_ps[c // 4][0:n, SLOTS * (c % 4):SLOTS * (c % 4) + SLOTS],
                                        hidden[:, p, 128 * c:128 * c + n], ident[:, :])
                last.then_inc(hT_ready, 1)

            def down(j, p):
                x = expert(j)
                pe.wait_ge(hT_evac_a, j + 1)
                pe.wait_ge(hT_evac_b, 2 * j + 2)
                wait(pe, y_evac, j)
                for c in range(FC):
                    n = min(128, FF - 128 * c)
                    last = pe.matmul(y_ps[:, 0:E], h_T[0:n, c, :], dn[0:n, bass.ds(x, 1), c, :].rearrange("p a e -> p (a e)"),
                                     start=(c == 0), stop=(c == FC - 1))
                last.then_inc(y_ready, 1)

            def position(j, p):
                if live(j - 1):
                    turn_hidden(j - 1, 1 - p)
                if live(j):
                    gate_up(j, p)
                if live(j - 1):
                    down(j - 1, 1 - p)
                if live(j + 1):
                    turn(j + 1, 1 - p)

            turn(0, 0)
            pe.wait_ge(experts_ready, 1)
            pe.wait_ge(gu_in, 16 * X * KE)
            pe.wait_ge(dn_in, 16 * X)
            run(pe, position)

        @block.scalar
        def _(act):
            def position(j, p):
                if live(j - 1):
                    act.wait_ge(hT_ready, j)
                    wait(act, y_ready, j - 1)
                    act.activation(h_T[:, 4, :], hT_ps[1][:, 0:SLOTS], ACT.Copy).then_inc(hT_evac_b, 1)
                    act.activation(h_T[0:FF - 640, 5, :], hT_ps[1][0:FF - 640, SLOTS:2 * SLOTS], ACT.Copy).then_inc(hT_evac_b, 1)
                if live(j):
                    for h in range(2):
                        act.wait_ge(gate_ready, 2 * j + h + 1)
                        wait(act, gated, 2 * (j - 1) + h + 1)
                        act.activation(gate[:, h, :], gate_ps[h][:, 0:QF], ACT.Silu).then_inc(silu_done, 1)
                if live(j - 1):
                    act.wait_ge(y_ready, j)
                    if live(j - 3):
                        act.wait_ge(tile_out[1 - p], 8 * (j - 3 - (1 - p) + 2))
                    act.activation(y_tile[:, 1 - p, :], y_ps[:, 0:E], ACT.Copy).then_inc(y_evac, 1)

            run(act, position)

        @block.vector
        def _(dve):
            steps = [0]

            def then(instruction):
                steps[0] += 1
                instruction.then_inc(math, 1)
                dve.wait_ge(math, steps[0])

            def running_sum(buffers, n):
                at, step = 0, 1
                while step < n:
                    old, new = buffers(at), buffers(1 - at)
                    then(dve.tensor_copy(new(0, step), old(0, step)))
                    then(dve.tensor_tensor(new(step, n), old(step, n), old(0, n - step), ALU.add))
                    at, step = 1 - at, 2 * step
                return at

            dve.wait_ge(consts_in, 16 * 5)
            dve.wait_ge(counted, 2)
            per_batch = lambda t: t.rearrange("s (b x) -> s x b", x=X)
            then(dve.tensor_copy(count[:, :, :], per_batch(count_ps[0:S, 0:B * X])))
            then(dve.tensor_copy(upto[:, 0], count[:, :, :]))
            u = running_sum(lambda i: lambda a, z: upto[:, i, :, a:z], B)
            then(dve.tensor_tensor(over[:, :, :], upto[:, u, :, B - 1:B].to_broadcast([S, X, CT]),
                                   full[:, :].unsqueeze(1).to_broadcast([S, X, CT]), ALU.is_gt))
            then(dve.tensor_reduce(tiles_of[:, :], over[:, :, :], AX_X, ALU.add))
            then(dve.tensor_copy(ends[:, 0, :], tiles_of[:, :]))
            e = running_sum(lambda i: lambda a, z: ends[:, i, a:z], X)
            then(dve.tensor_tensor(passed[:, :, :], ends[0:1, e, :].unsqueeze(1).to_broadcast([1, NT, X]),
                                   tile_no[:, :].unsqueeze(2).to_broadcast([1, NT, X]), ALU.is_le))
            then(dve.tensor_reduce(expert_f[:, :], passed[:, :, :], AX_X, ALU.add))
            dve.tensor_scalar(expert_of[:, :], expert_f[:, :], float(X - 1), None, ALU.min).then_inc(experts_ready, 1)
            then(dve.tensor_tensor(start[:, :], ends[:, e, :], tiles_of[:, :], ALU.subtract))
            then(dve.tensor_scalar(start[:, :], start[:, :], float(SLOTS), None, ALU.mult))
            turned = lambda t: t.rearrange("s x b -> s b x")
            then(dve.tensor_tensor(place[:, :, :], before_ps[0:S, 0:B * X].rearrange("s (b x) -> s b x", x=X),
                                   turned(upto[:, u]), ALU.add))
            then(dve.tensor_tensor(place[:, :, :], place[:, :, :], turned(count[:, :, :]), ALU.subtract))
            then(dve.tensor_tensor(place[:, :, :], place[:, :, :], start[:, :].unsqueeze(1).to_broadcast([S, B, X]), ALU.add))
            then(dve.tensor_tensor(place[:, :, :], place[:, :, :], oh[:, :, :], ALU.mult))
            then(dve.tensor_reduce(slot_f[:, :], place[:, :, :], AX_X, ALU.add))
            dve.tensor_copy(slot_of[:, :], slot_f[:, :]).then_inc(slots_ready, 1)

            def turned_tile(j, p):
                dve.wait_ge(xT_ready, j + 1)
                wait(dve, up_ready, 2 * (j - 1))
                dve.tensor_copy(x_T[:, p].rearrange("p k s -> p (k s)"), xT_ps[:, 0:KE * SLOTS]).then_inc(xT_evac, 1)

            def position(j, p):
                if live(j - 1):
                    dve.wait_ge(hT_ready, j)
                    wait(dve, y_ready, j - 1)
                    dve.tensor_copy(h_T[:, 0:4, :].rearrange("p c s -> p (c s)"), hT_ps[0][:, 0:4 * SLOTS]).then_inc(hT_evac_a, 1)
                if live(j):
                    wait(dve, hT_ready, j - 1)
                    for h in range(2):
                        dve.wait_ge(silu_done, 2 * j + h + 1)
                        dve.wait_ge(up_ready, 2 * j + h + 1)
                        dve.tensor_tensor(hidden[:, p, QF * h:QF * h + QF], gate[:, h, :], up_ps[h][:, 0:QF],
                                          ALU.mult).then_inc(gated, 1)
                if live(j + 1):
                    turned_tile(j + 1, 1 - p)

            turned_tile(0, 0)
            run(dve, position)

            def finish(g):
                dve.wait_ge(rstd_ready, g + 1)
                for b in range(GB):
                    last = dve.tensor_scalar(answer[:, g % 2, b, :], answer[:, g % 2, b, :], mv[:, g % 2, b, 0:1],
                                             rstd[:, g % 2, b:b + 1], ALU.subtract, ALU.mult)
                last.then_inc(out_ready, 1)

            for g in range(G1):
                dve.wait_ge(gather_in[g % 2], 16 * GB * (g // 2 + 1))
                dve.tensor_tensor(answer[:, g % 2], answer[:, g % 2], x2[:, GB * g:GB * g + GB, :], ALU.add).then_inc(added, 1)
                dve.wait_ge(added, g + 1)
                wait(dve, stats_done, 2 * GB * g)
                for b in range(GB):
                    dve.bn_stats(stats[:, b, :], answer[:, g % 2, b, :]).then_inc(stats_done, 1)
                if g >= 2:
                    dve.wait_ge(out_ready, g - 1)
                for b in range(GB):
                    dve.wait_ge(stats_done, 2 * GB * g + b + 1)
                    dve.bn_aggr(mv[:, g % 2, b, :], stats[:, b, :]).then_inc(stats_done, 1)
                dve.wait_ge(stats_done, 2 * GB * g + 2 * GB)
                wait(dve, rstd_ready, g)
                dve.tensor_scalar(veps[:, :], mv[:, g % 2, :, 1], EPS, None, ALU.add).then_inc(var_ready, 1)
                if g >= 1:
                    finish(g - 1)
            finish(G1 - 1)


def decoder_layer(nc, io, phases="abc"):
    with ExitStack() as ctx:
        gu = ctx.enter_context(nc.sbuf_tensor("gate_up", [128, X, KE, 2 * FF], F32))
        dn = ctx.enter_context(nc.sbuf_tensor("down", [128, X, FC, E], F32))
        choice = ctx.enter_context(nc.sbuf_tensor("choice", [S, B, X], F32))
        gate_up_in = ctx.enter_context(nc.semaphore("gate_up_in"))
        for name, rows, cols in (("x1", B * S, E), ("x2", B * S, E), ("mask_f", B, S2),
                                 ("sorted", NT * SLOTS, E), ("answers", NT * SLOTS, E)):
            if name not in io:
                io[name] = nc.dram_tensor(name, (rows, cols), F32).ap()

        def carve(space, parts):
            mem, at = {}, 0
            for name, (a, b) in parts.items():
                mem[name] = space[:, at:at + a * b].rearrange("p (a b) -> p a b", a=a)
                at += a * b
            return mem

        gu_flat = gu[:, :, :, :].rearrange("p x k f -> p (x k f)")
        dn_flat = dn[:, :, :, :].rearrange("p x c e -> p (x c e)")
        if "a" in phases:
            self_attention(nc, io, carve(gu_flat, {"wq": (KE, 1024), "wk": (KE, 1024), "wv": (KE, 1024),
                                                   "wu": (C1, E), "xT": (KE, B * S)}))
        if "b" in phases:
            cross_attention(nc, io, carve(dn_flat, {"q_w": (KE, 3 * PR), "k_w": (KE, 3 * PR), "v_w": (KE, E),
                                                    "p_w": (4, E), "probs": (3, N2 * S)})
                            | {"choice": choice, "gate_up": gu_flat, "gate_up_in": gate_up_in})
        if "c" in phases:
            experts(nc, io, {"gate_up": gu, "down": dn, "choice": choice, "gate_up_in": gate_up_in})



def _constants(np):
    block_of = np.zeros((PR, N2), np.float32)
    for h0, n in PARTS:
        for h in range(n):
            block_of[D2 * h:D2 * h + D2, h0 + h] = D2 ** -0.5
    sum_of = np.zeros((128, 128), np.float32)
    for q in range(4):
        sum_of[32 * q + D2, 32 * q:32 * q + 32] = 1.0
    ones = np.ones((S, S), np.float32)
    return {
        "ident": np.eye(128, dtype=np.float32), "below": np.tril(ones, -1), "earlier": np.triu(ones, 1), "ones": ones,
        "block_of": block_of, "sum_of": sum_of, "rank": np.tile((X - np.arange(X, dtype=np.float32)) / (2 * X), (S, 1)),
        "full": np.tile(SLOTS * np.arange(CT, dtype=np.float32), (S, 1)), "tile_no": np.arange(NT, dtype=np.float32)[None],
    }


def _arrays(np, a):
    rows = lambda w: w.reshape(-1, 128, w.shape[-1]).transpose(1, 0, 2)

    def parts(w):
        out = np.zeros((w.shape[0], len(PARTS) * PR), w.dtype)
        for i, (h0, n) in enumerate(PARTS):
            out[:, PR * i:PR * i + D2 * n] = w[:, D2 * h0:D2 * (h0 + n)]
        return out

    p_w = np.zeros((4, 32, 4, E), np.float32)
    p_w[:, 0:D2] = a["L0_xattn_proj_w"].reshape(4, 4, D2, E).transpose(1, 2, 0, 3)
    p_w[0, D2, 0] = a["L0_xattn_proj_b"]
    down = np.zeros((X, FC * 128, E), np.float32)
    down[:, 0:FF] = a["L0_ffn_down_w"].transpose(0, 2, 1)
    gate_up = np.concatenate([a["L0_ffn_gate_w"], a["L0_ffn_up_w"]], axis=1).transpose(0, 2, 1)
    heads = lambda w: rows(w.transpose(1, 0, 2).reshape(E, N1 * D1))
    return {
        "x": a["x"], "xT": a["x"].reshape(B * S, E).T.reshape(KE, 128, B * S),
        "wq": heads(a["L0_attn_WQ"]), "wk": heads(a["L0_attn_WK"]), "wv": heads(a["L0_attn_WV_down"]),
        "wu": rows(a["L0_attn_WV_up"].reshape(N1 * D1, E)),
        "ctxT": a["ctx_1024"].transpose(0, 2, 1).reshape(B, KE, 128, S2).transpose(0, 2, 1, 3),
        "mask": a["mask_BxS2_bk0"],
        "q_w": rows(parts(a["L0_xattn_q_w"])), "q_b": parts(a["L0_xattn_q_b"][None]).reshape(-1, PR).T,
        "k_w": rows(parts(a["L0_xattn_kv_w"][:, 0:E])), "k_b": parts(a["L0_xattn_kv_b"][None, 0:E]).reshape(-1, PR).T,
        "v_w": rows(a["L0_xattn_kv_w"][:, E:]), "v_b": a["L0_xattn_kv_b"][E:],
        "p_w": p_w.reshape(128, 4, E), "router": rows(a["L0_ffn_router_w"].T),
        "gate_up": gate_up.reshape(X * KE * 128, 2 * FF),
        "down": down.reshape(X, FC, 128, E).transpose(0, 2, 1, 3),
    }


def kernel(**inputs):
    import numpy as _np
    import concourse.bacc as _bacc
    from concourse.bass_utils import run_bass_kernel_spmd as _run

    nc = _bacc.Bacc("TRN2", target_bir_lowering=False, num_devices=1)
    given = {name: _np.asarray(value) for name, value in inputs.items()}
    arrays, io = {}, {}
    for name, a in {**_arrays(_np, given), **_constants(_np)}.items():
        a = arrays[f"in_{name}"] = _np.ascontiguousarray(a)
        io[name] = nc.dram_tensor(f"in_{name}", a.shape, mybir.dt.from_np(a.dtype), kind="ExternalInput").ap()
    io["out"] = nc.dram_tensor("out_0", (B, S, E), F32, kind="ExternalOutput").ap()
    decoder_layer(nc, io)
    r = _run(nc, [arrays], core_ids=[0])
    return r.results[0]["out_0"]
```

```python
from contextlib import ExitStack

import concourse.bass as bass
from concourse import mybir

F32 = mybir.dt.float32
F32R = mybir.dt.float32r
U8 = mybir.dt.uint8
U32 = mybir.dt.uint32
I32 = mybir.dt.int32
ALU = mybir.AluOpType
ACT = mybir.ActivationFunctionType
AX_X = mybir.AxisListType.X

B, S, E = 32, 100, 256
KE = E // 128
EPS = 1e-5

N1, D1 = 16, 64
C1 = N1 * D1 // 128
GB = 4
G1 = B // GB
GS = GB * S
BELOW = -3.0e38


N2, D2 = 16, 16
S2 = 361
PARTS = [(0, 5), (5, 5), (10, 6)]
PR = 96
MASK_ROW, MAX_ROW = 96, 97
CTX = [(0, 121), (121, 120), (241, 120)]
TILES = [(p, S * h0 + w * i, w) for p, (h0, n) in enumerate(PARTS)
         for w in [S * n // (4 if n == 5 else 5)] for i in range(S * n // w)]
RUNS = [(0, 0, 500), (1, 500, 500), (2, 1000, 300), (2, 1300, 300)]
MASKED = -2.0 ** 100

X, FF = 8, 704
FC = -(-FF // 128)
QF = FF // 2
SLOTS = 128
NT = (B * S + X * (SLOTS - 1)) // SLOTS
CT = B * S // SLOTS


def wait(eng, sem, value):
    if isinstance(value, int) and value <= 0:
        return
    eng.wait_ge(sem, value)


def self_attention(nc, io, mem):
    wq, wk, wv, wu, xT = mem["wq"], mem["wk"], mem["wv"], mem["wu"], mem["xT"]
    with ExitStack() as ctx:
        sb = lambda name, shape, dt=F32: ctx.enter_context(nc.sbuf_tensor(name, shape, dt))
        sem = lambda name: ctx.enter_context(nc.semaphore(name))
        bank = [ctx.enter_context(nc.psum_tensor(f"a_bank{i}", [128, 512], F32)) for i in range(8)]
        q_ps, k_ps = bank[0], bank[1]
        score_ps = [bank[2], bank[3]]
        share_ps, v_ps = bank[4], bank[5]
        delta_ps = [bank[6], bank[7]]

        ident = sb("a_ident", [128, 128])
        below = sb("a_below", [S, S])
        q_blk = sb("a_q_blk", [128, 2, GB, 2, S])
        kT = sb("a_kT", [128, 2, GS])
        dead = sb("a_dead", [S, 2, GB, S])
        scores = sb("a_scores", [S, 2, 2, GB, S])
        neg_max = sb("a_neg_max", [S, 2, 2, GB])
        probs = sb("a_probs", [S, 2, 2, GB, S])
        total = sb("a_total", [S, 2, 2, GB])
        diag = sb("a_diag", [S, 2, 2, GB, S])
        top = sb("a_top", [S, 2, GB])
        inv = sb("a_inv", [S, 2, GB])
        share = sb("a_share", [S, 2, GB, 2 * D1])
        shareT = sb("a_shareT", [128, 2, GS])
        vT = sb("a_vT", [128, 2, GS])
        x_nat = sb("a_x", [S, GB, E])
        y = sb("a_y", [S, GB, E])
        stats = sb("a_stats", [S, GB, 6])
        pause = sb("a_pause", [1, 1])
        mv = sb("a_mv", [S, GB, 2])
        veps = sb("a_veps", [S, GB])
        rstd = sb("a_rstd", [S, GB])
        half = sb("a_half", [S, GB])

        consts_in, qk_in, vu_in, x_in, x1_out = (sem(n) for n in ("a_consts_in", "a_qk_in", "a_vu_in", "a_x_in", "a_x1_out"))
        half_set = sem("a_half_set")
        q_ready, k_ready, q_evac, k_evac = (sem(n) for n in ("a_q_ready", "a_k_ready", "a_q_evac", "a_k_evac"))
        scores_ready, dead_found, masked, max_ready = (sem(n) for n in ("a_scores_ready", "a_dead_found", "a_masked", "a_max_ready"))
        exp_done, diag_ready, sums_ready, share_ready = (sem(n) for n in ("a_exp_done", "a_diag_ready", "a_sums_ready", "a_share_ready"))
        shareT_ready, shareT_evac, v_ready, v_scaled = (sem(n) for n in ("a_shareT_ready", "a_shareT_evac", "a_v_ready", "a_v_scaled"))
        delta_steps, added, stats_done, var_ready, rstd_ready, x1_ready = (
            sem(n) for n in ("a_delta_steps", "a_added", "a_stats_done", "a_var_ready", "a_rstd_ready", "a_x1_ready"))

        def schedule(stages):
            def positions(g, cs, first=False, last=False):
                for c in cs:
                    for lag, do in stages:
                        if lag <= c:
                            if not last:
                                do(g, c - lag, C1 * g + c - lag)
                        elif lag <= c + C1 and not first:
                            do(g - 1, c - lag + C1, C1 * g + c - lag)
            return positions

        def run(eng, stages):
            positions = schedule(stages)
            positions(0, range(C1), first=True)
            with eng.Fori(1, G1) as g:
                positions(g, range(C1))
            positions(G1, range(C1), last=True)

        block = ctx.enter_context(nc.Block())

        @block.sync
        def _(sp):
            sp.dma_start(xT[:, 0, :], io["xT"][0]).then_inc(qk_in, 16)
            sp.dma_start(wq, io["wq"]).then_inc(qk_in, 16)
            sp.dma_start(xT[:, 1, :], io["xT"][1]).then_inc(qk_in, 16)
            sp.dma_start(wk, io["wk"]).then_inc(qk_in, 16)
            sp.dma_start(below[:, :], io["below"]).then_inc(consts_in, 16)
            sp.dma_start(ident[:, :], io["ident"]).then_inc(consts_in, 16)
            sp.dma_start(wv, io["wv"]).then_inc(vu_in, 16)
            sp.dma_start(wu, io["wu"]).then_inc(vu_in, 16)
            x_of = io["x"].rearrange("(g b) s e -> g s b e", b=GB)
            x1_of = io["x1"].rearrange("(g b s) e -> g s b e", b=GB, s=S)

            def load(g):
                wait(sp, added, GB * g)
                sp.dma_start(x_nat[:, :, :], x_of[g]).then_inc(x_in, 16)

            def store(g):
                sp.wait_ge(x1_ready, g + 1)
                sp.dma_start(x1_of[g], y[:, :, :]).then_inc(x1_out, 16)

            load(0)
            with sp.Fori(1, G1) as g:
                load(g)
                store(g - 1)
            store(G1 - 1)
            sp.wait_ge(x1_out, 16 * G1 + 1)

        @block.tensor
        def _(pe):
            def project_qk(g, c, n):
                for w, ps, ready, evac in ((wq, q_ps, q_ready, q_evac), (wk, k_ps, k_ready, k_evac)):
                    wait(pe, evac, n)
                    for k in range(KE):
                        last = pe.matmul(ps[:, 0:GS], w[:, k, 128 * c:128 * c + 128], xT[:, k, bass.ds(g * GS, GS)],
                                         start=(k == 0), stop=(k == KE - 1))
                    last.then_inc(ready, 1)

            def score(g, c, n):
                pe.wait_ge(q_evac, n + 1)
                pe.wait_ge(k_evac, n + 1)
                for i in range(2):
                    wait(pe, masked, 2 * n - 1 + i)
                    for b in (2 * i, 2 * i + 1):
                        last = pe.matmul(score_ps[i][0:S, 2 * S * (b % 2):2 * S * (b % 2) + 2 * S],
                                         kT[:, c % 2, S * b:S * b + S], q_blk[:, c % 2, b].rearrange("p h s -> p (h s)"),
                                         start=True, stop=True)
                    last.then_inc(scores_ready, 1)

            def values(g, c, n):
                pe.wait_ge(share_ready, n + 1)
                wait(pe, shareT_evac, n)
                for b in range(GB):
                    last = pe.transpose(share_ps[:, S * b:S * b + S], share[:, c % 2, b, :], ident[0:S, 0:S])
                last.then_inc(shareT_ready, 1)
                wait(pe, v_scaled, n)
                for k in range(KE):
                    last = pe.matmul(v_ps[:, 0:GS], wv[:, k, 128 * c:128 * c + 128], xT[:, k, bass.ds(g * GS, GS)],
                                     start=(k == 0), stop=(k == KE - 1))
                last.then_inc(v_ready, 1)

            def expand(g, c, n):
                pe.wait_ge(v_scaled, n + 1)
                if c == 0:
                    wait(pe, added, GB * g)
                for b in range(GB):
                    last = pe.matmul(delta_ps[b // 2][0:S, E * (b % 2):E * (b % 2) + E], vT[:, c % 2, S * b:S * b + S],
                                     wu[:, c, :], start=(c == 0 and b % 2 == 0), stop=(c == C1 - 1),
                                     skip_group_check=True)
                last.then_inc(delta_steps, 1)

            pe.wait_ge(qk_in, 64)
            pe.wait_ge(consts_in, 32)
            pe.wait_ge(vu_in, 32)
            run(pe, [(0, project_qk), (1, score), (4, values), (6, expand)])

        @block.scalar
        def _(act):
            def evacuate(g, c, n):
                act.wait_ge(q_ready, n + 1)
                wait(act, scores_ready, 2 * n - 2)
                for h in range(2):
                    rows = slice(64 * h, 64 * h + 64)
                    last = act.activation(q_blk[rows, c % 2, :, h, :], q_ps[rows, 0:GS].rearrange("p (b s) -> p b s", b=GB),
                                          ACT.Copy, scale=D1 ** -0.5)
                last.then_inc(q_evac, 1)
                act.wait_ge(k_ready, n + 1)
                act.activation(kT[:, c % 2, :], k_ps[:, 0:GS], ACT.Copy).then_inc(k_evac, 1)

            def exps(g, c, n):
                wait(act, diag_ready, n - 1)
                wait(act, share_ready, n - 1)
                for i in range(2):
                    act.wait_ge(max_ready, 2 * n + 1 + i)
                    for b in range(GB):
                        last = act.activation(probs[:, c % 2, i, b, :], scores[:, c % 2, i, b, :], ACT.Exp,
                                              bias=neg_max[:, c % 2, i, b:b + 1],
                                              accum_out=total[:, c % 2, i, b:b + 1])
                last.then_inc(exp_done, 1)

            def share_copy(g, c, n):
                act.wait_ge(shareT_ready, n + 1)
                wait(act, v_scaled, n - 1)
                act.activation(shareT[:, c % 2, :], share_ps[:, 0:GS], ACT.Copy, scale=1.0 / N1).then_inc(shareT_evac, 1)

            act.wait_ge(half_set, 2)
            run(act, [(0, evacuate), (2, exps), (4, share_copy)])

        @block.gpsimd
        def _(pool):
            def pick(g, c, n):
                pool.wait_ge(exp_done, n + 1)
                wait(pool, sums_ready, n - 1)
                eye = ident[0:S, 0:S].unsqueeze(1).to_broadcast([S, 2 * GB, S])
                pool.tensor_tensor(diag[:, c % 2].rearrange("s i b t -> s (i b) t"),
                                   probs[:, c % 2].rearrange("s i b t -> s (i b) t"), eye, ALU.mult).then_inc(diag_ready, 1)

            def inverse_root(g, c, n):
                if c == C1 - 1:
                    pool.wait_ge(var_ready, g + 1)
                    pool.tensor_tensor(rstd[:, :], veps[:, :], half[:, :], ALU.pow).then_inc(rstd_ready, 1)

            pool.memset(half[:, :], -0.5).then_inc(half_set, 1)
            pool.wait_ge(half_set, 1)
            pool.memset(q_blk[:, :, :, :, :], 0.0).then_inc(half_set, 1)
            pool.wait_ge(consts_in, 32)
            run(pool, [(2, pick), (7, inverse_root)])

        @block.vector
        def _(dve):
            def mask(g, c, n):
                for i in range(2):
                    dve.wait_ge(scores_ready, 2 * n + 1 + i)
                    sc = score_ps[i][0:S, 0:GS].rearrange("s (b t) -> s b t", b=GB)
                    low = below[:, :].unsqueeze(1).to_broadcast([S, GB, S])
                    dve.scalar_tensor_tensor(out=dead[:, i], in0=sc, scalar=0.0, in1=low,
                                             op0=ALU.is_equal, op1=ALU.max).then_inc(dead_found, 1)
                wait(dve, exp_done, n - 1)
                for i in range(2):
                    dve.wait_ge(dead_found, 2 * n + 1 + i)
                    sc = score_ps[i][0:S, 0:GS].rearrange("s (b t) -> s b t", b=GB)
                    dve.scalar_tensor_tensor(out=scores[:, c % 2, i], in0=dead[:, i], scalar=BELOW, in1=sc,
                                             op0=ALU.mult, op1=ALU.add).then_inc(masked, 1)
                for i in range(2):
                    dve.wait_ge(masked, 2 * n + 1 + i)
                    dve.tensor_reduce(neg_max[:, c % 2, i], scores[:, c % 2, i], AX_X, ALU.max,
                                      negate=True).then_inc(max_ready, 1)

            def shares(g, c, n):
                dve.wait_ge(diag_ready, n + 1)
                wait(dve, share_ready, n)
                dve.tensor_reduce(top[:, :, :], diag[:, c % 2], AX_X, ALU.add).then_inc(sums_ready, 1)
                dve.reciprocal(inv[:, :, :], total[:, c % 2]).then_inc(sums_ready, 1)
                wait(dve, shareT_ready, n - 1)
                dve.wait_ge(sums_ready, 2 * n + 2)
                wide = lambda t: t[:, :, :].rearrange("s i b -> s (i b)").unsqueeze(2).to_broadcast([S, 2 * GB, D1])
                dve.tensor_tensor(share[:, c % 2].rearrange("s b (h d) -> s (b h) d", h=2), wide(top), wide(inv),
                                  ALU.mult).then_inc(share_ready, 1)

            def scale_values(g, c, n):
                dve.wait_ge(shareT_evac, n + 1)
                dve.wait_ge(v_ready, n + 1)
                wait(dve, delta_steps, n - 1)
                dve.tensor_tensor(vT[:, c % 2, :], v_ps[:, 0:GS], shareT[:, c % 2, :], ALU.mult).then_inc(v_scaled, 1)

            def add_up(g, c, n):
                if c < C1 - 1:
                    return
                dve.wait_ge(delta_steps, C1 * g + C1)
                dve.wait_ge(x_in, 16 * g + 16)
                dve.wait_ge(x1_out, 16 * g + 1)
                for b in range(GB):
                    dve.scalar_tensor_tensor(out=y[:, b, :], in0=x_nat[:, b, :], scalar=2.0,
                                             in1=delta_ps[b // 2][0:S, E * (b % 2):E * (b % 2) + E],
                                             op0=ALU.mult, op1=ALU.add).then_inc(added, 1)
                for b in range(GB):
                    dve.wait_ge(added, GB * g + b + 1)
                    dve.bn_stats(stats[:, b, :], y[:, b, :]).then_inc(stats_done, 1)
                dve.wait_ge(stats_done, 2 * GB * g + GB)
                dve.memset(pause[:, :], 0.0)
                for b in range(GB):
                    dve.bn_aggr(mv[:, b, :], stats[:, b, :]).then_inc(stats_done, 1)
                dve.wait_ge(stats_done, 2 * GB * g + 2 * GB)
                dve.tensor_scalar(veps[:, :], mv[:, :, 1], EPS, None, ALU.add).then_inc(var_ready, 1)

            def normalize(g, c, n):
                if c < C1 - 1:
                    return
                dve.wait_ge(rstd_ready, g + 1)
                for b in range(GB):
                    last = dve.tensor_scalar(y[:, b, :], y[:, b, :], mv[:, b, 0:1], rstd[:, b:b + 1],
                                             ALU.subtract, ALU.mult)
                last.then_inc(x1_ready, 1)

            dve.memset(pause[:, :], 0.0).then_inc(x1_out, 1)
            dve.wait_ge(consts_in, 32)
            run(dve, [(5, scale_values), (1, mask), (3, shares), (7, add_up), (8, normalize)])



def cross_attention(nc, io, mem):
    wq, wp, oh = mem["q_w"], mem["p_w"], mem["choice"]
    with ExitStack() as ctx:
        SC = S2 + S2 % 2
        raw = lambda t: t.bitcast(F32)
        sb = lambda name, shape, dt=F32: ctx.enter_context(nc.sbuf_tensor(name, shape, dt))
        sem = lambda name: ctx.enter_context(nc.semaphore(name))
        bank = [ctx.enter_context(nc.psum_tensor(f"b_bank{i}", [128, 512], F32)) for i in range(8)]
        front_ps, stream_ps, exp_ps, o_ps, misc_ps = bank[0], bank[1:4], bank[4:6], bank[6], bank[7]

        ident = sb("b_ident", [128, 128])
        q_bias, k_bias = sb("b_q_bias", [PR, 3]), sb("b_k_bias", [PR, 3])
        v_bias = mem["v_bias"]
        wk_hi, wk_lo = (sb(f"b_wk_{n}", [128, KE, 3 * PR], F32R) for n in ("hi", "lo"))
        wv_hi, wv_lo = (sb(f"b_wv_{n}", [128, KE, E], F32R) for n in ("hi", "lo"))
        block_of = sb("b_block_of", [PR, N2])
        sum_of = sb("b_sum_of", [128, 128])
        rank = sb("b_rank", [S, X])
        router = sb("b_router", [128, KE, X])
        mask_u8 = sb("b_mask_u8", [B, S2], U8)
        mask_f = mem["probs"][0:B, 0, 0:SC]
        x1_nat, x1_res = mem["x1_nat"], mem["x1_res"][:, 0, :]
        c_T = mem["c_T"]
        c_hi, c_lo = (sb(f"b_c_{n}", [128, 2, KE, SC], F32R) for n in ("hi", "lo"))
        x1_T = mem["x1_T"]
        q_T = mem["q_T"]
        qT_hi, qT_lo = (sb(f"b_qT_{n}", [PR, 3, S], F32R) for n in ("hi", "lo"))
        q_hi, q_lo = (sb(f"b_q_{n}", [PR + 2, 2, N2 * S], F32R) for n in ("hi", "lo"))
        k_hi, k_lo = (sb(f"b_k_{n}", [PR + 2, 2, 3, SC], F32R) for n in ("hi", "lo"))
        v = mem["v"].rearrange("c a (i h d) -> c a i h d", i=3, h=N2)
        neg_max = sb("b_neg_max", [125, len(TILES)])
        max_hi, max_lo = (sb(f"b_max_{n}", [8, 2, 125], F32R) for n in ("hi", "lo"))
        probs = mem["probs"]
        o_raw, inv, o_T = (mem[n][:, 0, :] for n in ("o_raw", "inv", "o_T"))
        y = sb("b_y", [S, 2, E])
        pause = sb("b_pause", [1, 1])
        stats, mv = sb("b_stats", [S, 6]), sb("b_mv", [S, 2, 2])
        veps, rstd, half = sb("b_veps", [S, 1]), sb("b_rstd", [S, 1]), sb("b_half", [S, 1])
        x2_T = mem["x2_T"]
        best, value, first = sb("b_best", [S, 1]), sb("b_value", [S, X]), sb("b_first", [S, 1])

        zeros = mem["zeros"][:, 0, :]

        zeros_out = sem("b_zeros_out")
        consts_in, mask_read, mask_made, mask_out, ones_set = (sem(n) for n in (
            "b_consts_in", "b_mask_read", "b_mask_made", "b_mask_out", "b_ones_set"))
        x1_in, mask_in, max_in = ([sem(f"b_{n}{p}") for p in range(2)] for n in ("x1_in", "mask_in", "max_in"))
        ctx_in = sem("b_ctx_in")
        res_in, x2_out = sem("b_res_in"), [sem(f"b_x2_out{p}") for p in range(2)]
        x1T_ready, x1T_evac, q_ready, q_evac, q_split, blk_ready = (sem(n) for n in (
            "b_x1T_ready", "b_x1T_evac", "b_q_ready", "b_q_evac", "b_q_split", "b_blk_ready"))
        w_hi_made, w_split, c_hi_made, c_split, k_hi_made, max_hi_made = (sem(n) for n in (
            "b_w_hi_made", "b_w_split", "b_c_hi_made", "b_c_split", "b_k_hi_made", "b_max_hi_made"))
        k_ready, k_evac, v_ready, v_evac, score_ready, max_done = (sem(n) for n in (
            "b_k_ready", "b_k_evac", "b_v_ready", "b_v_evac", "b_score_ready", "b_max_done"))
        maxT_ready, maxT_evac, shifted_ready, exp_done = (sem(n) for n in (
            "b_maxT_ready", "b_maxT_evac", "b_shifted_ready", "b_exp_done"))
        o_ready, o_evac, sums_ready, inv_ready, o_normed, y_ready = (sem(n) for n in (
            "b_o_ready", "b_o_evac", "b_sums_ready", "b_inv_ready", "b_o_normed", "b_y_ready"))
        added, stats_done, var_ready, rstd_ready, x2_ready = (sem(n) for n in (
            "b_added", "b_stats_done", "b_var_ready", "b_rstd_ready", "b_x2_ready"))
        x2T_ready, x2T_evac, logits_ready, picked = (sem(n) for n in (
            "b_x2T_ready", "b_x2T_evac", "b_logits_ready", "b_picked"))

        def run(eng, position):
            for b in range(4):
                position(b, b % 2)
            with eng.Fori(2, B // 2 - 1) as pair:
                for p in range(2):
                    position(2 * pair + p, p)
            for b in range(B - 2, B + 2):
                position(b, b % 2)

        def live(b):
            return not isinstance(b, int) or 0 <= b < B

        def slot(b, p):
            return b - p + 2

        ROWS = ((v[:, :, :, :, :], 0.0), (v[:, :, :, :, D2:D2 + 1], 1.0), (raw(k_hi[PR:PR + 2, :, :, :]), 1.0),
                (raw(k_lo[PR:PR + 2, :, :, :]), 0.0), (raw(q_hi[PR:PR + 2, :, :]), 1.0),
                (raw(q_lo[PR:PR + 2, :, :]), 0.0), (half[:, :], -0.5), (zeros, 0.0))
        passes = lambda hi_a, lo_a, hi_b, lo_b: ((hi_a, hi_b), (lo_a, hi_b), (hi_a, lo_b))

        block = ctx.enter_context(nc.Block())

        @block.sync
        def _(sp):
            for dst, src in ((ident[:, :], io["ident"]), (q_bias[:, :], io["q_b"]), (k_bias[:, :], io["k_b"]),
                             (v_bias[0:CTX[0][1], 0, :], io["v_b"].partition_broadcast(CTX[0][1])), (block_of[:, :], io["block_of"]),
                             (sum_of[:, :], io["sum_of"]), (rank[:, :], io["rank"]), (router[:, :, :], io["router"]),
                             (mem["k_w"], io["k_w"]), (mem["v_w"], io["v_w"]), (wq, io["q_w"]), (wp, io["p_w"])):
                sp.dma_start(dst, src).then_inc(consts_in, 16)
            sp.dma_start(mask_u8[:, :], io["mask"]).then_inc(mask_read, 16)
            sp.wait_ge(mask_made, 2)
            sp.dma_start(io["mask_f"], mask_f[:, :]).then_inc(mask_out, 16)
            sp.wait_ge(mask_out, 16)
            sp.wait_ge(ones_set, len(ROWS))

            def load(b, p):
                if not live(b):
                    return
                wait(sp, x1T_ready, b - 1)
                sp.dma_start(x1_nat[:, p, :], io["x1"][bass.ds(b * S, S), :]).then_inc(x1_in[p], 16)
                wait(sp, shifted_ready, 12 * (b - 1))
                for part in range(3):
                    sp.dma_start(raw(k_hi[MASK_ROW:MASK_ROW + 1, p, part, :]), io["mask_f"][bass.ds(b, 1), :]).then_inc(mask_in[p], 16)

            def load_context(b):
                if live(b):
                    wait(sp, c_split, b)
                    sp.dma_start(c_T, io["ctxT"][bass.ds(b, 1)].rearrange("a p k s -> (a p) k s")).then_inc(ctx_in, 16)

            def fetch(b):
                sp.dma_start(mem["gate_up"][:, bass.ds(b * FF, 2 * FF)], io["gate_up"][bass.ds(b * 64, 128), :])\
                  .then_inc(mem["gate_up_in"], 16)

            def position(b, p):
                if live(b) and p == 0 and not (isinstance(b, int) and b == 2 * (X * KE - 1)):
                    fetch(b)
                if live(b - 1):
                    wait(sp, added, b - 1)
                    sp.dma_start(x1_res[:, :], io["x1"][bass.ds((b - 1) * S, S), :]).then_inc(res_in, 16)
                if live(b - 2):
                    sp.wait_ge(x2_ready, b - 1)
                    sp.dma_start(io["x2"][bass.ds((b - 2) * S, S), :], y[:, p, :]).then_inc(x2_out[p], 16)
                load(b + 1, 1 - p)
                if live(b):
                    for i, (q, m) in enumerate(((q_hi, max_hi), (q_lo, max_lo))):
                        sp.wait_ge((max_hi_made, maxT_evac)[i], 2 * b + 2)
                        sp.dma_start(raw(q[MAX_ROW:MAX_ROW + 1, p, 0:1000]).rearrange("o (t w) -> o t w", t=8),
                                     raw(m[0:8, 0, 0:125])).then_inc(max_in[p], 16)
                        sp.dma_start(raw(q[MAX_ROW:MAX_ROW + 1, p, 1000:1600]).rearrange("o (t w) -> o t w", t=5),
                                     raw(m[0:5, 1, 0:120])).then_inc(max_in[p], 16)
                load_context(b + 2)

            load(0, 0)
            load_context(0)
            load_context(1)
            sp.dma_start(io["sorted"].rearrange("(p r) e -> p r e", p=128),
                         zeros[:, :].unsqueeze(1).to_broadcast([128, NT * SLOTS // 128, E])).then_inc(zeros_out, 16)
            run(sp, position)
            sp.wait_ge(zeros_out, 16)
            for p in range(2):
                sp.wait_ge(x2_out[p], 16 * (B // 2))

        @block.gpsimd
        def _(pool):
            for n, (rows, value) in enumerate(ROWS):
                pool.memset(rows, value).then_inc(ones_set, 1)
                pool.wait_ge(ones_set, n + 1)
            pool.wait_ge(consts_in, 16 * 12)

            def position(b, p):
                if live(b):
                    wait(pool, shifted_ready, 12 * (b - 1))
                for i, (blk, q) in enumerate(((q_hi, qT_hi), (q_lo, qT_lo))):
                    if live(b):
                        pool.wait_ge(q_split, 2 * b + i + 1)
                        for part, (h0, n) in enumerate(PARTS):
                            cols = blk[0:PR, p, S * h0:S * (h0 + n)].rearrange("r (h s) -> r h s", h=n)
                            pool.tensor_tensor(cols, raw(q[:, part, :]).unsqueeze(1).to_broadcast([PR, n, S]),
                                               block_of[:, h0:h0 + n].unsqueeze(2).to_broadcast([PR, n, S]),
                                               ALU.mult).then_inc(blk_ready, 1)
                    if i == 0 and live(b - 2):
                        pool.wait_ge(var_ready, b - 1)
                        pool.tensor_tensor(rstd[:, :], veps[:, :], half[:, :], ALU.pow).then_inc(rstd_ready, 1)

            run(pool, position)

        @block.tensor
        def _(pe):
            pe.wait_ge(consts_in, 16 * 12)
            pe.wait_ge(ones_set, len(ROWS))
            pe.wait_ge(w_split, 2)

            def front(b, p):
                pe.wait_ge(x1_in[p], 8 * slot(b, p))
                wait(pe, q_evac, b)
                for k in range(KE):
                    last = pe.transpose(front_ps[:, S * k:S * k + S], x1_nat[:, p, 128 * k:128 * k + 128], ident[0:S, 0:S])
                last.then_inc(x1T_ready, 1)
                pe.wait_ge(c_split, b + 1)
                wait(pe, max_done, 13 * b)
                for part in range(3):
                    for i, (w, c) in enumerate(passes(wk_hi, wk_lo, c_hi, c_lo)):
                        for k in range(KE):
                            last = pe.matmul(stream_ps[part][0:PR, 0:SC], w[:, k, PR * part:PR * part + PR], c[:, p, k, :],
                                             start=(i == k == 0), stop=(i == 2 and k == KE - 1))
                    last.then_inc(k_ready, 1)
                pe.wait_ge(x1T_evac, b + 1)
                for part in range(3):
                    for k in range(KE):
                        last = pe.matmul(front_ps[0:PR, S * (2 + part):S * (3 + part)], wq[:, k, PR * part:PR * part + PR],
                                         x1_T[:, k, :], start=(k == 0), stop=(k == KE - 1))
                last.then_inc(q_ready, 1)

            def values(b, p):
                for i, (c0, n) in enumerate(CTX):
                    pe.wait_ge(k_evac, 3 * b + i + 1)
                    for j, (c, w) in enumerate(passes(c_hi, c_lo, wv_hi, wv_lo)):
                        for k in range(KE):
                            last = pe.matmul(stream_ps[i][0:n, 0:E], c[:, p, k, c0:c0 + n], w[:, k, :],
                                             start=(j == k == 0), stop=(j == 2 and k == KE - 1))
                    last.then_inc(v_ready, 1)

            def rows(b, p, t):
                part, col, w = TILES[t]
                if t == 0:
                    pe.wait_ge(k_evac, 3 * b + 3)
                    pe.wait_ge(mask_in[p], 24 * slot(b, p))
                pe.wait_ge(blk_ready, 6 * b + part + 1)
                if t < 3:
                    pe.wait_ge(v_evac, 3 * b + t + 1)
                else:
                    pe.wait_ge(max_done, 13 * b + t - 2)
                pe.matmul(stream_ps[t % 3][0:w, 0:SC], q_hi[0:MASK_ROW + 1, p, col:col + w],
                          k_hi[0:MASK_ROW + 1, p, part, :], start=True, stop=True).then_inc(score_ready, 1)

            def maxima(b, p):
                pe.wait_ge(max_done, 13 * b + 13)
                wait(pe, o_evac, b)
                pe.transpose(o_ps[0:8, 0:125], neg_max[0:125, 0:8], ident[0:125, 0:125])
                pe.transpose(o_ps[0:5, 128:248], neg_max[0:120, 8:13], ident[0:120, 0:120]).then_inc(maxT_ready, 1)

            def shifted(b, p, r, j):
                part, col, w = RUNS[r]
                c0, n = CTX[j]
                if r == j == 0:
                    pe.wait_ge(max_in[p], 32 * slot(b, p))
                    pe.wait_ge(blk_ready, 6 * b + 6)
                e = 3 * r + j
                wait(pe, exp_done, 12 * b + e - 1)
                for i, (k, q) in enumerate(passes(k_hi, k_lo, q_hi, q_lo)):
                    last = pe.matmul(exp_ps[e % 2][0:n, 0:w], k[0:MAX_ROW + 1, p, part, c0:c0 + n],
                                     q[0:MAX_ROW + 1, p, col:col + w], start=(i == 0), stop=(i == 2))
                last.then_inc(shifted_ready, 1)

            def attend(b, p, quad):
                pe.wait_ge(exp_done, 12 * b + 3 * quad + 3)
                if quad == 0:
                    pe.wait_ge(v_evac, 3 * b + 3)
                    pe.wait_ge(maxT_evac, 2 * b + 2)
                for j, (c0, n) in enumerate(CTX):
                    for q in range(4):
                        h = 4 * quad + q
                        last = pe.matmul(o_ps[32 * q:32 * q + 32, S * quad:S * quad + S], v[0:n, p, j, h, :],
                                         probs[0:n, j, S * h:S * h + S], start=(j == 0), stop=(j == 2),
                                         tile_position=(0, 32 * q))
                if quad == 3:
                    last.then_inc(o_ready, 1)

            def sums(b):
                pe.wait_ge(o_evac, b + 1)
                wait(pe, picked, 4 * (b - 1) + 2)
                pe.matmul(misc_ps[:, 0:4 * S], sum_of[:, :], o_raw, start=True, stop=True).then_inc(sums_ready, 1)

            def project(b):
                pe.wait_ge(o_normed, b + 1)
                for quad in range(4):
                    last = pe.matmul(misc_ps[0:S, 0:E], o_T[:, S * quad:S * quad + S], wp[:, quad, :],
                                     start=(quad == 0), stop=(quad == 3))
                last.then_inc(y_ready, 1)

            def turn(b, p):
                pe.wait_ge(x2_ready, b + 1)
                for k in range(KE):
                    last = pe.transpose(misc_ps[:, S * k:S * k + S], y[:, p, 128 * k:128 * k + 128], ident[0:S, 0:S])
                last.then_inc(x2T_ready, 1)

            def route(b):
                pe.wait_ge(x2T_evac, b + 1)
                for k in range(KE):
                    last = pe.matmul(misc_ps[0:S, 0:X], x2_T[:, k, :], router[:, k, :], start=(k == 0), stop=(k == KE - 1))
                last.then_inc(logits_ready, 1)

            def position(b, p):
                now, then, old = live(b), live(b - 1), live(b - 2)
                if now:
                    front(b, p)
                if old:
                    project(b - 2)
                if now:
                    values(b, p)
                for r in range(4):
                    for j in range(3):
                        if then:
                            shifted(b - 1, 1 - p, r, j)
                        if now and 3 * r + j >= 1:
                            rows(b, p, 3 * r + j - 1)
                    if then and r >= 1:
                        attend(b - 1, 1 - p, r - 1)
                    if old and r == 1:
                        turn(b - 2, p)
                    if old and r == 2:
                        route(b - 2)
                if now:
                    rows(b, p, 11)
                    rows(b, p, 12)
                if then:
                    attend(b - 1, 1 - p, 3)
                if now:
                    maxima(b, p)
                if then:
                    sums(b - 1)

            run(pe, position)

        @block.scalar
        def _(act):
            def exps(b, r):
                part, col, w = RUNS[r]
                for j, (c0, n) in enumerate(CTX):
                    e = 3 * r + j
                    act.wait_ge(shifted_ready, 12 * b + e + 1)
                    act.activation(probs[0:n, j, col:col + w], exp_ps[e % 2][0:n, 0:w], ACT.Exp).then_inc(exp_done, 1)

            def position(b, p):
                now, then, old = live(b), live(b - 1), live(b - 2)
                if now:
                    act.wait_ge(x1T_ready, b + 1)
                    wait(act, q_ready, b)
                    act.activation(x1_T[:, :, :], front_ps[:, 0:KE * S].rearrange("p (k s) -> p k s", k=KE),
                                   ACT.Copy).then_inc(x1T_evac, 1)
                    wait(act, shifted_ready, 12 * (b - 1))
                    for part in range(3):
                        act.wait_ge(k_ready, 3 * b + part + 1)
                        act.activation(k_hi[0:PR, p, part, :], stream_ps[part][0:PR, 0:SC], ACT.Identity,
                                       bias=k_bias[:, part:part + 1]).then_inc(k_hi_made, 1)
                if then:
                    wait(act, o_ready, b - 1)
                    exps(b - 1, 0)
                    exps(b - 1, 1)
                context_hi(b + 1, 1 - p)
                if old:
                    act.wait_ge(x2T_ready, b - 1)
                    wait(act, logits_ready, b - 2)
                    act.activation(x2_T[:, :, :], misc_ps[:, 0:KE * S].rearrange("p (k s) -> p k s", k=KE),
                                   ACT.Copy).then_inc(x2T_evac, 1)
                if then:
                    exps(b - 1, 2)
                    exps(b - 1, 3)
                    act.wait_ge(o_ready, b)
                    wait(act, o_normed, b - 1)
                    act.activation(o_raw, o_ps[:, 0:4 * S], ACT.Copy).then_inc(o_evac, 1)
                if now:
                    act.wait_ge(maxT_ready, b + 1)
                    if live(b - 1):
                        act.wait_ge(max_in[1 - p], 32 * slot(b - 1, 1 - p))
                    act.activation(max_hi[0:8, 0, 0:125], o_ps[0:8, 0:125], ACT.Copy).then_inc(max_hi_made, 1)
                    act.activation(max_hi[0:5, 1, 0:120], o_ps[0:5, 128:248], ACT.Copy).then_inc(max_hi_made, 1)

            def context_hi(b, p):
                if live(b):
                    act.wait_ge(ctx_in, 16 * b + 16)
                    wait(act, v_ready, 3 * (b - 1))
                    act.activation(c_hi[:, p], c_T, ACT.Copy).then_inc(c_hi_made, 1)

            act.wait_ge(consts_in, 16 * 12)
            act.activation(wk_hi[:, :, :], mem["k_w"], ACT.Copy).then_inc(w_hi_made, 1)
            act.activation(wv_hi[:, :, :], mem["v_w"], ACT.Copy).then_inc(w_hi_made, 1)
            context_hi(0, 0)
            run(act, position)

        @block.vector
        def _(dve):
            dve.wait_ge(mask_read, 16)
            dve.memset(mask_f[:, S2:SC], MASKED).then_inc(mask_made, 1)
            dve.tensor_scalar(mask_f[:, 0:S2], mask_u8[:, :], MASKED, None, ALU.mult).then_inc(mask_made, 1)
            dve.wait_ge(consts_in, 16 * 12)
            dve.wait_ge(ones_set, len(ROWS))
            for i, (lo, hi, w) in enumerate(((wk_lo, wk_hi, mem["k_w"]), (wv_lo, wv_hi, mem["v_w"]))):
                dve.wait_ge(w_hi_made, i + 1)
                dve.tensor_tensor(lo[:, :, :], w, raw(hi[:, :, :]), ALU.subtract).then_inc(w_split, 1)

            def context_lo(b, p):
                if live(b):
                    dve.wait_ge(c_hi_made, b + 1)
                    wait(dve, v_ready, 3 * (b - 1))
                    dve.tensor_tensor(c_lo[:, p], c_T, raw(c_hi[:, p]), ALU.subtract).then_inc(c_split, 1)

            def keys_lo(b, p):
                wait(dve, shifted_ready, 12 * (b - 1))
                for part in range(3):
                    dve.wait_ge(k_hi_made, 3 * b + part + 1)
                    dve.scalar_tensor_tensor(out=k_lo[0:PR, p, part, :], in0=stream_ps[part][0:PR, 0:SC],
                                             scalar=k_bias[:, part:part + 1], in1=raw(k_hi[0:PR, p, part, :]),
                                             op0=ALU.add, op1=ALU.subtract).then_inc(k_evac, 1)

            def queries(b):
                dve.wait_ge(q_ready, b + 1)
                wait(dve, q_split, 2 * b)
                dve.tensor_tensor(q_T, front_ps[0:PR, 2 * S:5 * S].rearrange("r (t s) -> r t s", t=3),
                                  q_bias[:, :].unsqueeze(2).to_broadcast([PR, 3, S]), ALU.add).then_inc(q_evac, 1)
                dve.wait_ge(q_evac, b + 1)
                wait(dve, blk_ready, 6 * b)
                dve.tensor_copy(qT_hi[:, :, :], q_T).then_inc(q_split, 1)
                dve.wait_ge(q_split, 2 * b + 1)
                dve.tensor_tensor(qT_lo[:, :, :], q_T, raw(qT_hi[:, :, :]), ALU.subtract).then_inc(q_split, 1)

            def maxima_lo(b, p):
                dve.wait_ge(max_hi_made, 2 * b + 2)
                if live(b - 1):
                    dve.wait_ge(max_in[1 - p], 32 * slot(b - 1, 1 - p))
                dve.tensor_tensor(max_lo[0:5, 1, 0:120], o_ps[0:5, 128:248], raw(max_hi[0:5, 1, 0:120]),
                                  ALU.subtract).then_inc(maxT_evac, 1)
                dve.tensor_tensor(max_lo[0:8, 0, 0:125], o_ps[0:8, 0:125], raw(max_hi[0:8, 0, 0:125]),
                                  ALU.subtract).then_inc(maxT_evac, 1)

            def normalize(b, p):
                dve.wait_ge(rstd_ready, b + 1)
                dve.tensor_scalar(y[:, p, :], y[:, p, :], mv[:, p, 0:1], rstd[:, 0:1],
                                  ALU.subtract, ALU.mult).then_inc(x2_ready, 1)

            def pick(b):
                dve.wait_ge(logits_ready, b + 1)
                logits = misc_ps[0:S, 0:X]
                wait(dve, picked, 4 * b)
                dve.tensor_reduce(best[:, :], logits, AX_X, ALU.max).then_inc(picked, 1)
                dve.wait_ge(picked, 4 * b + 1)
                dve.scalar_tensor_tensor(out=value[:, :], in0=logits, scalar=best[:, 0:1], in1=rank[:, :],
                                         op0=ALU.is_equal, op1=ALU.add).then_inc(picked, 1)
                dve.wait_ge(picked, 4 * b + 2)
                dve.tensor_reduce(first[:, :], value[:, :], AX_X, ALU.max).then_inc(picked, 1)
                dve.wait_ge(picked, 4 * b + 3)
                dve.tensor_scalar(oh[:, bass.ds(b, 1), :], value[:, :].unsqueeze(1), first[:, 0:1], None,
                                  ALU.is_equal).then_inc(picked, 1)

            def biased(b, p):
                wait(dve, o_ready, b - 1)
                for i, (c0, n) in enumerate(CTX):
                    dve.wait_ge(v_ready, 3 * b + i + 1)
                    heads = lambda t: t.rearrange("c (h d) -> c h d", h=N2)
                    dve.tensor_tensor(v[0:n, p, i, :, 0:D2], heads(stream_ps[i][0:n, 0:E]), heads(v_bias[0:n, 0, :]),
                                      ALU.add).then_inc(v_evac, 1)

            def maxima(b, t0, t1):
                if t0 == 0:
                    wait(dve, maxT_ready, b)
                for t in range(t0, t1):
                    w = TILES[t][2]
                    dve.wait_ge(score_ready, 13 * b + t + 1)
                    dve.tensor_reduce(neg_max[0:w, t:t + 1], stream_ps[t % 3][0:w, 0:S2], AX_X, ALU.max,
                                      negate=True).then_inc(max_done, 1)

            def divide(b):
                dve.wait_ge(sums_ready, b + 1)
                wait(dve, o_normed, b)
                dve.reciprocal(inv, misc_ps[:, 0:4 * S]).then_inc(inv_ready, 1)
                dve.wait_ge(inv_ready, b + 1)
                wait(dve, y_ready, b)
                dve.tensor_tensor(o_T, o_raw, inv, ALU.mult).then_inc(o_normed, 1)

            def add_up(b, p):
                dve.wait_ge(y_ready, b + 1)
                dve.wait_ge(res_in, 16 * (b + 1))
                wait(dve, x2T_ready, b - 1)
                if live(b - 2):
                    dve.wait_ge(x2_out[p], 8 * slot(b - 2, p))
                dve.tensor_tensor(y[:, p, :], misc_ps[0:S, 0:E], x1_res[:, :], ALU.add).then_inc(added, 1)
                dve.wait_ge(added, b + 1)
                dve.bn_stats(stats[:, :], y[:, p, :]).then_inc(stats_done, 1)
                dve.wait_ge(stats_done, 2 * b + 1)
                wait(dve, x2_ready, b - 1)
                dve.memset(pause[:, :], 0.0)
                dve.bn_aggr(mv[:, p, :], stats[:, :]).then_inc(stats_done, 1)
                dve.wait_ge(stats_done, 2 * b + 2)
                dve.tensor_scalar(veps[:, :], mv[:, p, 1:2], EPS, None, ALU.add).then_inc(var_ready, 1)

            def position(b, p):
                now, then, old = live(b), live(b - 1), live(b - 2)
                if now:
                    keys_lo(b, p)
                    queries(b)
                if old:
                    add_up(b - 2, p)
                if now:
                    biased(b, p)
                    maxima(b, 0, 2)
                if old:
                    normalize(b - 2, p)
                if now:
                    maxima(b, 2, 6)
                context_lo(b + 1, 1 - p)
                if now:
                    maxima(b, 6, 9)
                if old:
                    pick(b - 2)
                if now:
                    maxima(b, 9, 13)
                    maxima_lo(b, p)
                if then:
                    divide(b - 1)

            context_lo(0, 0)
            run(dve, position)


def experts(nc, io, mem):
    gu, dn, oh, gu_in = mem["gate_up"], mem["down"], mem["choice"], mem["gate_up_in"]
    with ExitStack() as ctx:
        sb = lambda name, shape, dt=F32: ctx.enter_context(nc.sbuf_tensor(name, shape, dt))
        sem = lambda name: ctx.enter_context(nc.semaphore(name))
        bank = [ctx.enter_context(nc.psum_tensor(f"c_bank{i}", [128, 512], F32)) for i in range(8)]
        gate_ps, up_ps, hT_ps, y_ps, xT_ps = bank[0:2], bank[2:4], bank[4:6], bank[6], bank[7]
        before_ps, count_ps = bank[0], bank[1]

        ident = sb("c_ident", [128, 128])
        earlier, ones = sb("c_earlier", [S, S]), sb("c_ones", [S, S])
        full, tile_no = sb("c_full", [S, CT]), sb("c_tile_no", [1, NT])
        count = sb("c_count", [S, X, B])
        upto = sb("c_upto", [S, 2, X, B])
        over = sb("c_over", [S, X, CT])
        tiles_of = sb("c_tiles_of", [S, X])
        ends = sb("c_ends", [S, 2, X])
        start = sb("c_start", [S, X])
        passed = sb("c_passed", [1, NT, X])
        expert_f, expert_of = sb("c_expert_f", [1, NT]), sb("c_expert_of", [1, NT], I32)
        place = sb("c_place", [S, B, X])
        slot_f, slot_of = sb("c_slot_f", [S, B]), sb("c_slot_of", [S, B], U32)
        x2 = sb("c_x2", [S, B, E])
        x_tile = sb("c_x_tile", [SLOTS, 2, E])
        x_T = sb("c_x_T", [128, 2, KE, SLOTS])
        gate = sb("c_gate", [SLOTS, 2, QF])
        hidden = sb("c_hidden", [SLOTS, 2, FF])
        h_T = sb("c_h_T", [128, FC, SLOTS])
        y_tile = sb("c_y_tile", [SLOTS, 2, E])
        answer = sb("c_answer", [S, 2, GB, E])
        stats, mv = sb("c_stats", [S, GB, 6]), sb("c_mv", [S, 2, GB, 2])
        veps, rstd, half = sb("c_veps", [S, GB]), sb("c_rstd", [S, 2, GB]), sb("c_half", [S, GB])

        consts_in, x2_in, dn_in, half_set = (sem(n) for n in ("c_consts_in", "c_x2_in", "c_dn_in", "c_half_set"))
        counted, math, slots_ready, experts_ready = (sem(n) for n in ("c_counted", "c_math", "c_slots_ready", "c_experts_ready"))
        scattered = sem("c_scattered")
        tile_in, tile_out, gather_in, out_out = ([sem(f"c_{n}{p}") for p in range(2)] for n in ("tile_in", "tile_out", "gather_in", "out_out"))
        xT_ready, xT_evac, gate_ready, up_ready, silu_done, gated = (sem(n) for n in (
            "c_xT_ready", "c_xT_evac", "c_gate_ready", "c_up_ready", "c_silu_done", "c_gated"))
        hT_ready, hT_evac_a, hT_evac_b, y_ready, y_evac = (sem(n) for n in (
            "c_hT_ready", "c_hT_evac_a", "c_hT_evac_b", "c_y_ready", "c_y_evac"))
        added, stats_done, var_ready, rstd_ready, out_ready = (sem(n) for n in (
            "c_added", "c_stats_done", "c_var_ready", "c_rstd_ready", "c_out_ready"))

        def run(eng, position):
            for j in range(4):
                position(j, j % 2)
            with eng.Fori(2, NT // 2 - 1) as pair:
                for p in range(2):
                    position(2 * pair + p, p)
            for j in range(NT - 2, NT + 1):
                position(j, j % 2)

        def live(j):
            return not isinstance(j, int) or 0 <= j < NT

        block = ctx.enter_context(nc.Block())

        @block.sync
        def _(sp):
            for dst, src in ((earlier[:, :], io["earlier"]), (ones[:, :], io["ones"]), (full[:, :], io["full"]),
                             (tile_no[:, :], io["tile_no"]), (ident[:, :], io["ident"])):
                sp.dma_start(dst, src).then_inc(consts_in, 16)
            sp.dma_start(x2[:, :, :], io["x2"].rearrange("(b s) e -> s b e", s=S)).then_inc(x2_in, 16)
            gu_last = gu[:, X - 1, KE - 1, :]
            sp.dma_start(gu_last, io["gate_up"][(X * KE - 1) * 128:, :]).then_inc(gu_in, 16)
            for x in range(X):
                sp.dma_start(dn[:, x], io["down"][x]).then_inc(dn_in, 16)

            def load(j, p):
                if live(j):
                    wait(sp, xT_ready, j - 1)
                    sp.dma_start(x_tile[:, p, :], io["sorted"][bass.ds(j * SLOTS, SLOTS), :]).then_inc(tile_in[p], 16)

            def position(j, p):
                load(j + 2, p)
                if live(j - 1):
                    sp.wait_ge(y_evac, j)
                    sp.dma_start(io["answers"][bass.ds((j - 1) * SLOTS, SLOTS), :], y_tile[:, 1 - p, :])\
                      .then_inc(tile_out[1 - p], 16)

            sp.wait_ge(scattered, 16 * B)
            for j in range(2):
                load(j, j)
            run(sp, position)
            for g in range(G1):
                sp.wait_ge(out_ready, g + 1)
                sp.dma_start(io["out"][GB * g:GB * g + GB].rearrange("b s e -> s b e"), answer[:, g % 2])\
                  .then_inc(out_out[g % 2], 16)
            for p in range(2):
                sp.wait_ge(out_out[p], 16 * (G1 // 2))

        @block.gpsimd
        def _(pool):
            pool.memset(half[:, :], -0.5).then_inc(half_set, 1)
            pool.wait_ge(x2_in, 16)
            pool.wait_ge(slots_ready, 1)
            for b in range(B):
                pool.indirect_dma_start(out=io["sorted"], out_offset=bass.IndirectOffsetOnAxis(ap=slot_of[:, b:b + 1], axis=0),
                                        in_=x2[:, b, :], in_offset=None).then_inc(scattered, 16)
            for p in range(2):
                pool.wait_ge(tile_out[p], 16 * (NT // 2))

            def gather(g):
                if g >= 2:
                    pool.wait_ge(out_out[g % 2], 16 * (g // 2))
                for b in range(GB):
                    n = GB * g + b
                    pool.indirect_dma_start(out=answer[:, g % 2, b, :], out_offset=None, in_=io["answers"],
                                            in_offset=bass.IndirectOffsetOnAxis(ap=slot_of[:, n:n + 1], axis=0))\
                        .then_inc(gather_in[g % 2], 16)

            pool.wait_ge(half_set, 1)
            gather(0)
            for g in range(G1):
                if g + 1 < G1:
                    gather(g + 1)
                pool.wait_ge(var_ready, g + 1)
                pool.tensor_tensor(rstd[:, g % 2], veps[:, :], half[:, :], ALU.pow).then_inc(rstd_ready, 1)

        @block.tensor
        def _(pe):
            pe.wait_ge(consts_in, 16 * 5)
            flat = oh[:, :, :].rearrange("s b x -> s (b x)")
            pe.matmul(before_ps[0:S, 0:B * X], earlier[:, :], flat, start=True, stop=True).then_inc(counted, 1)
            pe.matmul(count_ps[0:S, 0:B * X], ones[:, :], flat, start=True, stop=True).then_inc(counted, 1)

            def expert(j):
                return pe.value_load(expert_of[0:1, bass.ds(j, 1)], min_val=0, max_val=X - 1)

            def turn(j, p):
                pe.wait_ge(tile_in[p], 8 * (j - p + 2))
                wait(pe, xT_evac, j)
                for k in range(KE):
                    last = pe.transpose(xT_ps[:, SLOTS * k:SLOTS * k + SLOTS], x_tile[:, p, 128 * k:128 * k + 128], ident[:, :])
                last.then_inc(xT_ready, 1)

            def gate_up(j, p):
                x = expert(j)
                pe.wait_ge(xT_evac, j + 1)
                for h in range(2):
                    for ps, col, ready, freed in ((gate_ps, 0, gate_ready, silu_done), (up_ps, FF, up_ready, gated)):
                        wait(pe, freed, 2 * (j - 1) + h + 1)
                        for k in range(KE):
                            cols = slice(col + QF * h, col + QF * h + QF)
                            last = pe.matmul(ps[h][:, 0:QF], x_T[:, p, k, :],
                                             gu[:, bass.ds(x, 1), k, cols].rearrange("p a f -> p (a f)"),
                                             start=(k == 0), stop=(k == KE - 1))
                        last.then_inc(ready, 1)

            def turn_hidden(j, p):
                pe.wait_ge(gated, 2 * j + 2)
                wait(pe, hT_evac_a, j)
                wait(pe, hT_evac_b, 2 * j)
                for c in range(FC):
                    n = min(128, FF - 128 * c)
                    last = pe.transpose(hT_ps[c // 4][0:n, SLOTS * (c % 4):SLOTS * (c % 4) + SLOTS],
                                        hidden[:, p, 128 * c:128 * c + n], ident[:, :])
                last.then_inc(hT_ready, 1)

            def down(j, p):
                x = expert(j)
                pe.wait_ge(hT_evac_a, j + 1)
                pe.wait_ge(hT_evac_b, 2 * j + 2)
                wait(pe, y_evac, j)
                for c in range(FC):
                    n = min(128, FF - 128 * c)
                    last = pe.matmul(y_ps[:, 0:E], h_T[0:n, c, :], dn[0:n, bass.ds(x, 1), c, :].rearrange("p a e -> p (a e)"),
                                     start=(c == 0), stop=(c == FC - 1))
                last.then_inc(y_ready, 1)

            def position(j, p):
                if live(j - 1):
                    turn_hidden(j - 1, 1 - p)
                if live(j):
                    gate_up(j, p)
                if live(j - 1):
                    down(j - 1, 1 - p)
                if live(j + 1):
                    turn(j + 1, 1 - p)

            turn(0, 0)
            pe.wait_ge(experts_ready, 1)
            pe.wait_ge(gu_in, 16 * X * KE)
            pe.wait_ge(dn_in, 16 * X)
            run(pe, position)

        @block.scalar
        def _(act):
            def position(j, p):
                if live(j - 1):
                    act.wait_ge(hT_ready, j)
                    wait(act, y_ready, j - 1)
                    act.activation(h_T[:, 4, :], hT_ps[1][:, 0:SLOTS], ACT.Copy).then_inc(hT_evac_b, 1)
                    act.activation(h_T[0:FF - 640, 5, :], hT_ps[1][0:FF - 640, SLOTS:2 * SLOTS], ACT.Copy).then_inc(hT_evac_b, 1)
                if live(j):
                    for h in range(2):
                        act.wait_ge(gate_ready, 2 * j + h + 1)
                        wait(act, gated, 2 * (j - 1) + h + 1)
                        act.activation(gate[:, h, :], gate_ps[h][:, 0:QF], ACT.Silu).then_inc(silu_done, 1)
                if live(j - 1):
                    act.wait_ge(y_ready, j)
                    if live(j - 3):
                        act.wait_ge(tile_out[1 - p], 8 * (j - 3 - (1 - p) + 2))
                    act.activation(y_tile[:, 1 - p, :], y_ps[:, 0:E], ACT.Copy).then_inc(y_evac, 1)

            run(act, position)

        @block.vector
        def _(dve):
            steps = [0]

            def then(instruction):
                steps[0] += 1
                instruction.then_inc(math, 1)
                dve.wait_ge(math, steps[0])

            def running_sum(buffers, n):
                at, step = 0, 1
                while step < n:
                    old, new = buffers(at), buffers(1 - at)
                    then(dve.tensor_copy(new(0, step), old(0, step)))
                    then(dve.tensor_tensor(new(step, n), old(step, n), old(0, n - step), ALU.add))
                    at, step = 1 - at, 2 * step
                return at

            dve.wait_ge(consts_in, 16 * 5)
            dve.wait_ge(counted, 2)
            per_batch = lambda t: t.rearrange("s (b x) -> s x b", x=X)
            then(dve.tensor_copy(count[:, :, :], per_batch(count_ps[0:S, 0:B * X])))
            then(dve.tensor_copy(upto[:, 0], count[:, :, :]))
            u = running_sum(lambda i: lambda a, z: upto[:, i, :, a:z], B)
            then(dve.tensor_tensor(over[:, :, :], upto[:, u, :, B - 1:B].to_broadcast([S, X, CT]),
                                   full[:, :].unsqueeze(1).to_broadcast([S, X, CT]), ALU.is_gt))
            then(dve.tensor_reduce(tiles_of[:, :], over[:, :, :], AX_X, ALU.add))
            then(dve.tensor_copy(ends[:, 0, :], tiles_of[:, :]))
            e = running_sum(lambda i: lambda a, z: ends[:, i, a:z], X)
            then(dve.tensor_tensor(passed[:, :, :], ends[0:1, e, :].unsqueeze(1).to_broadcast([1, NT, X]),
                                   tile_no[:, :].unsqueeze(2).to_broadcast([1, NT, X]), ALU.is_le))
            then(dve.tensor_reduce(expert_f[:, :], passed[:, :, :], AX_X, ALU.add))
            dve.tensor_scalar(expert_of[:, :], expert_f[:, :], float(X - 1), None, ALU.min).then_inc(experts_ready, 1)
            then(dve.tensor_tensor(start[:, :], ends[:, e, :], tiles_of[:, :], ALU.subtract))
            then(dve.tensor_scalar(start[:, :], start[:, :], float(SLOTS), None, ALU.mult))
            turned = lambda t: t.rearrange("s x b -> s b x")
            then(dve.tensor_tensor(place[:, :, :], before_ps[0:S, 0:B * X].rearrange("s (b x) -> s b x", x=X),
                                   turned(upto[:, u]), ALU.add))
            then(dve.tensor_tensor(place[:, :, :], place[:, :, :], turned(count[:, :, :]), ALU.subtract))
            then(dve.tensor_tensor(place[:, :, :], place[:, :, :], start[:, :].unsqueeze(1).to_broadcast([S, B, X]), ALU.add))
            then(dve.tensor_tensor(place[:, :, :], place[:, :, :], oh[:, :, :], ALU.mult))
            then(dve.tensor_reduce(slot_f[:, :], place[:, :, :], AX_X, ALU.add))
            dve.tensor_copy(slot_of[:, :], slot_f[:, :]).then_inc(slots_ready, 1)

            def turned_tile(j, p):
                dve.wait_ge(xT_ready, j + 1)
                wait(dve, up_ready, 2 * (j - 1))
                dve.tensor_copy(x_T[:, p].rearrange("p k s -> p (k s)"), xT_ps[:, 0:KE * SLOTS]).then_inc(xT_evac, 1)

            def position(j, p):
                if live(j - 1):
                    dve.wait_ge(hT_ready, j)
                    wait(dve, y_ready, j - 1)
                    dve.tensor_copy(h_T[:, 0:4, :].rearrange("p c s -> p (c s)"), hT_ps[0][:, 0:4 * SLOTS]).then_inc(hT_evac_a, 1)
                if live(j):
                    wait(dve, hT_ready, j - 1)
                    for h in range(2):
                        dve.wait_ge(silu_done, 2 * j + h + 1)
                        dve.wait_ge(up_ready, 2 * j + h + 1)
                        dve.tensor_tensor(hidden[:, p, QF * h:QF * h + QF], gate[:, h, :], up_ps[h][:, 0:QF],
                                          ALU.mult).then_inc(gated, 1)
                if live(j + 1):
                    turned_tile(j + 1, 1 - p)

            turned_tile(0, 0)
            run(dve, position)

            def finish(g):
                dve.wait_ge(rstd_ready, g + 1)
                for b in range(GB):
                    last = dve.tensor_scalar(answer[:, g % 2, b, :], answer[:, g % 2, b, :], mv[:, g % 2, b, 0:1],
                                             rstd[:, g % 2, b:b + 1], ALU.subtract, ALU.mult)
                last.then_inc(out_ready, 1)

            for g in range(G1):
                dve.wait_ge(gather_in[g % 2], 16 * GB * (g // 2 + 1))
                dve.tensor_tensor(answer[:, g % 2], answer[:, g % 2], x2[:, GB * g:GB * g + GB, :], ALU.add).then_inc(added, 1)
                dve.wait_ge(added, g + 1)
                wait(dve, stats_done, 2 * GB * g)
                for b in range(GB):
                    dve.bn_stats(stats[:, b, :], answer[:, g % 2, b, :]).then_inc(stats_done, 1)
                if g >= 2:
                    dve.wait_ge(out_ready, g - 1)
                for b in range(GB):
                    dve.wait_ge(stats_done, 2 * GB * g + b + 1)
                    dve.bn_aggr(mv[:, g % 2, b, :], stats[:, b, :]).then_inc(stats_done, 1)
                dve.wait_ge(stats_done, 2 * GB * g + 2 * GB)
                wait(dve, rstd_ready, g)
                dve.tensor_scalar(veps[:, :], mv[:, g % 2, :, 1], EPS, None, ALU.add).then_inc(var_ready, 1)
                if g >= 1:
                    finish(g - 1)
            finish(G1 - 1)


def decoder_layer(nc, io, phases="abc"):
    with ExitStack() as ctx:
        gu = ctx.enter_context(nc.sbuf_tensor("gate_up", [128, X, KE, 2 * FF], F32))
        dn = ctx.enter_context(nc.sbuf_tensor("down", [128, X, FC, E], F32))
        choice = ctx.enter_context(nc.sbuf_tensor("choice", [S, B, X], F32))
        gate_up_in = ctx.enter_context(nc.semaphore("gate_up_in"))
        for name, rows, cols in (("x1", B * S, E), ("x2", B * S, E), ("mask_f", B, S2 + S2 % 2),
                                 ("sorted", NT * SLOTS, E), ("answers", NT * SLOTS, E)):
            if name not in io:
                io[name] = nc.dram_tensor(name, (rows, cols), F32).ap()

        def carve(space, parts):
            mem, at = {}, 0
            for name, (a, b) in parts.items():
                mem[name] = space[:, at:at + a * b].rearrange("p (a b) -> p a b", a=a)
                at += a * b
            return mem

        def rows_of(mem, rows):
            return {name: view[0:rows.get(name, 128)] for name, view in mem.items()}

        gu_flat = gu[:, :, :, :].rearrange("p x k f -> p (x k f)")
        dn_flat = dn[:, :, :, :].rearrange("p x c e -> p (x c e)")
        if "a" in phases:
            self_attention(nc, io, carve(gu_flat, {"wq": (KE, 1024), "wk": (KE, 1024), "wv": (KE, 1024),
                                                   "wu": (C1, E), "xT": (KE, B * S)}))
        if "b" in phases:
            SC = S2 + S2 % 2
            late = carve(gu_flat[:, (X * KE - 2) * 2 * FF:], {"k_w": (KE, 3 * PR), "v_w": (KE, E)})
            last = rows_of(carve(gu_flat[:, (X * KE - 1) * 2 * FF:], {
                "x1_nat": (2, E), "x1_res": (1, E), "x1_T": (KE, S), "x2_T": (KE, S)}), {"x1_nat": S, "x1_res": S})
            cross_attention(nc, io, late | last | rows_of(carve(dn_flat, {
                "q_w": (KE, 3 * PR), "p_w": (4, E), "probs": (3, N2 * S), "v_bias": (1, E), "c_T": (KE, SC), "q_T": (3, S),
                "v": (2, 3 * N2 * 32), "o_raw": (1, 4 * S), "inv": (1, 4 * S), "o_T": (1, 4 * S), "zeros": (1, E)}),
                {"probs": CTX[0][1], "v": CTX[0][1], "q_T": PR})
                            | {"choice": choice, "gate_up": gu_flat, "gate_up_in": gate_up_in})
        if "c" in phases:
            experts(nc, io, {"gate_up": gu, "down": dn, "choice": choice, "gate_up_in": gate_up_in})



def _constants(np):
    block_of = np.zeros((PR, N2), np.float32)
    for h0, n in PARTS:
        for h in range(n):
            block_of[D2 * h:D2 * h + D2, h0 + h] = D2 ** -0.5
    sum_of = np.zeros((128, 128), np.float32)
    for q in range(4):
        sum_of[32 * q + D2, 32 * q:32 * q + 32] = 1.0
    ones = np.ones((S, S), np.float32)
    return {
        "ident": np.eye(128, dtype=np.float32), "below": np.tril(ones, -1), "earlier": np.triu(ones, 1), "ones": ones,
        "block_of": block_of, "sum_of": sum_of, "rank": np.tile((X - np.arange(X, dtype=np.float32)) / (2 * X), (S, 1)),
        "full": np.tile(SLOTS * np.arange(CT, dtype=np.float32), (S, 1)), "tile_no": np.arange(NT, dtype=np.float32)[None],
    }


def _arrays(np, a):
    rows = lambda w: w.reshape(-1, 128, w.shape[-1]).transpose(1, 0, 2)

    def parts(w):
        out = np.zeros((w.shape[0], len(PARTS) * PR), w.dtype)
        for i, (h0, n) in enumerate(PARTS):
            out[:, PR * i:PR * i + D2 * n] = w[:, D2 * h0:D2 * (h0 + n)]
        return out

    p_w = np.zeros((4, 32, 4, E), np.float32)
    p_w[:, 0:D2] = a["L0_xattn_proj_w"].reshape(4, 4, D2, E).transpose(1, 2, 0, 3)
    p_w[0, D2, 0] = a["L0_xattn_proj_b"]
    down = np.zeros((X, FC * 128, E), np.float32)
    down[:, 0:FF] = a["L0_ffn_down_w"].transpose(0, 2, 1)
    gate_up = np.concatenate([a["L0_ffn_gate_w"], a["L0_ffn_up_w"]], axis=1).transpose(0, 2, 1)
    heads = lambda w: rows(w.transpose(1, 0, 2).reshape(E, N1 * D1))
    return {
        "x": a["x"], "xT": a["x"].reshape(B * S, E).T.reshape(KE, 128, B * S),
        "wq": heads(a["L0_attn_WQ"]), "wk": heads(a["L0_attn_WK"]), "wv": heads(a["L0_attn_WV_down"]),
        "wu": rows(a["L0_attn_WV_up"].reshape(N1 * D1, E)),
        "ctxT": np.pad(a["ctx_1024"].transpose(0, 2, 1).reshape(B, KE, 128, S2).transpose(0, 2, 1, 3),
                       ((0, 0), (0, 0), (0, 0), (0, S2 % 2))),
        "mask": a["mask_BxS2_bk0"],
        "q_w": rows(parts(a["L0_xattn_q_w"])), "q_b": parts(a["L0_xattn_q_b"][None]).reshape(-1, PR).T,
        "k_w": rows(parts(a["L0_xattn_kv_w"][:, 0:E])), "k_b": parts(a["L0_xattn_kv_b"][None, 0:E]).reshape(-1, PR).T,
        "v_w": rows(a["L0_xattn_kv_w"][:, E:]), "v_b": a["L0_xattn_kv_b"][E:],
        "p_w": p_w.reshape(128, 4, E), "router": rows(a["L0_ffn_router_w"].T),
        "gate_up": gate_up.reshape(X * KE * 128, 2 * FF),
        "down": down.reshape(X, FC, 128, E).transpose(0, 2, 1, 3),
    }


def kernel(**inputs):
    import numpy as _np
    import concourse.bacc as _bacc
    from concourse.bass_utils import run_bass_kernel_spmd as _run

    nc = _bacc.Bacc("TRN2", target_bir_lowering=False, num_devices=1)
    given = {name: _np.asarray(value) for name, value in inputs.items()}
    arrays, io = {}, {}
    for name, a in {**_arrays(_np, given), **_constants(_np)}.items():
        a = arrays[f"in_{name}"] = _np.ascontiguousarray(a)
        io[name] = nc.dram_tensor(f"in_{name}", a.shape, mybir.dt.from_np(a.dtype), kind="ExternalInput").ap()
    io["out"] = nc.dram_tensor("out_0", (B, S, E), F32, kind="ExternalOutput").ap()
    decoder_layer(nc, io)
    r = _run(nc, [arrays], core_ids=[0])
    return r.results[0]["out_0"]
```

```python
from contextlib import ExitStack

import concourse.bass as bass
from concourse import mybir

F32 = mybir.dt.float32
F32R = mybir.dt.float32r
U8 = mybir.dt.uint8
U32 = mybir.dt.uint32
I32 = mybir.dt.int32
ALU = mybir.AluOpType
ACT = mybir.ActivationFunctionType
AX_X = mybir.AxisListType.X

B, S, E = 32, 100, 256
KE = E // 128
EPS = 1e-5

N1, D1 = 16, 64
C1 = N1 * D1 // 128
GB = 4
G1 = B // GB
GS = GB * S
BELOW = -3.0e38


N2, D2 = 16, 16
S2 = 361
PARTS = [(0, 5), (5, 5), (10, 6)]
PR = 96
MASK_ROW, MAX_ROW = 96, 97
CTX = [(0, 121), (121, 120), (241, 120)]
TILES = [(p, S * h0 + w * i, w) for p, (h0, n) in enumerate(PARTS)
         for w in [S * n // (4 if n == 5 else 5)] for i in range(S * n // w)]
RUNS = [(0, 0, 500), (1, 500, 500), (2, 1000, 300), (2, 1300, 300)]
MASKED = -2.0 ** 100

X, FF = 8, 704
FC = -(-FF // 128)
QF = FF // 2
SLOTS = 128
NT = (B * S + X * (SLOTS - 1)) // SLOTS
CT = B * S // SLOTS
ROOM = B * S + SLOTS
IDLE = NT - CT


def wait(eng, sem, value):
    if isinstance(value, int) and value <= 0:
        return
    eng.wait_ge(sem, value)


def self_attention(nc, io):
    raw = lambda t: t.bitcast(F32)
    with ExitStack() as ctx:
        sb = lambda name, shape, dt=F32: ctx.enter_context(nc.sbuf_tensor(name, shape, dt))
        sem = lambda name: ctx.enter_context(nc.semaphore(name))
        bank = [ctx.enter_context(nc.psum_tensor(f"a_bank{i}", [128, 512], F32)) for i in range(8)]
        q_ps, k_ps = bank[0], bank[1]
        score_ps = [bank[2], bank[3]]
        share_ps, v_ps = bank[4], bank[5]
        delta_ps = [bank[6], bank[7]]

        ident = sb("a_ident", [128, 128])
        below = sb("a_below", [S, S])
        w = [sb(f"a_{n}", [128, KE, N1 * D1]) for n in ("wq", "wk", "wv")]
        wu = sb("a_wu", [128, C1, E])
        wu_hi, wu_lo = (sb(f"a_wu_{half}", [128, C1, E], F32R) for half in ("hi", "lo"))
        w_hi, w_lo = ([sb(f"a_{n}_{half}", [128, KE, N1 * D1], F32R) for n in ("wq", "wk", "wv")] for half in ("hi", "lo"))
        x_raw = sb("a_x_raw", [128, KE, GS])
        x_hi, x_lo = (sb(f"a_x_{half}", [128, 2, KE, GS], F32R) for half in ("hi", "lo"))
        q_blk = sb("a_q_blk", [128, 2, GB, 2, S])
        kT = sb("a_kT", [128, 2, GS])
        dead = sb("a_dead", [S, 2, GB, S])
        scores = sb("a_scores", [S, 2, 2, GB, S])
        neg_max = sb("a_neg_max", [S, 2, 2, GB])
        probs = sb("a_probs", [S, 2, 2, GB, S])
        total = sb("a_total", [S, 2, 2, GB])
        diag = sb("a_diag", [S, 2, 2, GB, S])
        top = sb("a_top", [S, 2, GB])
        inv = sb("a_inv", [S, 2, GB])
        share = sb("a_share", [S, 2, GB, 2 * D1])
        shareT = sb("a_shareT", [128, 2, GS])
        vT = sb("a_vT", [128, 2, GS])
        vT_hi, vT_lo = (sb(f"a_vT_{half}", [128, 2, GS], F32R) for half in ("hi", "lo"))
        x_nat = sb("a_x_nat", [S, GB, E])
        y = sb("a_y", [S, GB, E])
        stats = sb("a_stats", [S, GB, 6])
        pause = sb("a_pause", [1, 1])
        mv = sb("a_mv", [S, GB, 2])
        veps = sb("a_veps", [S, GB])
        rstd = sb("a_rstd", [S, GB])
        half = sb("a_half", [S, GB])

        consts_in, x_in, x1_out = (sem(n) for n in ("a_consts_in", "a_x_in", "a_x1_out"))
        w_in = [sem(f"a_{n}_in") for n in ("wq", "wk", "wv", "wu")]
        w_hi_made, w_split, xT_in, x_hi_made, x_split = (sem(n) for n in (
            "a_w_hi_made", "a_w_split", "a_xT_in", "a_x_hi_made", "a_x_split"))
        half_set = sem("a_half_set")
        q_ready, k_ready, q_evac, k_evac = (sem(n) for n in ("a_q_ready", "a_k_ready", "a_q_evac", "a_k_evac"))
        scores_ready, dead_found, masked, max_ready = (sem(n) for n in ("a_scores_ready", "a_dead_found", "a_masked", "a_max_ready"))
        exp_done, diag_ready, sums_ready, share_ready = (sem(n) for n in ("a_exp_done", "a_diag_ready", "a_sums_ready", "a_share_ready"))
        shareT_ready, shareT_evac, v_ready, v_scaled = (sem(n) for n in ("a_shareT_ready", "a_shareT_evac", "a_v_ready", "a_v_scaled"))
        vT_hi_made, vT_split = sem("a_vT_hi_made"), sem("a_vT_split")
        delta_steps, added, stats_done, var_ready, rstd_ready, x1_ready = (
            sem(n) for n in ("a_delta_steps", "a_added", "a_stats_done", "a_var_ready", "a_rstd_ready", "a_x1_ready"))

        def schedule(stages):
            def positions(g, u):
                for c in range(C1):
                    for lag, do in stages:
                        back = -((c - lag) // C1)
                        if not isinstance(g, int) or 0 <= g - back < G1:
                            do(g - back, c - lag + C1 * back, C1 * g + c - lag, (u + back) % 2)
            return positions

        def run(eng, stages):
            positions = schedule(stages)
            positions(0, 0)
            positions(1, 1)
            with eng.Fori(1, G1 // 2) as pair:
                for u in range(2):
                    positions(2 * pair + u, u)
            positions(G1, 0)
            positions(G1 + 1, 1)

        block = ctx.enter_context(nc.Block())

        @block.sync
        def _(sp):
            def load_turned(g):
                wait(sp, x_split, g)
                sp.dma_start(x_raw[:, :, :], io["xT"][:, :, bass.ds(g * GS, GS)]).then_inc(xT_in, 16)

            load_turned(0)
            sp.dma_start(w[0][:, :, :], io["wq"]).then_inc(w_in[0], 16)
            sp.dma_start(w[1][:, :, :], io["wk"]).then_inc(w_in[1], 16)
            sp.dma_start(below[:, :], io["below"]).then_inc(consts_in, 16)
            sp.dma_start(ident[:, :], io["ident"]).then_inc(consts_in, 16)
            sp.dma_start(w[2][:, :, :], io["wv"]).then_inc(w_in[2], 16)
            sp.dma_start(wu[:, :, :], io["wu"]).then_inc(w_in[3], 16)
            x_of = io["x"].rearrange("(g b) s e -> g s b e", b=GB)
            x1_of = io["x1"].rearrange("(g b s) e -> g s b e", b=GB, s=S)

            def load(g):
                wait(sp, added, GB * g)
                sp.dma_start(x_nat[:, :, :], x_of[g]).then_inc(x_in, 16)

            def store(g):
                sp.wait_ge(x1_ready, g + 1)
                sp.dma_start(x1_of[g], y[:, :, :]).then_inc(x1_out, 16)

            load(0)
            load_turned(1)
            with sp.Fori(1, G1) as g:
                load_turned(g + 1)
                load(g)
                store(g - 1)
            store(G1 - 1)
            sp.wait_ge(x1_out, 16 * G1)

        @block.tensor
        def _(pe):
            def project(i, ps, c, u):
                cols = slice(128 * c, 128 * c + 128)
                for j, (half, x) in enumerate(((w_hi[i], x_hi), (w_lo[i], x_hi), (w_hi[i], x_lo))):
                    for k in range(KE):
                        last = pe.matmul(ps[:, 0:GS], half[:, k, cols], x[:, u, k, :],
                                         start=(j == k == 0), stop=(j == 2 and k == KE - 1))
                return last

            def project_qk(g, c, n, u):
                if c == 0:
                    pe.wait_ge(x_split, g + 1)
                for i, ps, ready, evac in ((0, q_ps, q_ready, q_evac), (1, k_ps, k_ready, k_evac)):
                    if isinstance(n, int) and n == 0:
                        pe.wait_ge(w_split, i + 1)
                    wait(pe, evac, n)
                    project(i, ps, c, u).then_inc(ready, 1)

            def score(g, c, n, u):
                pe.wait_ge(q_evac, n + 1)
                pe.wait_ge(k_evac, n + 1)
                for i in range(2):
                    wait(pe, masked, 2 * n - 1 + i)
                    for b in (2 * i, 2 * i + 1):
                        last = pe.matmul(score_ps[i][0:S, 2 * S * (b % 2):2 * S * (b % 2) + 2 * S],
                                         kT[:, c % 2, S * b:S * b + S], q_blk[:, c % 2, b].rearrange("p h s -> p (h s)"),
                                         start=True, stop=True)
                    last.then_inc(scores_ready, 1)

            def values(g, c, n, u):
                pe.wait_ge(share_ready, n + 1)
                wait(pe, shareT_evac, n)
                for b in range(GB):
                    last = pe.transpose(share_ps[:, S * b:S * b + S], share[:, c % 2, b, :], ident[0:S, 0:S])
                last.then_inc(shareT_ready, 1)
                if isinstance(n, int) and n == 0:
                    pe.wait_ge(w_split, 3)
                wait(pe, v_scaled, n)
                project(2, v_ps, c, u).then_inc(v_ready, 1)

            def expand(g, c, n, u):
                pe.wait_ge(vT_split, n + 1)
                if isinstance(n, int) and n == 0:
                    pe.wait_ge(w_split, 4)
                if c == 0:
                    wait(pe, added, GB * g)
                for b in range(GB):
                    cols = slice(S * b, S * b + S)
                    for j, (v, half) in enumerate(((vT_hi, wu_hi), (vT_lo, wu_hi), (vT_hi, wu_lo))):
                        last = pe.matmul(delta_ps[b // 2][0:S, E * (b % 2):E * (b % 2) + E], v[:, c % 2, cols],
                                         half[:, c, :], start=(c == j == 0 and b % 2 == 0), stop=(c == C1 - 1 and j == 2),
                                         skip_group_check=True)
                last.then_inc(delta_steps, 1)

            pe.wait_ge(consts_in, 32)
            run(pe, [(0, project_qk), (1, score), (4, values), (7, expand)])

        @block.scalar
        def _(act):
            def evacuate(g, c, n, u):
                act.wait_ge(q_ready, n + 1)
                wait(act, scores_ready, 2 * n - 2)
                for h in range(2):
                    rows = slice(64 * h, 64 * h + 64)
                    last = act.activation(q_blk[rows, c % 2, :, h, :], q_ps[rows, 0:GS].rearrange("p (b s) -> p b s", b=GB),
                                          ACT.Copy, scale=D1 ** -0.5)
                last.then_inc(q_evac, 1)
                act.wait_ge(k_ready, n + 1)
                act.activation(kT[:, c % 2, :], k_ps[:, 0:GS], ACT.Copy).then_inc(k_evac, 1)

            def exps(g, c, n, u):
                wait(act, diag_ready, n - 1)
                wait(act, share_ready, n - 1)
                for i in range(2):
                    act.wait_ge(max_ready, 2 * n + 1 + i)
                    for b in range(GB):
                        last = act.activation(probs[:, c % 2, i, b, :], scores[:, c % 2, i, b, :], ACT.Exp,
                                              bias=neg_max[:, c % 2, i, b:b + 1],
                                              accum_out=total[:, c % 2, i, b:b + 1])
                last.then_inc(exp_done, 1)

            def share_copy(g, c, n, u):
                act.wait_ge(shareT_ready, n + 1)
                wait(act, v_scaled, n - 1)
                act.activation(shareT[:, c % 2, :], share_ps[:, 0:GS], ACT.Copy, scale=1.0 / N1).then_inc(shareT_evac, 1)

            def tokens_hi(g, u):
                act.wait_ge(xT_in, 16 * g + 16)
                wait(act, v_ready, C1 * (g - 1))
                act.activation(x_hi[:, u], x_raw[:, :, :], ACT.Copy).then_inc(x_hi_made, 1)

            def next_tokens_hi(g, c, n, u):
                if c == 4:
                    tokens_hi(g + 1, 1 - u)

            def weights_hi(i):
                hi, given = (w_hi[i], w[i]) if i < 3 else (wu_hi, wu)
                act.wait_ge(w_in[i], 16)
                act.activation(hi[:, :, :], given[:, :, :], ACT.Copy).then_inc(w_hi_made, 1)

            def later_weights_hi(g, c, n, u):
                if isinstance(n, int) and n in (1, 3):
                    weights_hi(2 + n // 2)

            def values_hi(g, c, n, u):
                act.wait_ge(v_scaled, n + 1)
                wait(act, delta_steps, n - 1)
                act.activation(vT_hi[:, c % 2, :], vT[:, c % 2, :], ACT.Copy).then_inc(vT_hi_made, 1)

            tokens_hi(0, 0)
            weights_hi(0)
            weights_hi(1)
            act.wait_ge(half_set, 2)
            run(act, [(0, evacuate), (2, exps), (4, share_copy), (5, values_hi), (0, next_tokens_hi), (0, later_weights_hi)])

        @block.gpsimd
        def _(pool):
            def pick(g, c, n, u):
                pool.wait_ge(exp_done, n + 1)
                wait(pool, sums_ready, n - 1)
                eye = ident[0:S, 0:S].unsqueeze(1).to_broadcast([S, 2 * GB, S])
                pool.tensor_tensor(diag[:, c % 2].rearrange("s i b t -> s (i b) t"),
                                   probs[:, c % 2].rearrange("s i b t -> s (i b) t"), eye, ALU.mult).then_inc(diag_ready, 1)

            def values_lo(g, c, n, u):
                pool.wait_ge(vT_hi_made, n + 1)
                wait(pool, delta_steps, n - 1)
                pool.tensor_tensor(vT_lo[:, c % 2, :], vT[:, c % 2, :], raw(vT_hi[:, c % 2, :]), ALU.subtract).then_inc(vT_split, 1)

            def inverse_root(g, c, n, u):
                if c == C1 - 1:
                    pool.wait_ge(var_ready, g + 1)
                    pool.tensor_tensor(rstd[:, :], veps[:, :], half[:, :], ALU.pow).then_inc(rstd_ready, 1)

            pool.memset(half[:, :], -0.5).then_inc(half_set, 1)
            pool.wait_ge(half_set, 1)
            pool.memset(q_blk[:, :, :, :, :], 0.0).then_inc(half_set, 1)
            pool.wait_ge(consts_in, 32)
            run(pool, [(2, pick), (6, values_lo), (8, inverse_root)])

        @block.vector
        def _(dve):
            def mask(g, c, n, u):
                for i in range(2):
                    dve.wait_ge(scores_ready, 2 * n + 1 + i)
                    sc = score_ps[i][0:S, 0:GS].rearrange("s (b t) -> s b t", b=GB)
                    low = below[:, :].unsqueeze(1).to_broadcast([S, GB, S])
                    dve.scalar_tensor_tensor(out=dead[:, i], in0=sc, scalar=0.0, in1=low,
                                             op0=ALU.is_equal, op1=ALU.max).then_inc(dead_found, 1)
                wait(dve, exp_done, n - 1)
                for i in range(2):
                    dve.wait_ge(dead_found, 2 * n + 1 + i)
                    sc = score_ps[i][0:S, 0:GS].rearrange("s (b t) -> s b t", b=GB)
                    dve.scalar_tensor_tensor(out=scores[:, c % 2, i], in0=dead[:, i], scalar=BELOW, in1=sc,
                                             op0=ALU.mult, op1=ALU.add).then_inc(masked, 1)
                for i in range(2):
                    dve.wait_ge(masked, 2 * n + 1 + i)
                    dve.tensor_reduce(neg_max[:, c % 2, i], scores[:, c % 2, i], AX_X, ALU.max,
                                      negate=True).then_inc(max_ready, 1)

            def shares(g, c, n, u):
                dve.wait_ge(diag_ready, n + 1)
                wait(dve, share_ready, n)
                dve.tensor_reduce(top[:, :, :], diag[:, c % 2], AX_X, ALU.add).then_inc(sums_ready, 1)
                dve.reciprocal(inv[:, :, :], total[:, c % 2]).then_inc(sums_ready, 1)
                wait(dve, shareT_ready, n - 1)
                dve.wait_ge(sums_ready, 2 * n + 2)
                wide = lambda t: t[:, :, :].rearrange("s i b -> s (i b)").unsqueeze(2).to_broadcast([S, 2 * GB, D1])
                dve.tensor_tensor(share[:, c % 2].rearrange("s b (h d) -> s (b h) d", h=2), wide(top), wide(inv),
                                  ALU.mult).then_inc(share_ready, 1)

            def scale_values(g, c, n, u):
                dve.wait_ge(shareT_evac, n + 1)
                dve.wait_ge(v_ready, n + 1)
                wait(dve, vT_split, n - 1)
                dve.tensor_tensor(vT[:, c % 2, :], v_ps[:, 0:GS], shareT[:, c % 2, :], ALU.mult).then_inc(v_scaled, 1)

            def add_up(g, c, n, u):
                if c < C1 - 1:
                    return
                dve.wait_ge(delta_steps, C1 * g + C1)
                dve.wait_ge(x_in, 16 * g + 16)
                wait(dve, x1_out, 16 * g)
                for b in range(GB):
                    dve.scalar_tensor_tensor(out=y[:, b, :], in0=x_nat[:, b, :], scalar=2.0,
                                             in1=delta_ps[b // 2][0:S, E * (b % 2):E * (b % 2) + E],
                                             op0=ALU.mult, op1=ALU.add).then_inc(added, 1)

            def statistics(g, c, n, u):
                if c < C1 - 1:
                    return
                for b in range(GB):
                    dve.wait_ge(added, GB * g + b + 1)
                    dve.bn_stats(stats[:, b, :], y[:, b, :]).then_inc(stats_done, 1)
                dve.wait_ge(stats_done, 2 * GB * g + GB)
                dve.memset(pause[:, :], 0.0)
                for b in range(GB):
                    dve.bn_aggr(mv[:, b, :], stats[:, b, :]).then_inc(stats_done, 1)
                dve.wait_ge(stats_done, 2 * GB * g + 2 * GB)
                dve.tensor_scalar(veps[:, :], mv[:, :, 1], EPS, None, ALU.add).then_inc(var_ready, 1)

            def normalize(g, c, n, u):
                if c < C1 - 1:
                    return
                dve.wait_ge(rstd_ready, g + 1)
                for b in range(GB):
                    last = dve.tensor_scalar(y[:, b, :], y[:, b, :], mv[:, b, 0:1], rstd[:, b:b + 1],
                                             ALU.subtract, ALU.mult)
                last.then_inc(x1_ready, 1)

            def tokens_lo(g, u):
                dve.wait_ge(x_hi_made, g + 1)
                wait(dve, v_ready, C1 * (g - 1))
                dve.tensor_tensor(x_lo[:, u], x_raw[:, :, :], raw(x_hi[:, u]), ALU.subtract).then_inc(x_split, 1)

            def next_tokens_lo(g, c, n, u):
                if c == 5:
                    tokens_lo(g + 1, 1 - u)

            def weights_lo(i):
                lo, hi, given = (w_lo[i], w_hi[i], w[i]) if i < 3 else (wu_lo, wu_hi, wu)
                dve.wait_ge(w_hi_made, i + 1)
                dve.tensor_tensor(lo[:, :, :], given[:, :, :], raw(hi[:, :, :]), ALU.subtract).then_inc(w_split, 1)

            def later_weights_lo(g, c, n, u):
                if isinstance(n, int) and n in (2, 4):
                    weights_lo(1 + n // 2)

            tokens_lo(0, 0)
            weights_lo(0)
            weights_lo(1)
            dve.wait_ge(consts_in, 32)
            run(dve, [(8, add_up), (5, scale_values), (1, mask), (3, shares), (8, statistics), (9, normalize), (0, next_tokens_lo),
                      (0, later_weights_lo)])



def cross_attention(nc, io, mem):
    wq, wp, tally = mem["q_w"], mem["p_w"], mem["tally"]
    with ExitStack() as ctx:
        SC = S2 + S2 % 2
        raw = lambda t: t.bitcast(F32)
        sb = lambda name, shape, dt=F32: ctx.enter_context(nc.sbuf_tensor(name, shape, dt))
        sem = lambda name: ctx.enter_context(nc.semaphore(name))
        bank = [ctx.enter_context(nc.psum_tensor(f"b_bank{i}", [128, 512], F32)) for i in range(8)]
        front_ps, stream_ps, exp_ps, o_ps, misc_ps = bank[0], bank[1:4], bank[4:6], bank[6], bank[7]

        ident = sb("b_ident", [128, 128])
        q_bias, k_bias = sb("b_q_bias", [PR, 3]), sb("b_k_bias", [PR, 3])
        v_bias = mem["v_bias"]
        wk_hi, wk_lo = (sb(f"b_wk_{n}", [128, KE, 3 * PR], F32R) for n in ("hi", "lo"))
        wv_hi, wv_lo = (sb(f"b_wv_{n}", [128, KE, E], F32R) for n in ("hi", "lo"))
        block_of = sb("b_block_of", [PR, N2])
        sum_of = sb("b_sum_of", [128, 128])
        rank = sb("b_rank", [S, X])
        router = sb("b_router", [128, KE, X])
        earlier, ones = sb("b_earlier", [S, S]), sb("b_ones", [S, S])
        number = sb("b_number", [S, B])
        mask_u8 = sb("b_mask_u8", [B, S2], U8)
        mask_f = mem["probs"][0:B, 0, 0:SC]
        x1_nat, x1_res = mem["x1_nat"], mem["x1_res"][:, 0, :]
        c_T = mem["c_T"]
        c_hi, c_lo = (sb(f"b_c_{n}", [128, 2, KE, SC], F32R) for n in ("hi", "lo"))
        x1_T = mem["x1_T"]
        q_T = mem["q_T"]
        qT_hi, qT_lo = (sb(f"b_qT_{n}", [PR, 3, S], F32R) for n in ("hi", "lo"))
        q_hi, q_lo = (sb(f"b_q_{n}", [PR + 2, 2, N2 * S], F32R) for n in ("hi", "lo"))
        k_hi, k_lo = (sb(f"b_k_{n}", [PR + 2, 2, 3, SC], F32R) for n in ("hi", "lo"))
        v = mem["v"].rearrange("c a (i h d) -> c a i h d", i=3, h=N2)
        neg_max = sb("b_neg_max", [125, len(TILES)])
        max_hi, max_lo = (sb(f"b_max_{n}", [8, 2, 125], F32R) for n in ("hi", "lo"))
        probs = mem["probs"]
        o_raw, inv, o_T = (mem[n][:, 0, :] for n in ("o_raw", "inv", "o_T"))
        y = sb("b_y", [S, 2, E + 1])
        pause = sb("b_pause", [1, 1])
        stats, mv = sb("b_stats", [S, 6]), sb("b_mv", [S, 2, 2])
        veps, rstd, half = sb("b_veps", [S, 1]), sb("b_rstd", [S, 1]), sb("b_half", [S, 1])
        x2_T = mem["x2_T"]
        best, value, first = sb("b_best", [S, 1]), sb("b_value", [S, X]), sb("b_first", [S, 1])
        oh = sb("b_oh", [S, 2, X])
        place, slot_f, slot_of = sb("b_place", [S, X]), sb("b_slot_f", [S, 1]), sb("b_slot_of", [S, 2], U32)

        zeros = mem["zeros"][:, 0, :]

        zeros_out = sem("b_zeros_out")
        kw_in, vw_in, early_in, late_in, mask_read, mask_made, mask_out, ones_set = (sem(n) for n in (
            "b_kw_in", "b_vw_in", "b_early_in", "b_late_in", "b_mask_read", "b_mask_made", "b_mask_out", "b_ones_set"))
        x1_in, mask_in, max_in = ([sem(f"b_{n}{p}") for p in range(2)] for n in ("x1_in", "mask_in", "max_in"))
        ctx_in = sem("b_ctx_in")
        res_in, x2_out = sem("b_res_in"), [sem(f"b_x2_out{p}") for p in range(2)]
        x1T_ready, x1T_evac, q_ready, q_evac, q_split, blk_ready = (sem(n) for n in (
            "b_x1T_ready", "b_x1T_evac", "b_q_ready", "b_q_evac", "b_q_split", "b_blk_ready"))
        w_hi_made, w_split, c_hi_made, c_split, k_hi_made, max_hi_made = (sem(n) for n in (
            "b_w_hi_made", "b_w_split", "b_c_hi_made", "b_c_split", "b_k_hi_made", "b_max_hi_made"))
        k_ready, k_evac, v_ready, v_evac, score_ready, max_done = (sem(n) for n in (
            "b_k_ready", "b_k_evac", "b_v_ready", "b_v_evac", "b_score_ready", "b_max_done"))
        maxT_ready, maxT_evac, shifted_ready, exp_done = (sem(n) for n in (
            "b_maxT_ready", "b_maxT_evac", "b_shifted_ready", "b_exp_done"))
        o_ready, o_evac, sums_ready, inv_ready, o_normed, y_ready = (sem(n) for n in (
            "b_o_ready", "b_o_evac", "b_sums_ready", "b_inv_ready", "b_o_normed", "b_y_ready"))
        added, stats_done, var_ready, rstd_ready, x2_ready = (sem(n) for n in (
            "b_added", "b_stats_done", "b_var_ready", "b_rstd_ready", "b_x2_ready"))
        x2T_ready, x2T_evac, logits_ready, picked, placed, slot_steps = (sem(n) for n in (
            "b_x2T_ready", "b_x2T_evac", "b_logits_ready", "b_picked", "b_placed", "b_slot_steps"))

        def run(eng, position):
            for b in range(4):
                position(b, b % 2)
            with eng.Fori(2, B // 2 - 1) as pair:
                for p in range(2):
                    position(2 * pair + p, p)
            for b in range(B - 2, B + 3):
                position(b, b % 2)

        def live(b):
            return not isinstance(b, int) or 0 <= b < B

        def slot(b, p):
            return b - p + 2

        ROWS = ((v[:, :, :, :, :], 0.0), (v[:, :, :, :, D2:D2 + 1], 1.0), (raw(k_hi[PR:PR + 2, :, :, :]), 1.0),
                (raw(k_lo[PR:PR + 2, :, :, :]), 0.0), (raw(q_hi[PR:PR + 2, :, :]), 1.0),
                (raw(q_lo[PR:PR + 2, :, :]), 0.0), (half[:, :], -0.5), (zeros, 0.0),
                (zeros[:, E:E + 1], float(B * S)))
        early = ((ident[:, :], io["ident"]), (k_bias[:, :], io["k_b"]), (wq, io["q_w"]), (q_bias[:, :], io["q_b"]),
                 (block_of[:, :], io["block_of"]))
        late = ((v_bias[0:CTX[0][1], 0, :], io["v_b"].partition_broadcast(CTX[0][1])), (sum_of[:, :], io["sum_of"]),
                (wp, io["p_w"]), (earlier[:, :], io["earlier"]), (ones[:, :], io["ones"][:, 0:S]),
                (number[:, :], io["number"]), (tally[:, :], io["tally"]), (rank[:, :], io["rank"]), (router[:, :, :], io["router"]))
        passes = lambda hi_a, lo_a, hi_b, lo_b: ((hi_a, hi_b), (lo_a, hi_b), (hi_a, lo_b))

        block = ctx.enter_context(nc.Block())

        @block.sync
        def _(sp):
            def load_x1(b, p):
                if live(b):
                    wait(sp, x1T_ready, b - 1)
                    sp.dma_start(x1_nat[:, p, :], io["x1"][bass.ds(b * S, S), :]).then_inc(x1_in[p], 16)

            def load_mask(b, p):
                if live(b):
                    wait(sp, shifted_ready, 12 * (b - 1))
                    for part in range(3):
                        sp.dma_start(raw(k_hi[MASK_ROW:MASK_ROW + 1, p, part, :]), io["mask_f"][bass.ds(b, 1), :]).then_inc(mask_in[p], 16)

            def load_context(b):
                if live(b):
                    wait(sp, c_split, b)
                    sp.dma_start(c_T, io["ctxT"][bass.ds(b, 1)].rearrange("a p k s -> (a p) k s")).then_inc(ctx_in, 16)

            def fetch(b):
                sp.dma_start(mem["gate_up"][:, bass.ds(b * FF, 2 * FF)], io["gate_up"][bass.ds(b * 64, 128), :])\
                  .then_inc(mem["gate_up_in"], 16)

            def position(b, p):
                if live(b) and p == 0 and not (isinstance(b, int) and b == 2 * (X * KE - 1)):
                    fetch(b)
                if live(b - 1):
                    wait(sp, added, b - 1)
                    sp.dma_start(x1_res[:, :], io["x1"][bass.ds((b - 1) * S, S), :]).then_inc(res_in, 16)
                load_x1(b + 1, 1 - p)
                load_mask(b + 1, 1 - p)
                if isinstance(b, int) and b == 3:
                    sp.dma_start(io["sorted"][X * ROOM:, :].rearrange("(p r) e -> p r e", p=128),
                                 zeros[:, :].unsqueeze(1).to_broadcast([128, IDLE * SLOTS // 128, E + 1])).then_inc(zeros_out, 16)
                if live(b):
                    for i, (q, m) in enumerate(((q_hi, max_hi), (q_lo, max_lo))):
                        sp.wait_ge((max_hi_made, maxT_evac)[i], 2 * b + 2)
                        sp.dma_start(raw(q[MAX_ROW:MAX_ROW + 1, p, 0:1000]).rearrange("o (t w) -> o t w", t=8),
                                     raw(m[0:8, 0, 0:125])).then_inc(max_in[p], 16)
                        sp.dma_start(raw(q[MAX_ROW:MAX_ROW + 1, p, 1000:1600]).rearrange("o (t w) -> o t w", t=5),
                                     raw(m[0:5, 1, 0:120])).then_inc(max_in[p], 16)
                load_context(b + 2)

            sp.dma_start(mem["k_w"], io["k_w"]).then_inc(kw_in, 16)
            load_context(0)
            sp.dma_start(mem["v_w"], io["v_w"]).then_inc(vw_in, 16)
            for dst, src in early:
                sp.dma_start(dst, src).then_inc(early_in, 16)
            load_x1(0, 0)
            sp.dma_start(mask_u8[:, :], io["mask"]).then_inc(mask_read, 16)
            for dst, src in late:
                sp.dma_start(dst, src).then_inc(late_in, 16)
            load_context(1)
            sp.wait_ge(mask_made, 2)
            sp.dma_start(io["mask_f"], mask_f[:, :]).then_inc(mask_out, 16)
            sp.wait_ge(mask_out, 16)
            sp.wait_ge(ones_set, len(ROWS))
            load_mask(0, 0)
            run(sp, position)
            sp.wait_ge(zeros_out, 16)
            for p in range(2):
                sp.wait_ge(x2_out[p], 16 * (B // 2))

        @block.gpsimd
        def _(pool):
            for n, (rows, value) in enumerate(ROWS):
                pool.memset(rows, value).then_inc(ones_set, 1)
                pool.wait_ge(ones_set, n + 1)
            pool.wait_ge(early_in, 16 * len(early))

            def position(b, p):
                if live(b):
                    wait(pool, shifted_ready, 12 * (b - 1))
                for i, (blk, q) in enumerate(((q_hi, qT_hi), (q_lo, qT_lo))):
                    if i == 1 and live(b - 3):
                        pool.wait_ge(slot_steps, 4 * (b - 3) + 3)
                    if live(b):
                        pool.wait_ge(q_split, 2 * b + i + 1)
                        for part, (h0, n) in enumerate(PARTS):
                            cols = blk[0:PR, p, S * h0:S * (h0 + n)].rearrange("r (h s) -> r h s", h=n)
                            pool.tensor_tensor(cols, raw(q[:, part, :]).unsqueeze(1).to_broadcast([PR, n, S]),
                                               block_of[:, h0:h0 + n].unsqueeze(2).to_broadcast([PR, n, S]),
                                               ALU.mult).then_inc(blk_ready, 1)
                    if i == 0 and live(b - 2):
                        pool.wait_ge(var_ready, b - 1)
                        pool.tensor_tensor(rstd[:, :], veps[:, :], half[:, :], ALU.pow).then_inc(rstd_ready, 1)
                if live(b - 3):
                    o = 1 - p
                    pool.indirect_dma_start(out=io["sorted"], out_offset=bass.IndirectOffsetOnAxis(ap=slot_of[:, o:o + 1], axis=0),
                                            in_=y[:, o, :], in_offset=None).then_inc(x2_out[o], 16)

            run(pool, position)

        @block.tensor
        def _(pe):
            first = lambda b: isinstance(b, int) and b == 0

            def turn_x1(b, p):
                pe.wait_ge(x1_in[p], 8 * slot(b, p))
                wait(pe, q_evac, b)
                for k in range(KE):
                    last = pe.transpose(front_ps[:, S * k:S * k + S], x1_nat[:, p, 128 * k:128 * k + 128], ident[0:S, 0:S])
                last.then_inc(x1T_ready, 1)

            def front(b, p):
                pe.wait_ge(c_split, b + 1)
                wait(pe, max_done, 13 * b)
                for part in range(3):
                    for i, (w, c) in enumerate(passes(wk_hi, wk_lo, c_hi, c_lo)):
                        for k in range(KE):
                            last = pe.matmul(stream_ps[part][0:PR, 0:SC], w[:, k, PR * part:PR * part + PR], c[:, p, k, :],
                                             start=(i == k == 0), stop=(i == 2 and k == KE - 1))
                    last.then_inc(k_ready, 1)
                pe.wait_ge(x1T_evac, b + 1)
                for part in range(3):
                    for k in range(KE):
                        last = pe.matmul(front_ps[0:PR, S * (2 + part):S * (3 + part)], wq[:, k, PR * part:PR * part + PR],
                                         x1_T[:, k, :], start=(k == 0), stop=(k == KE - 1))
                last.then_inc(q_ready, 1)

            def values(b, p):
                for i, (c0, n) in enumerate(CTX):
                    if first(b):
                        pe.wait_ge(w_split, 2)
                    pe.wait_ge(k_evac, 3 * b + i + 1)
                    for j, (c, w) in enumerate(passes(c_hi, c_lo, wv_hi, wv_lo)):
                        for k in range(KE):
                            last = pe.matmul(stream_ps[i][0:n, 0:E], c[:, p, k, c0:c0 + n], w[:, k, :],
                                             start=(j == k == 0), stop=(j == 2 and k == KE - 1))
                    last.then_inc(v_ready, 1)

            def rows(b, p, t):
                part, col, w = TILES[t]
                if t == 0:
                    if first(b):
                        pe.wait_ge(ones_set, len(ROWS))
                    pe.wait_ge(k_evac, 3 * b + 3)
                    pe.wait_ge(mask_in[p], 24 * slot(b, p))
                pe.wait_ge(blk_ready, 6 * b + part + 1)
                if t < 3:
                    pe.wait_ge(v_evac, 3 * b + t + 1)
                else:
                    pe.wait_ge(max_done, 13 * b + t - 2)
                pe.matmul(stream_ps[t % 3][0:w, 0:SC], q_hi[0:MASK_ROW + 1, p, col:col + w],
                          k_hi[0:MASK_ROW + 1, p, part, :], start=True, stop=True).then_inc(score_ready, 1)

            def maxima(b, p):
                pe.wait_ge(max_done, 13 * b + 13)
                wait(pe, o_evac, b)
                pe.transpose(o_ps[0:8, 0:125], neg_max[0:125, 0:8], ident[0:125, 0:125])
                pe.transpose(o_ps[0:5, 128:248], neg_max[0:120, 8:13], ident[0:120, 0:120]).then_inc(maxT_ready, 1)

            def shifted(b, p, r, j):
                part, col, w = RUNS[r]
                c0, n = CTX[j]
                if r == j == 0:
                    pe.wait_ge(max_in[p], 32 * slot(b, p))
                    pe.wait_ge(blk_ready, 6 * b + 6)
                e = 3 * r + j
                wait(pe, exp_done, 12 * b + e - 1)
                for i, (k, q) in enumerate(passes(k_hi, k_lo, q_hi, q_lo)):
                    last = pe.matmul(exp_ps[e % 2][0:n, 0:w], k[0:MAX_ROW + 1, p, part, c0:c0 + n],
                                     q[0:MAX_ROW + 1, p, col:col + w], start=(i == 0), stop=(i == 2))
                last.then_inc(shifted_ready, 1)

            def attend(b, p, quad):
                pe.wait_ge(exp_done, 12 * b + 3 * quad + 3)
                if quad == 0:
                    pe.wait_ge(v_evac, 3 * b + 3)
                    pe.wait_ge(maxT_evac, 2 * b + 2)
                for j, (c0, n) in enumerate(CTX):
                    for q in range(4):
                        h = 4 * quad + q
                        last = pe.matmul(o_ps[32 * q:32 * q + 32, S * quad:S * quad + S], v[0:n, p, j, h, :],
                                         probs[0:n, j, S * h:S * h + S], start=(j == 0), stop=(j == 2),
                                         tile_position=(0, 32 * q))
                if quad == 3:
                    last.then_inc(o_ready, 1)

            def sums(b):
                if first(b):
                    pe.wait_ge(late_in, 16 * len(late))
                pe.wait_ge(o_evac, b + 1)
                wait(pe, slot_steps, 4 * (b - 1) + 1)
                pe.matmul(misc_ps[:, 0:4 * S], sum_of[:, :], o_raw, start=True, stop=True).then_inc(sums_ready, 1)

            def project(b):
                pe.wait_ge(o_normed, b + 1)
                for quad in range(4):
                    last = pe.matmul(misc_ps[0:S, 0:E], o_T[:, S * quad:S * quad + S], wp[:, quad, :],
                                     start=(quad == 0), stop=(quad == 3))
                last.then_inc(y_ready, 1)

            def turn(b, p):
                pe.wait_ge(x2_ready, b + 1)
                for k in range(KE):
                    last = pe.transpose(misc_ps[:, S * k:S * k + S], y[:, p, 128 * k:128 * k + 128], ident[0:S, 0:S])
                last.then_inc(x2T_ready, 1)

            def route(b):
                pe.wait_ge(x2T_evac, b + 1)
                for k in range(KE):
                    last = pe.matmul(misc_ps[0:S, 0:X], x2_T[:, k, :], router[:, k, :], start=(k == 0), stop=(k == KE - 1))
                last.then_inc(logits_ready, 1)

            def slots(b, p):
                pe.wait_ge(picked, 4 * b + 4)
                if first(b):
                    pe.wait_ge(late_in, 16 * len(late))
                wait(pe, slot_steps, 4 * b)
                pe.matmul(misc_ps[0:S, 4 * S:4 * S + X], earlier[:, :], oh[:, p, :], start=True, stop=False)
                pe.matmul(misc_ps[0:S, 4 * S:4 * S + X], ones[:, :], tally[:, :], start=False, stop=True).then_inc(placed, 1)

            def position(b, p):
                now, then, old = live(b), live(b - 1), live(b - 2)
                if now:
                    front(b, p)
                if old:
                    project(b - 2)
                if now:
                    values(b, p)
                for r in range(4):
                    for j in range(3):
                        if then:
                            shifted(b - 1, 1 - p, r, j)
                        if now and 3 * r + j >= 1:
                            rows(b, p, 3 * r + j - 1)
                    if then and r >= 1:
                        attend(b - 1, 1 - p, r - 1)
                    if old and r == 1:
                        turn(b - 2, p)
                    if old and r == 2:
                        route(b - 2)
                if now:
                    rows(b, p, 11)
                if old:
                    slots(b - 2, p)
                if now:
                    rows(b, p, 12)
                if then:
                    attend(b - 1, 1 - p, 3)
                if live(b + 1):
                    turn_x1(b + 1, 1 - p)
                if now:
                    maxima(b, p)
                if then:
                    sums(b - 1)

            pe.wait_ge(early_in, 16 * len(early))
            turn_x1(0, 0)
            pe.wait_ge(w_split, 1)
            run(pe, position)

        @block.scalar
        def _(act):
            def exps(b, r):
                part, col, w = RUNS[r]
                for j, (c0, n) in enumerate(CTX):
                    e = 3 * r + j
                    act.wait_ge(shifted_ready, 12 * b + e + 1)
                    act.activation(probs[0:n, j, col:col + w], exp_ps[e % 2][0:n, 0:w], ACT.Exp).then_inc(exp_done, 1)

            def position(b, p):
                now, then, old = live(b), live(b - 1), live(b - 2)
                if now:
                    wait(act, shifted_ready, 12 * (b - 1))
                    for part in range(3):
                        act.wait_ge(k_ready, 3 * b + part + 1)
                        act.activation(k_hi[0:PR, p, part, :], stream_ps[part][0:PR, 0:SC], ACT.Identity,
                                       bias=k_bias[:, part:part + 1]).then_inc(k_hi_made, 1)
                if then:
                    wait(act, o_ready, b - 1)
                    exps(b - 1, 0)
                    exps(b - 1, 1)
                context_hi(b + 1, 1 - p)
                if old:
                    act.wait_ge(x2T_ready, b - 1)
                    wait(act, logits_ready, b - 2)
                    act.activation(x2_T[:, :, :], misc_ps[:, 0:KE * S].rearrange("p (k s) -> p k s", k=KE),
                                   ACT.Copy).then_inc(x2T_evac, 1)
                if then:
                    exps(b - 1, 2)
                    exps(b - 1, 3)
                    act.wait_ge(o_ready, b)
                    wait(act, o_normed, b - 1)
                    act.activation(o_raw, o_ps[:, 0:4 * S], ACT.Copy).then_inc(o_evac, 1)
                if now:
                    act.wait_ge(maxT_ready, b + 1)
                    if live(b - 1):
                        act.wait_ge(max_in[1 - p], 32 * slot(b - 1, 1 - p))
                    act.activation(max_hi[0:8, 0, 0:125], o_ps[0:8, 0:125], ACT.Copy).then_inc(max_hi_made, 1)
                    act.activation(max_hi[0:5, 1, 0:120], o_ps[0:5, 128:248], ACT.Copy).then_inc(max_hi_made, 1)
                x1_turned(b + 1)

            def x1_turned(b):
                if live(b):
                    act.wait_ge(x1T_ready, b + 1)
                    wait(act, q_ready, b)
                    act.activation(x1_T[:, :, :], front_ps[:, 0:KE * S].rearrange("p (k s) -> p k s", k=KE),
                                   ACT.Copy).then_inc(x1T_evac, 1)

            def context_hi(b, p):
                if live(b):
                    act.wait_ge(ctx_in, 16 * b + 16)
                    wait(act, v_ready, 3 * (b - 1))
                    act.activation(c_hi[:, p], c_T, ACT.Copy).then_inc(c_hi_made, 1)

            act.wait_ge(kw_in, 16)
            act.activation(wk_hi[:, :, :], mem["k_w"], ACT.Copy).then_inc(w_hi_made, 1)
            context_hi(0, 0)
            act.wait_ge(vw_in, 16)
            act.activation(wv_hi[:, :, :], mem["v_w"], ACT.Copy).then_inc(w_hi_made, 1)
            act.wait_ge(early_in, 16 * len(early))
            x1_turned(0)
            run(act, position)

        @block.vector
        def _(dve):
            def weights_lo(i, lo, hi, w):
                dve.wait_ge(w_hi_made, i + 1)
                dve.tensor_tensor(lo[:, :, :], w, raw(hi[:, :, :]), ALU.subtract).then_inc(w_split, 1)

            def context_lo(b, p):
                if live(b):
                    dve.wait_ge(c_hi_made, b + 1)
                    wait(dve, v_ready, 3 * (b - 1))
                    dve.tensor_tensor(c_lo[:, p], c_T, raw(c_hi[:, p]), ALU.subtract).then_inc(c_split, 1)

            def keys_lo(b, p):
                wait(dve, shifted_ready, 12 * (b - 1))
                for part in range(3):
                    dve.wait_ge(k_hi_made, 3 * b + part + 1)
                    dve.scalar_tensor_tensor(out=k_lo[0:PR, p, part, :], in0=stream_ps[part][0:PR, 0:SC],
                                             scalar=k_bias[:, part:part + 1], in1=raw(k_hi[0:PR, p, part, :]),
                                             op0=ALU.add, op1=ALU.subtract).then_inc(k_evac, 1)

            def queries(b):
                dve.wait_ge(q_ready, b + 1)
                wait(dve, q_split, 2 * b)
                dve.tensor_tensor(q_T, front_ps[0:PR, 2 * S:5 * S].rearrange("r (t s) -> r t s", t=3),
                                  q_bias[:, :].unsqueeze(2).to_broadcast([PR, 3, S]), ALU.add).then_inc(q_evac, 1)
                dve.wait_ge(q_evac, b + 1)
                wait(dve, blk_ready, 6 * b)
                dve.tensor_copy(qT_hi[:, :, :], q_T).then_inc(q_split, 1)
                dve.wait_ge(q_split, 2 * b + 1)
                dve.tensor_tensor(qT_lo[:, :, :], q_T, raw(qT_hi[:, :, :]), ALU.subtract).then_inc(q_split, 1)

            def maxima_lo(b, p):
                dve.wait_ge(max_hi_made, 2 * b + 2)
                if live(b - 1):
                    dve.wait_ge(max_in[1 - p], 32 * slot(b - 1, 1 - p))
                dve.tensor_tensor(max_lo[0:5, 1, 0:120], o_ps[0:5, 128:248], raw(max_hi[0:5, 1, 0:120]),
                                  ALU.subtract).then_inc(maxT_evac, 1)
                dve.tensor_tensor(max_lo[0:8, 0, 0:125], o_ps[0:8, 0:125], raw(max_hi[0:8, 0, 0:125]),
                                  ALU.subtract).then_inc(maxT_evac, 1)

            def normalize(b, p):
                dve.wait_ge(rstd_ready, b + 1)
                dve.tensor_copy(y[:, p, E:E + 1], number[:, bass.ds(b, 1)])
                dve.tensor_scalar(y[:, p, 0:E], y[:, p, 0:E], mv[:, p, 0:1], rstd[:, 0:1],
                                  ALU.subtract, ALU.mult).then_inc(x2_ready, 1)

            def pick(b, p):
                dve.wait_ge(logits_ready, b + 1)
                logits = misc_ps[0:S, 0:X]
                wait(dve, picked, 4 * b)
                dve.tensor_reduce(best[:, :], logits, AX_X, ALU.max).then_inc(picked, 1)
                dve.wait_ge(picked, 4 * b + 1)
                dve.scalar_tensor_tensor(out=value[:, :], in0=logits, scalar=best[:, 0:1], in1=rank[:, :],
                                         op0=ALU.is_equal, op1=ALU.add).then_inc(picked, 1)
                dve.wait_ge(picked, 4 * b + 2)
                dve.tensor_reduce(first[:, :], value[:, :], AX_X, ALU.max).then_inc(picked, 1)
                dve.wait_ge(picked, 4 * b + 3)
                dve.tensor_scalar(oh[:, p, :], value[:, :], first[:, 0:1], None, ALU.is_equal).then_inc(picked, 1)

            def chosen_places(b, p):
                dve.wait_ge(placed, b + 1)
                wait(dve, slot_steps, 4 * b)
                dve.tensor_tensor(place[:, :], misc_ps[0:S, 4 * S:4 * S + X], oh[:, p, :], ALU.mult).then_inc(slot_steps, 1)

            def chosen_slots(b, p):
                dve.wait_ge(slot_steps, 4 * b + 1)
                dve.tensor_reduce(slot_f[:, :], place[:, :], AX_X, ALU.add).then_inc(slot_steps, 1)
                dve.wait_ge(slot_steps, 4 * b + 2)
                dve.tensor_copy(slot_of[:, p:p + 1], slot_f[:, :]).then_inc(slot_steps, 1)
                dve.tensor_tensor(tally[:, :], tally[:, :], oh[:, p, :], ALU.add).then_inc(slot_steps, 1)

            def biased(b, p):
                wait(dve, o_ready, b - 1)
                for i, (c0, n) in enumerate(CTX):
                    dve.wait_ge(v_ready, 3 * b + i + 1)
                    heads = lambda t: t.rearrange("c (h d) -> c h d", h=N2)
                    dve.tensor_tensor(v[0:n, p, i, :, 0:D2], heads(stream_ps[i][0:n, 0:E]), heads(v_bias[0:n, 0, :]),
                                      ALU.add).then_inc(v_evac, 1)

            def maxima(b, t0, t1):
                if t0 == 0:
                    wait(dve, maxT_ready, b)
                for t in range(t0, t1):
                    w = TILES[t][2]
                    dve.wait_ge(score_ready, 13 * b + t + 1)
                    dve.tensor_reduce(neg_max[0:w, t:t + 1], stream_ps[t % 3][0:w, 0:S2], AX_X, ALU.max,
                                      negate=True).then_inc(max_done, 1)

            def divide(b):
                dve.wait_ge(sums_ready, b + 1)
                wait(dve, o_normed, b)
                dve.reciprocal(inv, misc_ps[:, 0:4 * S]).then_inc(inv_ready, 1)
                dve.wait_ge(inv_ready, b + 1)
                wait(dve, y_ready, b)
                dve.tensor_tensor(o_T, o_raw, inv, ALU.mult).then_inc(o_normed, 1)

            def add_up(b, p):
                dve.wait_ge(y_ready, b + 1)
                dve.wait_ge(res_in, 16 * (b + 1))
                wait(dve, x2T_ready, b - 1)
                if live(b - 2):
                    dve.wait_ge(x2_out[p], 8 * slot(b - 2, p))
                dve.tensor_tensor(y[:, p, 0:E], misc_ps[0:S, 0:E], x1_res[:, :], ALU.add).then_inc(added, 1)
                dve.wait_ge(added, b + 1)
                dve.bn_stats(stats[:, :], y[:, p, 0:E]).then_inc(stats_done, 1)
                dve.wait_ge(stats_done, 2 * b + 1)
                wait(dve, x2_ready, b - 1)
                dve.memset(pause[:, :], 0.0)
                dve.bn_aggr(mv[:, p, :], stats[:, :]).then_inc(stats_done, 1)
                dve.wait_ge(stats_done, 2 * b + 2)
                dve.tensor_scalar(veps[:, :], mv[:, p, 1:2], EPS, None, ALU.add).then_inc(var_ready, 1)

            def position(b, p):
                now, then, old = live(b), live(b - 1), live(b - 2)
                if now:
                    keys_lo(b, p)
                    queries(b)
                if old:
                    add_up(b - 2, p)
                if now:
                    biased(b, p)
                    maxima(b, 0, 2)
                if old:
                    normalize(b - 2, p)
                if now:
                    maxima(b, 2, 6)
                context_lo(b + 1, 1 - p)
                if now:
                    maxima(b, 6, 9)
                if old:
                    pick(b - 2, p)
                if now:
                    maxima(b, 9, 13)
                if old:
                    chosen_places(b - 2, p)
                if now:
                    maxima_lo(b, p)
                if old:
                    chosen_slots(b - 2, p)
                if then:
                    divide(b - 1)

            weights_lo(0, wk_lo, wk_hi, mem["k_w"])
            context_lo(0, 0)
            weights_lo(1, wv_lo, wv_hi, mem["v_w"])
            dve.wait_ge(mask_read, 16)
            dve.memset(mask_f[:, S2:SC], MASKED).then_inc(mask_made, 1)
            dve.tensor_scalar(mask_f[:, 0:S2], mask_u8[:, :], MASKED, None, ALU.mult).then_inc(mask_made, 1)
            dve.wait_ge(early_in, 16 * len(early))
            dve.wait_ge(late_in, 16 * len(late))
            dve.wait_ge(ones_set, len(ROWS))
            run(dve, position)


def experts(nc, io, mem):
    gu, dn, tally, gu_in = mem["gate_up"], mem["down"], mem["tally"], mem["gate_up_in"]
    with ExitStack() as ctx:
        sb = lambda name, shape, dt=F32: ctx.enter_context(nc.sbuf_tensor(name, shape, dt))
        sem = lambda name: ctx.enter_context(nc.semaphore(name))
        bank = [ctx.enter_context(nc.psum_tensor(f"c_bank{i}", [128, 512], F32)) for i in range(8)]
        gate_ps, up_ps, hT_ps, y_ps, xT_ps = bank[0:2], bank[2:4], bank[4:6], bank[6], bank[7]
        count_ps = bank[0]

        ident = sb("c_ident", [128, 128])
        ones = sb("c_ones", [S, 128])
        full, tile_no = sb("c_full", [1, CT]), sb("c_tile_no", [1, NT])
        region, lane = sb("c_region", [128, X]), sb("c_lane", [128, 1])
        count = sb("c_count", [1, X])
        over = sb("c_over", [1, X, CT])
        tiles_of = sb("c_tiles_of", [1, X])
        ends = sb("c_ends", [1, 2, X])
        step = sb("c_step", [1, X])
        passed, jump = sb("c_passed", [1, NT, X]), sb("c_jump", [1, NT, X])
        expert_f, expert_of = sb("c_expert_f", [1, NT]), sb("c_expert_of", [1, NT], I32)
        row_f, row_of = sb("c_row_f", [1, NT]), sb("c_row_of", [1, NT], I32)
        fill_f, fill_of = sb("c_fill_f", [128, X]), sb("c_fill_of", [128, X], U32)
        zeros = sb("c_zeros", [128, E + 1])
        x_tile = sb("c_x_tile", [SLOTS, 4, E + 1])
        x_T = sb("c_x_T", [128, 2, KE, SLOTS])
        gate = sb("c_gate", [SLOTS, 2, QF])
        hidden = sb("c_hidden", [SLOTS, 2, FF])
        h_T = sb("c_h_T", [128, FC, SLOTS])
        y = sb("c_y", [SLOTS, 2, E])
        token = sb("c_token", [SLOTS, 2], U32)
        stats, mv = sb("c_stats", [SLOTS, 6]), sb("c_mv", [SLOTS, 2, 2])
        veps, rstd, half = sb("c_veps", [SLOTS, 1]), sb("c_rstd", [SLOTS, 2]), sb("c_half", [SLOTS, 1])
        pause = sb("c_pause", [1, 1])

        ones_in, consts_in, dn_in, half_set = (sem(n) for n in ("c_ones_in", "c_consts_in", "c_dn_in", "c_half_set"))
        counted, math, fill_ready, experts_ready, rows_ready = (sem(n) for n in (
            "c_counted", "c_math", "c_fill_ready", "c_experts_ready", "c_rows_ready"))
        filled = sem("c_filled")
        tile_in, out_out = [sem(f"c_tile_in{q}") for q in range(4)], [sem(f"c_out_out{p}") for p in range(2)]
        xT_ready, xT_evac, gate_ready, up_ready, silu_done, gated = (sem(n) for n in (
            "c_xT_ready", "c_xT_evac", "c_gate_ready", "c_up_ready", "c_silu_done", "c_gated"))
        hT_ready, hT_evac_a, hT_evac_b, y_ready = (sem(n) for n in (
            "c_hT_ready", "c_hT_evac_a", "c_hT_evac_b", "c_y_ready"))
        added, stats_done, var_ready, rstd_ready, out_ready = (sem(n) for n in (
            "c_added", "c_stats_done", "c_var_ready", "c_rstd_ready", "c_out_ready"))

        def run(eng, position):
            for j in range(4):
                position(j, j % 4)
            with eng.Fori(1, NT // 4 - 1) as four:
                for q in range(4):
                    position(4 * four + q, q)
            for j in range(NT - 4, NT + 2):
                position(j, j % 4)

        def live(j):
            return not isinstance(j, int) or 0 <= j < NT

        block = ctx.enter_context(nc.Block())

        @block.sync
        def _(sp):
            sp.dma_start(ones[:, :], io["ones"]).then_inc(ones_in, 16)
            for dst, src in ((lane[:, :], io["lane"]), (region[:, :], io["region"]),
                             (full[:, :], io["full"]), (tile_no[:, :], io["tile_no"]), (ident[:, :], io["ident"])):
                sp.dma_start(dst, src).then_inc(consts_in, 16)

            def load(j, q):
                if live(j):
                    row = sp.value_load(row_of[0:1, bass.ds(j, 1)], min_val=0, max_val=(X * ROOM + IDLE * SLOTS) - SLOTS)
                    wait(sp, added, j - 3)
                    sp.dma_start(x_tile[:, q, :], io["sorted"][bass.ds(row, SLOTS), :]).then_inc(tile_in[q], 16)

            def position(j, q):
                load(j + 2, (q + 2) % 4)

            sp.wait_ge(rows_ready, 1)
            sp.wait_ge(filled, 16 * X)
            for j in range(2):
                load(j, j)
            run(sp, position)
            for p in range(2):
                sp.wait_ge(out_out[p], 16 * (NT // 2))

        @block.gpsimd
        def _(pool):
            pool.memset(half[:, :], -0.5).then_inc(half_set, 1)
            pool.wait_ge(half_set, 1)
            pool.memset(h_T[FF - 128 * (FC - 1):, FC - 1, :], 0.0).then_inc(half_set, 1)
            pool.wait_ge(half_set, 2)
            pool.memset(zeros[:, :], 0.0).then_inc(half_set, 1)
            pool.wait_ge(half_set, 3)
            pool.memset(zeros[:, E:E + 1], float(B * S)).then_inc(half_set, 1)
            pool.wait_ge(half_set, 4)
            pool.wait_ge(fill_ready, 1)
            for x in range(X):
                pool.indirect_dma_start(out=io["sorted"], out_offset=bass.IndirectOffsetOnAxis(ap=fill_of[:, x:x + 1], axis=0),
                                        in_=zeros[:, :], in_offset=None).then_inc(filled, 16)

            def position(j, q):
                p = q % 2
                if live(j - 2):
                    pool.wait_ge(out_ready, j - 1)
                if live(j - 1):
                    pool.wait_ge(var_ready, j)
                    pool.tensor_tensor(rstd[:, 1 - p:2 - p], veps[:, :], half[:, :], ALU.pow).then_inc(rstd_ready, 1)
                if live(j - 2):
                    pool.indirect_dma_start(out=io["out"].rearrange("b s e -> (b s) e"),
                                            out_offset=bass.IndirectOffsetOnAxis(ap=token[:, p:p + 1], axis=0),
                                            in_=y[:, p, :], in_offset=None, bounds_check=B * S - 1,
                                            oob_is_err=False).then_inc(out_out[p], 16)

            run(pool, position)

        @block.tensor
        def _(pe):
            pe.wait_ge(ones_in, 16)
            pe.matmul(count_ps[:, 0:X], ones[:, :], tally[:, :], start=True, stop=True).then_inc(counted, 1)

            def expert(j):
                return pe.value_load(expert_of[0:1, bass.ds(j, 1)], min_val=0, max_val=X - 1)

            def turn(j, q):
                pe.wait_ge(tile_in[q], 4 * (j - q + 4))
                wait(pe, xT_evac, j)
                for k in range(KE):
                    last = pe.transpose(xT_ps[:, SLOTS * k:SLOTS * k + SLOTS], x_tile[:, q, 128 * k:128 * k + 128], ident[:, :])
                last.then_inc(xT_ready, 1)

            def gate_up(j, p):
                x = expert(j)
                pe.wait_ge(xT_evac, j + 1)
                for h in range(2):
                    for ps, col, ready, freed in ((gate_ps, 0, gate_ready, silu_done), (up_ps, FF, up_ready, gated)):
                        wait(pe, freed, 2 * (j - 1) + h + 1)
                        for k in range(KE):
                            cols = slice(col + QF * h, col + QF * h + QF)
                            last = pe.matmul(ps[h][:, 0:QF], x_T[:, p, k, :],
                                             gu[:, bass.ds(x, 1), k, cols].rearrange("p a f -> p (a f)"),
                                             start=(k == 0), stop=(k == KE - 1))
                        last.then_inc(ready, 1)

            def turn_hidden(j, p):
                pe.wait_ge(gated, 2 * j + 2)
                wait(pe, hT_evac_a, j)
                wait(pe, hT_evac_b, 2 * j)
                for c in range(FC):
                    n = min(128, FF - 128 * c)
                    last = pe.transpose(hT_ps[c // 4][0:n, SLOTS * (c % 4):SLOTS * (c % 4) + SLOTS],
                                        hidden[:, p, 128 * c:128 * c + n], ident[:, :])
                last.then_inc(hT_ready, 1)

            def down(j, p):
                x = expert(j)
                if isinstance(j, int) and j == 0:
                    pe.wait_ge(dn_in, 16 * X)
                pe.wait_ge(hT_evac_a, j + 1)
                pe.wait_ge(hT_evac_b, 2 * j + 2)
                wait(pe, added, j)
                for c in range(FC):
                    last = pe.matmul(y_ps[:, 0:E], h_T[:, c, :], dn[:, bass.ds(x, 1), c, :].rearrange("p a e -> p (a e)"),
                                     start=(c == 0), stop=(c == FC - 1))
                last.then_inc(y_ready, 1)

            def position(j, q):
                p = q % 2
                if live(j - 1):
                    turn_hidden(j - 1, 1 - p)
                if live(j):
                    gate_up(j, p)
                if live(j + 1):
                    turn(j + 1, (q + 1) % 4)
                if live(j - 1):
                    down(j - 1, 1 - p)

            pe.wait_ge(consts_in, 16 * 5)
            turn(0, 0)
            pe.wait_ge(half_set, 2)
            pe.wait_ge(experts_ready, 1)
            pe.wait_ge(gu_in, 16 * X * KE)
            run(pe, position)

        @block.scalar
        def _(act):
            def turned_tile(j, p):
                act.wait_ge(xT_ready, j + 1)
                wait(act, up_ready, 2 * (j - 1))
                act.activation(x_T[:, p].rearrange("p k s -> p (k s)"), xT_ps[:, 0:KE * SLOTS], ACT.Copy).then_inc(xT_evac, 1)

            def position(j, q):
                p = q % 2
                if live(j - 1):
                    act.wait_ge(hT_ready, j)
                    wait(act, y_ready, j - 1)
                    act.activation(h_T[:, 4, :], hT_ps[1][:, 0:SLOTS], ACT.Copy).then_inc(hT_evac_b, 1)
                    act.activation(h_T[0:FF - 640, 5, :], hT_ps[1][0:FF - 640, SLOTS:2 * SLOTS], ACT.Copy).then_inc(hT_evac_b, 1)
                if live(j):
                    for h in range(2):
                        act.wait_ge(gate_ready, 2 * j + h + 1)
                        wait(act, gated, 2 * (j - 1) + h + 1)
                        act.activation(gate[:, h, :], gate_ps[h][:, 0:QF], ACT.Silu).then_inc(silu_done, 1)
                if live(j + 1):
                    turned_tile(j + 1, 1 - p)

            act.wait_ge(consts_in, 16 * 5)
            gu_last = gu[:, X - 1, KE - 1, :]
            act.dma_start(gu_last, io["gate_up"][(X * KE - 1) * 128:, :]).then_inc(gu_in, 16)
            for x in range(X):
                if x == X // 2:
                    turned_tile(0, 0)
                act.dma_start(dn[:, x], io["down"][x]).then_inc(dn_in, 16)
            run(act, position)

        @block.vector
        def _(dve):
            steps = [0]

            def then(instruction):
                steps[0] += 1
                instruction.then_inc(math, 1)
                dve.wait_ge(math, steps[0])

            def running_sum(buffers, n):
                at, step = 0, 1
                while step < n:
                    old, new = buffers(at), buffers(1 - at)
                    then(dve.tensor_copy(new(0, step), old(0, step)))
                    then(dve.tensor_tensor(new(step, n), old(step, n), old(0, n - step), ALU.add))
                    at, step = 1 - at, 2 * step
                return at

            dve.wait_ge(consts_in, 16 * 5)
            dve.wait_ge(counted, 1)
            then(dve.tensor_tensor(fill_f[:, :], count_ps[:, 0:X], lane[:, 0:1].to_broadcast([128, X]), ALU.add))
            dve.tensor_copy(fill_of[:, :], fill_f[:, :]).then_inc(fill_ready, 1)
            then(dve.tensor_tensor(count[:, :], count_ps[0:1, 0:X], region[0:1, :], ALU.subtract))
            then(dve.tensor_tensor(over[:, :, :], count[:, :].unsqueeze(2).to_broadcast([1, X, CT]),
                                   full[:, :].unsqueeze(1).to_broadcast([1, X, CT]), ALU.is_gt))
            then(dve.tensor_reduce(tiles_of[:, :], over[:, :, :], AX_X, ALU.add))
            then(dve.tensor_copy(ends[:, 0, :], tiles_of[:, :]))
            e = running_sum(lambda i: lambda a, z: ends[:, i, a:z], X)
            then(dve.tensor_tensor(passed[:, :, :], ends[:, e, :].unsqueeze(1).to_broadcast([1, NT, X]),
                                   tile_no[:, :].unsqueeze(2).to_broadcast([1, NT, X]), ALU.is_le))
            then(dve.tensor_scalar(step[:, :], tiles_of[:, :], -float(SLOTS), float(ROOM), ALU.mult, ALU.add))
            then(dve.tensor_tensor(jump[:, :, :], passed[:, :, :], step[:, :].unsqueeze(1).to_broadcast([1, NT, X]), ALU.mult))
            then(dve.tensor_reduce(row_f[:, :], jump[:, :, :], AX_X, ALU.add))
            then(dve.scalar_tensor_tensor(out=row_f[:, :], in0=tile_no[:, :], scalar=float(SLOTS), in1=row_f[:, :],
                                          op0=ALU.mult, op1=ALU.add))
            dve.tensor_copy(row_of[:, :], row_f[:, :]).then_inc(rows_ready, 1)
            then(dve.tensor_reduce(expert_f[:, :], passed[:, :, :], AX_X, ALU.add))
            dve.tensor_scalar(expert_of[:, :], expert_f[:, :], float(X - 1), None, ALU.min).then_inc(experts_ready, 1)

            def add_up(j, q):
                p = q % 2
                dve.wait_ge(y_ready, j + 1)
                if live(j - 2):
                    dve.wait_ge(out_out[p], 8 * (j - 2 - p + 2))
                dve.tensor_copy(token[:, p:p + 1], x_tile[:, q, E:E + 1])
                dve.tensor_tensor(y[:, p, :], y_ps[:, 0:E], x_tile[:, q, 0:E], ALU.add).then_inc(added, 1)
                dve.wait_ge(added, j + 1)
                wait(dve, stats_done, 2 * j)
                dve.bn_stats(stats[:, :], y[:, p, :]).then_inc(stats_done, 1)
                dve.wait_ge(stats_done, 2 * j + 1)
                dve.memset(pause[:, :], 0.0)
                dve.bn_aggr(mv[:, p, :], stats[:, :]).then_inc(stats_done, 1)
                dve.wait_ge(stats_done, 2 * j + 2)
                wait(dve, rstd_ready, j)
                dve.tensor_scalar(veps[:, :], mv[:, p, 1:2], EPS, None, ALU.add).then_inc(var_ready, 1)

            def normalize(j, p):
                dve.wait_ge(rstd_ready, j + 1)
                dve.tensor_scalar(y[:, p, :], y[:, p, :], mv[:, p, 0:1], rstd[:, p:p + 1],
                                  ALU.subtract, ALU.mult).then_inc(out_ready, 1)

            def position(j, q):
                p = q % 2
                if live(j - 1):
                    dve.wait_ge(hT_ready, j)
                    wait(dve, y_ready, j - 1)
                    dve.tensor_copy(h_T[:, 0:4, :].rearrange("p c s -> p (c s)"), hT_ps[0][:, 0:4 * SLOTS]).then_inc(hT_evac_a, 1)
                if live(j - 2):
                    normalize(j - 2, p)
                if live(j):
                    wait(dve, hT_ready, j - 1)
                    for h in range(2):
                        dve.wait_ge(silu_done, 2 * j + h + 1)
                        dve.wait_ge(up_ready, 2 * j + h + 1)
                        dve.tensor_tensor(hidden[:, p, QF * h:QF * h + QF], gate[:, h, :], up_ps[h][:, 0:QF],
                                          ALU.mult).then_inc(gated, 1)
                if live(j - 1):
                    add_up(j - 1, (q - 1) % 4)

            run(dve, position)


def decoder_layer(nc, io, phases="abc"):
    with ExitStack() as ctx:
        for name, rows, cols in (("x1", B * S, E), ("mask_f", B, S2 + S2 % 2),
                                 ("sorted", X * ROOM + IDLE * SLOTS, E + 1)):
            if name not in io:
                io[name] = nc.dram_tensor(name, (rows, cols), F32).ap()

        if "a" in phases:
            self_attention(nc, io)

        def carve(space, parts):
            mem, at = {}, 0
            for name, (a, b) in parts.items():
                mem[name] = space[:, at:at + a * b].rearrange("p (a b) -> p a b", a=a)
                at += a * b
            return mem

        def rows_of(mem, rows):
            return {name: view[0:rows.get(name, 128)] for name, view in mem.items()}

        gu = ctx.enter_context(nc.sbuf_tensor("gate_up", [128, X, KE, 2 * FF], F32))
        dn = ctx.enter_context(nc.sbuf_tensor("down", [128, X, FC, E], F32))
        tally = ctx.enter_context(nc.sbuf_tensor("tally", [S, X], F32))
        gate_up_in = ctx.enter_context(nc.semaphore("gate_up_in"))
        gu_flat = gu[:, :, :, :].rearrange("p x k f -> p (x k f)")
        dn_flat = dn[:, :, :, :].rearrange("p x c e -> p (x c e)")
        if "b" in phases:
            SC = S2 + S2 % 2
            late = carve(gu_flat[:, (X * KE - 2) * 2 * FF:], {"k_w": (KE, 3 * PR), "v_w": (KE, E)})
            last = rows_of(carve(gu_flat[:, (X * KE - 1) * 2 * FF:], {
                "x1_nat": (2, E), "x1_res": (1, E), "x1_T": (KE, S), "x2_T": (KE, S)}), {"x1_nat": S, "x1_res": S})
            cross_attention(nc, io, late | last | rows_of(carve(dn_flat, {
                "q_w": (KE, 3 * PR), "p_w": (4, E), "probs": (3, N2 * S), "v_bias": (1, E), "c_T": (KE, SC), "q_T": (3, S),
                "v": (2, 3 * N2 * 32), "o_raw": (1, 4 * S), "inv": (1, 4 * S), "o_T": (1, 4 * S), "zeros": (1, E + 1)}),
                {"probs": CTX[0][1], "v": CTX[0][1], "q_T": PR})
                            | {"tally": tally, "gate_up": gu_flat, "gate_up_in": gate_up_in})
        if "c" in phases:
            experts(nc, io, {"gate_up": gu, "down": dn, "tally": tally, "gate_up_in": gate_up_in})



def _constants(np):
    block_of = np.zeros((PR, N2), np.float32)
    for h0, n in PARTS:
        for h in range(n):
            block_of[D2 * h:D2 * h + D2, h0 + h] = D2 ** -0.5
    sum_of = np.zeros((128, 128), np.float32)
    for q in range(4):
        sum_of[32 * q + D2, 32 * q:32 * q + 32] = 1.0
    ones = np.ones((S, 128), np.float32)
    starts = ROOM * np.arange(X, dtype=np.float32)
    return {
        "ident": np.eye(128, dtype=np.float32), "below": np.tril(ones[:, 0:S], -1), "earlier": np.triu(ones[:, 0:S], 1), "ones": ones,
        "tally": np.concatenate([starts[None], np.zeros((S - 1, X), np.float32)]), "region": np.tile(starts, (128, 1)),
        "lane": np.arange(128, dtype=np.float32)[:, None],
        "block_of": block_of, "sum_of": sum_of, "rank": np.tile((X - np.arange(X, dtype=np.float32)) / (2 * X), (S, 1)),
        "full": SLOTS * np.arange(CT, dtype=np.float32)[None], "tile_no": np.arange(NT, dtype=np.float32)[None],
        "number": np.arange(B * S, dtype=np.float32).reshape(B, S).T,
    }


def _arrays(np, a):
    rows = lambda w: w.reshape(-1, 128, w.shape[-1]).transpose(1, 0, 2)

    def parts(w):
        out = np.zeros((w.shape[0], len(PARTS) * PR), w.dtype)
        for i, (h0, n) in enumerate(PARTS):
            out[:, PR * i:PR * i + D2 * n] = w[:, D2 * h0:D2 * (h0 + n)]
        return out

    p_w = np.zeros((4, 32, 4, E), np.float32)
    p_w[:, 0:D2] = a["L0_xattn_proj_w"].reshape(4, 4, D2, E).transpose(1, 2, 0, 3)
    p_w[0, D2, 0] = a["L0_xattn_proj_b"]
    down = np.zeros((X, FC * 128, E), np.float32)
    down[:, 0:FF] = a["L0_ffn_down_w"].transpose(0, 2, 1)
    gate_up = np.concatenate([a["L0_ffn_gate_w"], a["L0_ffn_up_w"]], axis=1).transpose(0, 2, 1)
    heads = lambda w: rows(w.transpose(1, 0, 2).reshape(E, N1 * D1))
    return {
        "x": a["x"], "xT": np.pad(rows(a["x"].reshape(B * S, E).T), ((0, 0), (0, 0), (0, GS))),
        "wq": heads(a["L0_attn_WQ"]), "wk": heads(a["L0_attn_WK"]), "wv": heads(a["L0_attn_WV_down"]),
        "wu": rows(a["L0_attn_WV_up"].reshape(N1 * D1, E)),
        "ctxT": np.pad(a["ctx_1024"].transpose(0, 2, 1).reshape(B, KE, 128, S2).transpose(0, 2, 1, 3),
                       ((0, 0), (0, 0), (0, 0), (0, S2 % 2))),
        "mask": a["mask_BxS2_bk0"],
        "q_w": rows(parts(a["L0_xattn_q_w"])), "q_b": parts(a["L0_xattn_q_b"][None]).reshape(-1, PR).T,
        "k_w": rows(parts(a["L0_xattn_kv_w"][:, 0:E])), "k_b": parts(a["L0_xattn_kv_b"][None, 0:E]).reshape(-1, PR).T,
        "v_w": rows(a["L0_xattn_kv_w"][:, E:]), "v_b": a["L0_xattn_kv_b"][E:],
        "p_w": p_w.reshape(128, 4, E), "router": rows(a["L0_ffn_router_w"].T),
        "gate_up": gate_up.reshape(X * KE * 128, 2 * FF),
        "down": down.reshape(X, FC, 128, E).transpose(0, 2, 1, 3),
    }


def kernel(**inputs):
    import numpy as _np
    import concourse.bacc as _bacc
    from concourse.bass_utils import run_bass_kernel_spmd as _run

    nc = _bacc.Bacc("TRN2", target_bir_lowering=False, num_devices=1)
    given = {name: _np.asarray(value) for name, value in inputs.items()}
    arrays, io = {}, {}
    for name, a in {**_arrays(_np, given), **_constants(_np)}.items():
        a = arrays[f"in_{name}"] = _np.ascontiguousarray(a)
        io[name] = nc.dram_tensor(f"in_{name}", a.shape, mybir.dt.from_np(a.dtype), kind="ExternalInput").ap()
    io["out"] = nc.dram_tensor("out_0", (B, S, E), F32, kind="ExternalOutput").ap()
    decoder_layer(nc, io)
    r = _run(nc, [arrays], core_ids=[0])
    return r.results[0]["out_0"]
```
